# Optimizing a Trainium2 kernel written in Bass

```python
import numpy as np
import jax
import jax.numpy as jnp

def _softmax(x, axis=-1):
    return jax.nn.softmax(x, axis=axis)

def _gelu(x):
    return jax.nn.gelu(x, approximate=True)

def _silu(x):
    return jax.nn.silu(x)

def _sigmoid(x):
    return jax.nn.sigmoid(x)

def _layernorm(x, axis=-1, eps=1e-05):
    m = jnp.mean(x, axis=axis, keepdims=True)
    v = jnp.var(x, axis=axis, keepdims=True)
    return (x - m) / jnp.sqrt(v + eps)

def _scatter_add(tgt, idx, src, axis=0):
    return tgt.at[idx].add(src)

def _segment_sum(src, seg, n):
    return jax.ops.segment_sum(src, seg, n)
kernel_name = 'mk_decoder_preln_d2_seqx_r8_cdc68a'

def setup_inputs(seed: int=0):
    np.random.seed(seed)
    _w = jnp.asarray

    def _rec_inputs():
        import jax
        import jax.numpy as jnp
        _rk = jax.random.key(seed)
        x = 7.22e-05 + 1 * jax.random.normal(jax.random.fold_in(_rk, 1), (4, 256, 256), jnp.float32)
        _lenS = 256 - jax.random.randint(jax.random.fold_in(_rk, 7), (4,), 0, max(1, 256 // 4) + 1, jnp.int32)
        _lenS2 = 256 - jax.random.randint(jax.random.fold_in(_rk, 8), (4,), 0, max(1, 256 // 4) + 1, jnp.int32)
        _ctx_2048P = jax.random.normal(jax.random.fold_in(_rk, 11), (4, 16, 256), jnp.float32)
        _ctx_2048c = jax.random.dirichlet(jax.random.fold_in(_rk, 511), 0.3 * jnp.ones((16,), jnp.float32), (4, 256))
        _ctx_2048t = jnp.einsum('bsk,bkd->bsd', _ctx_2048c, _ctx_2048P)
        _ctx_2048t = _ctx_2048t * jax.lax.rsqrt(jnp.mean(jnp.square(_ctx_2048t)) + 1e-12) * 0.953939
        ctx_2048 = 4.13588e-05 + 0.999923 * (_ctx_2048t + 0.3 * jax.random.normal(jax.random.fold_in(_rk, 611), (4, 256, 256), jnp.float32))
        return (x, ctx_2048)
    x, ctx_2048 = _rec_inputs()

    def _L0_attn_setup():
        import jax, jax.numpy as jnp
        import numpy as np
        HID = 256
        NK, DK = (16, 128)
        NV, DV = (32, 128)
        KC = 4
        P = NV // NK
        SV = P * DV
        QD = NK * DK
        VD = NV * DV
        QKV = QD + QD + VD
        B, T = (2, 256)
        EPS_NORM = 1e-12
        EPS_RMS = 1e-06

        def _l2norm(x):
            n = jnp.sqrt(jnp.sum(x * x, axis=-1, keepdims=True))
            return x / jnp.maximum(n, EPS_NORM)

        def _reference_tuple_inner(x, W_qkv, W_z, W_b, W_a, conv_w, dt_bias, A_log, norm_w, W_out):
            Bq, Tq, _ = x.shape
            qkv = jnp.einsum('btc,dc->btd', x, W_qkv)
            z = jnp.einsum('btc,dc->btd', x, W_z)
            beta = jax.nn.sigmoid(jnp.einsum('btc,hc->bth', x, W_b))
            dt = jax.nn.softplus(jnp.einsum('btc,hc->bth', x, W_a) + dt_bias)
            decay = jnp.exp(-dt * jnp.exp(A_log))
            xp = jnp.pad(qkv, ((0, 0), (KC - 1, 0), (0, 0)))
            qkv_c = sum((xp[:, j:j + Tq, :] * conv_w[:, j] for j in range(KC)))
            new_conv_buf = jnp.transpose(xp[:, -(KC - 1):, :], (0, 2, 1))
            q = _l2norm(qkv_c[..., :QD].reshape(Bq, Tq, NK, DK))
            k = _l2norm(qkv_c[..., QD:2 * QD].reshape(Bq, Tq, NK, DK))
            v = qkv_c[..., 2 * QD:].reshape(Bq, Tq, NK, P, DV)
            beta_r = beta.reshape(Bq, Tq, NK, P)
            decay_r = decay.reshape(Bq, Tq, NK, P)
            qT = jnp.swapaxes(q, 0, 1)
            kT = jnp.swapaxes(k, 0, 1)
            vT = jnp.swapaxes(v, 0, 1)
            bT = jnp.swapaxes(beta_r, 0, 1)
            dT = jnp.swapaxes(decay_r, 0, 1)

            def step(S, inp):
                q_t, k_t, v_t, b_t, d_t = inp
                Sk = jnp.einsum('bhi,bhipj->bhpj', k_t, S)
                dv = b_t[..., None] * (v_t - Sk)
                upd = jnp.einsum('bhi,bhpj->bhipj', k_t, dv)
                S = S * d_t[:, :, None, :, None] + upd
                o = jnp.einsum('bhi,bhipj->bhpj', q_t, S)
                return (S, o)
            S0 = jnp.zeros((Bq, NK, DK, P, DV), x.dtype)
            S_final, outs = jax.lax.scan(step, S0, (qT, kT, vT, bT, dT))
            out = jnp.swapaxes(outs, 0, 1).reshape(Bq, Tq, NV, DV)
            rms = jax.lax.rsqrt(jnp.mean(out * out, axis=-1, keepdims=True) + EPS_RMS)
            out = out * rms * norm_w
            out = out.reshape(Bq, Tq, VD) * jax.nn.silu(z)
            y = jnp.einsum('btd,cd->btc', out, W_out)
            return (y, S_final.reshape(Bq, NK, DK, SV), new_conv_buf)
        key = jax.random.key(seed)
        ks = jax.random.split(key, 8)
        lin = lambda k, o, i: jax.random.normal(k, (o, i), jnp.float32) / np.sqrt(i).astype(np.float32)
        return {'x': jax.random.normal(ks[0], (B, T, HID), jnp.float32), 'W_qkv': lin(ks[1], QKV, HID), 'W_z': lin(ks[2], VD, HID), 'W_b': lin(ks[3], NV, HID), 'W_a': lin(ks[4], NV, HID), 'conv_w': jax.random.normal(ks[5], (QKV, KC), jnp.float32) * 0.1, 'dt_bias': jnp.zeros((NV,), jnp.float32), 'A_log': jnp.zeros((NV,), jnp.float32), 'norm_w': jnp.ones((DV,), jnp.float32), 'W_out': lin(ks[6], HID, VD)}
    _L0_attn_all = _L0_attn_setup()
    _L0_attn_in = {k: v for k, v in _L0_attn_all.items() if k in ('W_qkv', 'W_z', 'W_b', 'W_a', 'conv_w', 'dt_bias', 'A_log', 'norm_w', 'W_out')}
    del _L0_attn_all

    def _L0_xattn_setup():
        import jax, jax.numpy as jnp
        import numpy as np
        BS, S, DK = (8, 64, 256)
        key = jax.random.key(seed)
        kq, kk, kv = jax.random.split(key, 3)
        q = jax.random.normal(kq, (BS, S, DK), dtype=jnp.float32)
        k = jax.random.normal(kk, (BS, S, DK), dtype=jnp.float32)
        v = jax.random.normal(kv, (BS, S, DK), dtype=jnp.float32)
        return {'q': q, 'k': k, 'v': v}
    _L0_xattn_all = _L0_xattn_setup()
    _L0_xattn_in = {k: v for k, v in _L0_xattn_all.items() if k in ()}
    del _L0_xattn_all

    def _L0_ffn_setup():
        import jax, jax.numpy as jnp
        import numpy as np
        TOP_K = 2
        key = jax.random.key(seed)
        ks = jax.random.split(key, 4)
        G, S, F, E, H = (4, 256, 256, 8, 256)
        return {'x': jax.random.normal(ks[0], (G, S, F), dtype=jnp.float32), 'router_logits': jax.random.normal(ks[1], (F, E), dtype=jnp.float32) * 0.02, 'gating_einsum': jax.random.normal(ks[2], (E, 2, H, F), dtype=jnp.float32) * 0.02, 'linear': jax.random.normal(ks[3], (E, H, F), dtype=jnp.float32) * 0.02, 'per_expert_scale': jnp.ones((E,), dtype=jnp.float32), 'router_scale': jnp.ones((F,), dtype=jnp.float32)}
    _L0_ffn_all = _L0_ffn_setup()
    _L0_ffn_in = {k: v for k, v in _L0_ffn_all.items() if k in ('router_logits', 'gating_einsum', 'linear', 'per_expert_scale', 'router_scale')}
    del _L0_ffn_all

    def _L1_attn_setup():
        import jax, jax.numpy as jnp
        import numpy as np
        D_MODEL = 256
        H = 16
        HKV = 4
        DH = D_MODEL // H
        WINDOW = 32
        GROUP = H // HKV
        ROPE_BASE = 10000.0
        NEG_INF = -1e+30

        def _rotate_half(t):
            t1, t2 = jnp.split(t, 2, axis=-1)
            return jnp.concatenate([-t2, t1], axis=-1)

        def _apply_rope(q, k, positions):
            inv_freq = 1.0 / ROPE_BASE ** (jnp.arange(0, DH, 2, dtype=jnp.float32) / DH)
            ang = positions.astype(jnp.float32)[:, None] * inv_freq[None, :]
            cos = jnp.concatenate([jnp.cos(ang), jnp.cos(ang)], axis=-1)[None, None]
            sin = jnp.concatenate([jnp.sin(ang), jnp.sin(ang)], axis=-1)[None, None]
            q = q * cos + _rotate_half(q) * sin
            k = k * cos + _rotate_half(k) * sin
            return (q, k)
        key = jax.random.key(seed)
        ks = jax.random.split(key, 5)
        B, L = (2, 256)
        x = jax.random.normal(ks[0], (B, L, D_MODEL), dtype=jnp.float32)
        Wq = jax.random.normal(ks[1], (H * DH, D_MODEL), dtype=jnp.float32) * 0.02
        Wkv = jax.random.normal(ks[2], (2 * HKV * DH, D_MODEL), dtype=jnp.float32) * 0.02
        Wo = jax.random.normal(ks[3], (D_MODEL, D_MODEL), dtype=jnp.float32) * 0.02
        qk_temp = jnp.full((H, 1, 1), np.sqrt(DH), dtype=jnp.float32)
        return {'x': x, 'Wq': Wq, 'Wkv': Wkv, 'Wo': Wo, 'qk_temp': qk_temp}
    _L1_attn_all = _L1_attn_setup()
    _L1_attn_in = {k: v for k, v in _L1_attn_all.items() if k in ('Wq', 'Wkv', 'Wo', 'qk_temp')}
    del _L1_attn_all

    def _L1_xattn_setup():
        import jax, jax.numpy as jnp
        import numpy as np
        N_HEAD = 8
        ALPHA = 5.0
        EPS = 1e-12

        def _l2norm(x, axis):
            n = jnp.sqrt(jnp.sum(x * x, axis=axis, keepdims=True))
            return x / jnp.maximum(n, EPS)
        key = jax.random.key(seed)
        kq, kk, kv = jax.random.split(key, 3)
        B, D, T = (4, 128, 256)
        q = jax.random.normal(kq, (B, D, T), dtype=jnp.float32)
        k = jax.random.normal(kk, (B, D, T), dtype=jnp.float32)
        v = jax.random.normal(kv, (B, D, T), dtype=jnp.float32)
        return {'q': q, 'k': k, 'v': v}
    _L1_xattn_all = _L1_xattn_setup()
    _L1_xattn_in = {k: v for k, v in _L1_xattn_all.items() if k in ()}
    del _L1_xattn_all

    def _L1_ffn_setup():
        import jax, jax.numpy as jnp
        import numpy as np
        TOP_K = 2
        key = jax.random.key(seed)
        k1, k2, k3, k4, k5 = jax.random.split(key, 5)
        B, S, H, O, E = (2, 128, 256, 256, 8)
        hidden_states = jax.random.normal(k1, (B, S, H), dtype=jnp.float32)
        router_w = jax.random.normal(k2, (O * E, H), dtype=jnp.float32) * 0.02
        router_b = jnp.zeros((O * E,), dtype=jnp.float32)
        expert_w = jax.random.normal(k3, (E, O, H), dtype=jnp.float32) * 0.02
        expert_b = jnp.zeros((E, O), dtype=jnp.float32)
        return {'hidden_states': hidden_states, 'router_w': router_w, 'router_b': router_b, 'expert_w': expert_w, 'expert_b': expert_b}
    _L1_ffn_all = _L1_ffn_setup()
    _L1_ffn_in = {k: v for k, v in _L1_ffn_all.items() if k in ('router_w', 'router_b', 'expert_w', 'expert_b')}
    del _L1_ffn_all
    return {'x': x, 'ctx_2048': ctx_2048, 'L0_attn_W_qkv': _L0_attn_in['W_qkv'], 'L0_attn_W_z': _L0_attn_in['W_z'], 'L0_attn_W_b': _L0_attn_in['W_b'], 'L0_attn_W_a': _L0_attn_in['W_a'], 'L0_attn_conv_w': _L0_attn_in['conv_w'], 'L0_attn_dt_bias': _L0_attn_in['dt_bias'], 'L0_attn_A_log': _L0_attn_in['A_log'], 'L0_attn_norm_w': _L0_attn_in['norm_w'], 'L0_attn_W_out': _L0_attn_in['W_out'], 'L0_ffn_router_logits': _L0_ffn_in['router_logits'], 'L0_ffn_gating_einsum': _L0_ffn_in['gating_einsum'], 'L0_ffn_linear': _L0_ffn_in['linear'], 'L0_ffn_per_expert_scale': _L0_ffn_in['per_expert_scale'], 'L0_ffn_router_scale': _L0_ffn_in['router_scale'], 'L1_attn_Wq': _L1_attn_in['Wq'], 'L1_attn_Wkv': _L1_attn_in['Wkv'], 'L1_attn_Wo': _L1_attn_in['Wo'], 'L1_attn_qk_temp': _L1_attn_in['qk_temp'], 'L1_ffn_router_w': _L1_ffn_in['router_w'], 'L1_ffn_router_b': _L1_ffn_in['router_b'], 'L1_ffn_expert_w': _L1_ffn_in['expert_w'], 'L1_ffn_expert_b': _L1_ffn_in['expert_b']}

def reference(x, ctx_2048, L0_attn_W_qkv, L0_attn_W_z, L0_attn_W_b, L0_attn_W_a, L0_attn_conv_w, L0_attn_dt_bias, L0_attn_A_log, L0_attn_norm_w, L0_attn_W_out, L0_ffn_router_logits, L0_ffn_gating_einsum, L0_ffn_linear, L0_ffn_per_expert_scale, L0_ffn_router_scale, L1_attn_Wq, L1_attn_Wkv, L1_attn_Wo, L1_attn_qk_temp, L1_ffn_router_w, L1_ffn_router_b, L1_ffn_expert_w, L1_ffn_expert_b):
    import jax
    import jax.numpy as jnp

    def _L0_attn_ref(x, W_qkv, W_z, W_b, W_a, conv_w, dt_bias, A_log, norm_w, W_out):
        import jax, jax.numpy as jnp
        import numpy as np
        HID = 256
        NK, DK = (16, 128)
        NV, DV = (32, 128)
        KC = 4
        P = NV // NK
        SV = P * DV
        QD = NK * DK
        VD = NV * DV
        QKV = QD + QD + VD
        B, T = (2, 256)
        EPS_NORM = 1e-12
        EPS_RMS = 1e-06

        def _l2norm(x):
            n = jnp.sqrt(jnp.sum(x * x, axis=-1, keepdims=True))
            return x / jnp.maximum(n, EPS_NORM)

        def _reference_tuple_inner(x, W_qkv, W_z, W_b, W_a, conv_w, dt_bias, A_log, norm_w, W_out):
            Bq, Tq, _ = x.shape
            qkv = jnp.einsum('btc,dc->btd', x, W_qkv)
            z = jnp.einsum('btc,dc->btd', x, W_z)
            beta = jax.nn.sigmoid(jnp.einsum('btc,hc->bth', x, W_b))
            dt = jax.nn.softplus(jnp.einsum('btc,hc->bth', x, W_a) + dt_bias)
            decay = jnp.exp(-dt * jnp.exp(A_log))
            xp = jnp.pad(qkv, ((0, 0), (KC - 1, 0), (0, 0)))
            qkv_c = sum((xp[:, j:j + Tq, :] * conv_w[:, j] for j in range(KC)))
            new_conv_buf = jnp.transpose(xp[:, -(KC - 1):, :], (0, 2, 1))
            q = _l2norm(qkv_c[..., :QD].reshape(Bq, Tq, NK, DK))
            k = _l2norm(qkv_c[..., QD:2 * QD].reshape(Bq, Tq, NK, DK))
            v = qkv_c[..., 2 * QD:].reshape(Bq, Tq, NK, P, DV)
            beta_r = beta.reshape(Bq, Tq, NK, P)
            decay_r = decay.reshape(Bq, Tq, NK, P)
            qT = jnp.swapaxes(q, 0, 1)
            kT = jnp.swapaxes(k, 0, 1)
            vT = jnp.swapaxes(v, 0, 1)
            bT = jnp.swapaxes(beta_r, 0, 1)
            dT = jnp.swapaxes(decay_r, 0, 1)

            def step(S, inp):
                q_t, k_t, v_t, b_t, d_t = inp
                Sk = jnp.einsum('bhi,bhipj->bhpj', k_t, S)
                dv = b_t[..., None] * (v_t - Sk)
                upd = jnp.einsum('bhi,bhpj->bhipj', k_t, dv)
                S = S * d_t[:, :, None, :, None] + upd
                o = jnp.einsum('bhi,bhipj->bhpj', q_t, S)
                return (S, o)
            S0 = jnp.zeros((Bq, NK, DK, P, DV), x.dtype)
            S_final, outs = jax.lax.scan(step, S0, (qT, kT, vT, bT, dT))
            out = jnp.swapaxes(outs, 0, 1).reshape(Bq, Tq, NV, DV)
            rms = jax.lax.rsqrt(jnp.mean(out * out, axis=-1, keepdims=True) + EPS_RMS)
            out = out * rms * norm_w
            out = out.reshape(Bq, Tq, VD) * jax.nn.silu(z)
            y = jnp.einsum('btd,cd->btc', out, W_out)
            return (y, S_final.reshape(Bq, NK, DK, SV), new_conv_buf)
        return _reference_tuple_inner(x, W_qkv, W_z, W_b, W_a, conv_w, dt_bias, A_log, norm_w, W_out)[0]

    def _L0_xattn_ref(q, k, v):
        import jax, jax.numpy as jnp
        import numpy as np
        BS, S, DK = (8, 64, 256)
        dk = q.shape[-1]
        scale = 1.0 / jnp.sqrt(jnp.asarray(dk, dtype=q.dtype))
        scaled = jnp.einsum('bsd,bse->bde', q, k) * scale
        attn = jax.nn.softmax(scaled, axis=1)
        out = jnp.einsum('bde,bse->bsd', attn, v)
        return out

    def _L0_ffn_ref(x, router_logits, gating_einsum, linear, per_expert_scale, router_scale):
        import jax, jax.numpy as jnp
        import numpy as np
        TOP_K = 2
        G, S, F = x.shape
        E = router_logits.shape[-1]
        H = linear.shape[1]
        k = TOP_K
        dtype = x.dtype
        var = jnp.mean(jnp.square(x.astype(jnp.float32)), axis=-1, keepdims=True)
        router_input = x * jax.lax.rsqrt(var + 1e-06).astype(dtype)
        root_size = jax.lax.rsqrt(jnp.array(F, dtype=dtype))
        router_input = router_input * root_size * router_scale.astype(dtype)
        logits = jnp.einsum('gsd,de->gse', router_input, router_logits.astype(dtype))
        logits32 = logits.astype(jnp.float32)
        probs = jax.nn.softmax(logits32, axis=-1)
        _, choices = jax.lax.approx_max_k(logits32, k=k)
        indicator = jax.nn.one_hot(choices, E, dtype=probs.dtype).sum(axis=-2)
        renorm = jnp.sum(indicator * probs, axis=-1, keepdims=True)
        renorm = jnp.where(renorm > 0.0, renorm, 1.0)
        weights = probs / renorm
        x_flat = x.reshape((-1, F))
        batch_size = G * S
        choices_flat = choices.ravel()
        xs_order = choices_flat.argsort()
        xs_reverse_argsort = xs_order.argsort()
        xs_indices = jnp.repeat(jnp.arange(batch_size), k)[xs_order]
        sorted_xs = x_flat[xs_indices, :]
        choices_oh = jax.nn.one_hot(choices, num_classes=E, dtype=jnp.int32)
        tokens_per_expert = jnp.sum(choices_oh, axis=(0, 1, 2))
        combine_weights = (choices_oh.astype(jnp.float32) * jnp.expand_dims(weights, axis=2)).sum(axis=-1).astype(weights.dtype)
        w_gate = jnp.transpose(gating_einsum, (0, 3, 1, 2)).reshape(E, F, 2 * H)
        gate_out = jax.lax.ragged_dot(sorted_xs, w_gate.astype(dtype), group_sizes=tokens_per_expert)
        gate_out = gate_out.reshape(gate_out.shape[0], 2, H)
        activation = jax.nn.gelu(gate_out[:, 0, :]) * gate_out[:, 1, :]
        expert_outputs = jax.lax.ragged_dot(activation, linear.astype(dtype), group_sizes=tokens_per_expert)
        expert_indices = jnp.repeat(jnp.arange(E), tokens_per_expert, total_repeat_length=expert_outputs.shape[0])
        expert_outputs = expert_outputs * per_expert_scale.astype(expert_outputs.dtype)[expert_indices, None]
        out = expert_outputs[xs_reverse_argsort].reshape((G, S, k, -1))
        out = jnp.einsum('blkd,blk->bld', out, combine_weights, preferred_element_type=out.dtype)
        return out

    def _L1_attn_ref(x, Wq, Wkv, Wo, qk_temp):
        import jax, jax.numpy as jnp
        import numpy as np
        D_MODEL = 256
        H = 16
        HKV = 4
        DH = D_MODEL // H
        WINDOW = 32
        GROUP = H // HKV
        ROPE_BASE = 10000.0
        NEG_INF = -1e+30

        def _rotate_half(t):
            t1, t2 = jnp.split(t, 2, axis=-1)
            return jnp.concatenate([-t2, t1], axis=-1)

        def _apply_rope(q, k, positions):
            inv_freq = 1.0 / ROPE_BASE ** (jnp.arange(0, DH, 2, dtype=jnp.float32) / DH)
            ang = positions.astype(jnp.float32)[:, None] * inv_freq[None, :]
            cos = jnp.concatenate([jnp.cos(ang), jnp.cos(ang)], axis=-1)[None, None]
            sin = jnp.concatenate([jnp.sin(ang), jnp.sin(ang)], axis=-1)[None, None]
            q = q * cos + _rotate_half(q) * sin
            k = k * cos + _rotate_half(k) * sin
            return (q, k)
        B, L, _ = x.shape
        q = (x @ Wq.T).reshape(B, L, H, DH).transpose(0, 2, 1, 3)
        kv = (x @ Wkv.T).reshape(B, L, 2, HKV, DH).transpose(2, 0, 3, 1, 4)
        k, v = (kv[0], kv[1])
        positions = jnp.arange(L)
        q, k = _apply_rope(q, k, positions)
        k = jnp.repeat(k, GROUP, axis=1)
        v = jnp.repeat(v, GROUP, axis=1)
        q = q / jnp.linalg.norm(q, axis=-1, keepdims=True).clip(1e-12) * qk_temp[None]
        k = k / jnp.linalg.norm(k, axis=-1, keepdims=True).clip(1e-12)
        row = jnp.arange(L)[:, None]
        col = jnp.arange(L)[None, :]
        allowed = (row >= col) & (row - col < WINDOW)
        scores = jnp.einsum('bhqd,bhkd->bhqk', q, k)
        scores = jnp.where(allowed[None, None], scores, NEG_INF)
        attn = jax.nn.softmax(scores, axis=-1)
        out = jnp.einsum('bhqk,bhkd->bhqd', attn, v)
        out = out.transpose(0, 2, 1, 3).reshape(B, L, D_MODEL)
        return out @ Wo.T

    def _L1_xattn_ref(q, k, v):
        import jax, jax.numpy as jnp
        import numpy as np
        N_HEAD = 8
        ALPHA = 5.0
        EPS = 1e-12

        def _l2norm(x, axis):
            n = jnp.sqrt(jnp.sum(x * x, axis=axis, keepdims=True))
            return x / jnp.maximum(n, EPS)
        B, D, Tq = q.shape
        Tk = k.shape[-1]
        Dv = v.shape[-2]
        h = N_HEAD
        d = D // h
        dv = Dv // h
        qh = q.reshape(B, h, d, Tq)
        kh = k.reshape(B, h, d, Tk)
        vh = v.reshape(B, h, dv, Tk)
        qn = _l2norm(qh, axis=-2)
        kn = _l2norm(kh, axis=-2)
        qk = ALPHA * jnp.einsum('bhdq,bhdk->bhqk', qn, kn)
        sm = jax.nn.softmax(qk, axis=-1)
        out = jnp.einsum('bhqk,bhdk->bhdq', sm, vh)
        return out.reshape(B, Dv, Tq)

    def _L1_ffn_ref(hidden_states, router_w, router_b, expert_w, expert_b):
        import jax, jax.numpy as jnp
        import numpy as np
        TOP_K = 2
        B, S, H = hidden_states.shape
        E, O, _ = expert_w.shape
        T = B * S
        h = hidden_states.reshape(T, H)
        logits = (h @ router_w.T + router_b).reshape(T, O, E)
        probs = jax.nn.softmax(logits.astype(jnp.float32), axis=-1)
        w, sel = jax.lax.top_k(probs, TOP_K)
        w = w / jnp.sum(w, axis=-1, keepdims=True)
        w = w.astype(h.dtype)
        t_idx = jnp.arange(T)[:, None, None]
        c = jnp.zeros((T, E), dtype=h.dtype).at[t_idx, sel].add(w)
        expert_out = jnp.einsum('th,eoh->teo', h, expert_w) + expert_b[None, :, :]
        final = jnp.einsum('te,teo->to', c, expert_out)
        return final.reshape(B, S, O)
    x = x + _L0_attn_ref(_layernorm(x, axis=-1), L0_attn_W_qkv, L0_attn_W_z, L0_attn_W_b, L0_attn_W_a, L0_attn_conv_w, L0_attn_dt_bias, L0_attn_A_log, L0_attn_norm_w, L0_attn_W_out)
    x = x + _L0_xattn_ref(_layernorm(x, axis=-1), ctx_2048, ctx_2048)
    x = x + _L0_ffn_ref(_layernorm(x, axis=-1), L0_ffn_router_logits, L0_ffn_gating_einsum, L0_ffn_linear, L0_ffn_per_expert_scale, L0_ffn_router_scale)
    x = x + _L1_attn_ref(_layernorm(x, axis=-1), L1_attn_Wq, L1_attn_Wkv, L1_attn_Wo, L1_attn_qk_temp)
    x = x + _L1_xattn_ref(_layernorm(x, axis=-1), ctx_2048, ctx_2048)
    x = x + _L1_ffn_ref(_layernorm(x, axis=-1), L1_ffn_router_w, L1_ffn_router_b, L1_ffn_expert_w, L1_ffn_expert_b)
    return x

_drawn_inputs = setup_inputs


def setup_inputs(seed=0):
    import zlib

    import numpy as np

    out = dict(_drawn_inputs(seed))
    spreads = {'L0_attn_dt_bias': (0.0, 0.389),
     'L0_attn_A_log': (0.0, 0.1),
     'L0_attn_norm_w': (1.0, 0.2),
     'L0_ffn_per_expert_scale': (1.0, 0.6),
     'L0_ffn_router_scale': (1.0, 0.6),
     'L1_attn_qk_temp': (4.0, 0.6),
     'L1_ffn_router_b': (0.0, 0.1),
     'L1_ffn_expert_b': (0.0, 0.1)}
    factors = {'L0_ffn_router_logits': 4.532,
     'L0_ffn_gating_einsum': 3.956,
     'L0_ffn_linear': 4.011,
     'L1_attn_Wq': 2.917}
    for name, (base, spread) in spreads.items():
        noise = np.random.default_rng([zlib.crc32(name.encode()), seed]).standard_normal(out[name].shape)
        drawn = base * np.exp(spread * noise) if base else spread * noise
        out[name] = jnp.asarray(drawn.astype(out[name].dtype))
    for name, factor in factors.items():
        out[name] = (out[name] * factor).astype(out[name].dtype)
    return out
```

```python
from contextlib import ExitStack

import concourse.bass as bass
import numpy as np
from concourse import mybir

F32 = mybir.dt.float32
ALU = mybir.AluOpType
ACT = mybir.ActivationFunctionType
AX = mybir.AxisListType
P = 128
BANK = 512
B, T, C = 4, 256, 256
TILES = B * T // P
KT = C // P
TOK = B * T
LN_EPS = 1e-5


class Names:
    pass


class Steps:

    def __init__(self, sem):
        self.sem, self.n = sem, 0

    def one(self):
        self.n += 1
        return 1


def layernorm(nc, k, name, transposed=True):
    with ExitStack() as ctx:
        sem = lambda n: k.semaphore(f"{name}_{n}")
        stats = ctx.enter_context(nc.sbuf_tensor(f"{name}_stats", [P, TILES, 6], F32))
        mv = ctx.enter_context(nc.sbuf_tensor(f"{name}_mv", [P, TILES, 2], F32))
        rstd = ctx.enter_context(nc.sbuf_tensor(f"{name}_rstd", [P, TILES], F32))
        vare = ctx.enter_context(nc.sbuf_tensor(f"{name}_vare", [P, TILES], F32))
        vare_done = sem("vare_done")
        stats_done, mv_done, rstd_done = sem("stats_done"), sem("mv_done"), sem("rstd_done")
        xn_done, turned, xT_done = sem("xn_done"), sem("turned"), sem("xT_done")
        block = ctx.enter_context(nc.Block())

        @block.vector
        def _(dve):
            if k.x_loaded is not None:
                dve.wait_ge(k.x_loaded, 16)
            for i in range(TILES):
                nc.vector.bn_stats(stats[:, i, :], k.x[:, i, :]).then_inc(stats_done, 1)
            for i in range(TILES):
                dve.wait_ge(stats_done, i + 1)
                nc.vector.bn_aggr(mv[:, i, :], stats[:, i, :]).then_inc(mv_done, 1)
            dve.wait_ge(rstd_done, 1)
            for i in range(TILES):
                nc.vector.tensor_scalar(k.xn[:, i, :], k.x[:, i, :], mv[:, i, 0:1], rstd[:, i:i + 1],
                                        ALU.subtract, ALU.mult).then_inc(xn_done, 1)

        @block.gpsimd
        def _(pool):
            pool.wait_ge(mv_done, TILES)
            nc.gpsimd.tensor_scalar(vare[:], mv[:, :, 1], LN_EPS, None, ALU.add).then_inc(vare_done, 1)
            pool.wait_ge(vare_done, 1)
            nc.gpsimd.tensor_tensor(rstd[:], vare[:], k.neghalf[:, 0:TILES], ALU.pow).then_inc(rstd_done, 1)

        if not transposed:
            return

        @block.tensor
        def _(pe):
            if k.ident_ready is not None:
                pe.wait_ge(k.ident_ready, 2)
            for i in range(TILES):
                pe.wait_ge(xn_done, i + 1)
                for c in range(KT):
                    last = nc.tensor.transpose(k.ps[:, c * 2 + i // 4, (i % 4) * P:(i % 4 + 1) * P],
                                               k.xn[:, i, c * P:(c + 1) * P], k.ident[:])
                if i % 4 == 3:
                    last.then_inc(turned, 1)

        @block.scalar
        def _(act):
            for g in range(TILES // 4):
                act.wait_ge(turned, g + 1)
                for c in range(KT):
                    nc.scalar.copy(k.xT[:, c, g * BANK:(g + 1) * BANK], k.ps[:, c * 2 + g, :]).then_inc(xT_done, 1)


def cross_attention_0(nc, k):
    with ExitStack() as ctx:
        sem = lambda n: k.semaphore(f"xa0_{n}")
        sb = lambda n, s: ctx.enter_context(nc.sbuf_tensor(f"xa0_{n}", s, F32))
        SCALE = float(C) ** -0.5
        probs, top, ntop = sb("probs", [P, B, KT, C]), sb("top", [P, B, KT]), sb("ntop", [P, B, KT])
        total, rtotal = sb("total", [P, B, KT]), sb("rtotal", [P, B, KT])
        scores_ready, top_ready, ntop_ready, exp_ready = sem("scores"), sem("top"), sem("ntop"), sem("exp")
        rtotal_ready, probs_ready, mixed = sem("rtotal"), sem("probs_s"), sem("mixed")
        block = ctx.enter_context(nc.Block())

        @block.tensor
        def _(pe):
            pe.wait_ge(k.ctx_loaded, 16)
            for b in range(B):
                for e in range(KT):
                    for s in range(KT):
                        last = nc.tensor.matmul(k.ps[:, b, e * C:(e + 1) * C], k.ctx[:, 2 * b + s, e * P:(e + 1) * P],
                                                k.xn[:, 2 * b + s, :], start=s == 0, stop=s == KT - 1)
                last.then_inc(scores_ready, 1)
            pe.wait_ge(k.ctxT_loaded, 16)
            for b in range(B):
                pe.wait_ge(probs_ready, KT * (b + 1))
                for t in range(KT):
                    for e in range(KT):
                        last = nc.tensor.matmul(k.ps[:, B + b, t * C:(t + 1) * C], k.ctxT[:, 2 * b + e, t * P:(t + 1) * P],
                                                probs[:, b, e, :], start=e == 0, stop=e == KT - 1)
                last.then_inc(mixed, 1)

        @block.vector
        def _(dve):
            for b in range(B):
                dve.wait_ge(scores_ready, b + 1)
                nc.vector.tensor_reduce(top[:, b, :], k.ps[:, b, :].rearrange("p (e d) -> p e d", e=KT),
                                        AX.X, ALU.max).then_inc(top_ready, 1)
                dve.wait_ge(top_ready, b + 1)
                nc.vector.tensor_scalar(ntop[:, b, :], top[:, b, :], -SCALE, None, ALU.mult).then_inc(ntop_ready, 1)
            for b in range(B):
                dve.wait_ge(exp_ready, KT * (b + 1))
                nc.vector.reciprocal(rtotal[:, b, :], total[:, b, :]).then_inc(rtotal_ready, 1)
                dve.wait_ge(rtotal_ready, b + 1)
                for e in range(KT):
                    nc.vector.tensor_scalar(probs[:, b, e, :], probs[:, b, e, :], rtotal[:, b, e:e + 1], None,
                                            ALU.mult).then_inc(probs_ready, 1)
            for b in range(B):
                dve.wait_ge(mixed, b + 1)
                nc.vector.tensor_tensor(k.x[:, 2 * b:2 * b + 2, :], k.ps[:, B + b, :].rearrange("p (t d) -> p t d", t=KT),
                                        k.x[:, 2 * b:2 * b + 2, :], ALU.add)

        @block.scalar
        def _(act):
            for b in range(B):
                act.wait_ge(ntop_ready, b + 1)
                for e in range(KT):
                    nc.scalar.activation(probs[:, b, e, :], k.ps[:, b, e * C:(e + 1) * C], ACT.Exp, bias=ntop[:, b, e:e + 1],
                                         scale=SCALE, accum_out=total[:, b, e:e + 1]).then_inc(exp_ready, 1)


E0, H0 = 8, 256


def moe_router_0(nc, k):
    with ExitStack() as ctx:
        sem = lambda n: k.semaphore(f"mr_{n}")
        sb = lambda n, s: ctx.enter_context(nc.sbuf_tensor(f"mr_{n}", s, F32))
        router = sb("router", [P, KT, E0])
        square, mean2, inv = sb("square", [P, C]), sb("mean2", [P, TILES]), sb("inv", [P, TILES])
        logits, prob = sb("logits", [P, TILES, E0]), sb("prob", [P, TILES, E0])
        top, total, before = sb("top", [P, TILES]), sb("total", [P, TILES]), sb("before", [P, TILES, E0])
        above, tied = sb("above", [P, TILES, E0, E0]), sb("tied", [P, TILES, E0, E0])
        router_ready, square_done, inv_ready, logits_done = sem("router"), sem("square"), sem("inv"), sem("logits")
        step, shifted, exp_ready = Steps(sem("vector_step")), sem("shifted"), sem("exp")
        pool_step = sem("pool_step")
        block = ctx.enter_context(nc.Block())

        @block.scalar
        def _(act):
            for i in range(TILES):
                if i:
                    act.wait_ge(square_done, i)
                nc.scalar.activation(square[:], k.xn[:, i, :], ACT.Square, accum_out=mean2[:, i:i + 1]).then_inc(square_done, 1)
            act.wait_ge(shifted, 1)
            nc.scalar.activation(prob[:], prob[:], ACT.Exp).then_inc(exp_ready, 1)

        @block.gpsimd
        def _(pool):
            pool.wait_ge(square_done, TILES)
            nc.gpsimd.tensor_scalar(mean2[:], mean2[:], 1.0 / C, 1e-6, ALU.mult, ALU.add).then_inc(pool_step, 1)
            pool.wait_ge(pool_step, 1)
            nc.gpsimd.tensor_tensor(inv[:], mean2[:], k.neghalf[:, 0:TILES], ALU.pow).then_inc(pool_step, 1)
            pool.wait_ge(pool_step, 2)
            nc.gpsimd.tensor_scalar(inv[:], inv[:], float(C) ** -0.5, None, ALU.mult).then_inc(inv_ready, 1)

        @block.tensor
        def _(pe):
            pe.wait_ge(router_ready, KT)
            for i in range(TILES):
                for c in range(KT):
                    last = nc.tensor.matmul(k.ps[:, 0, i * E0:(i + 1) * E0], k.xT[:, c, i * P:(i + 1) * P],
                                            router[:, c, :], start=c == 0, stop=c == KT - 1)
            last.then_inc(logits_done, 1)

        @block.vector
        def _(dve):
            for s in (k.router_loaded, k.rscale_loaded, k.escale_loaded, k.lower_loaded):
                dve.wait_ge(s, 16)
            for c in range(KT):
                nc.vector.tensor_scalar(router[:, c, :], k.router[:, c, :], k.rscale[:, c:c + 1], None,
                                        ALU.mult).then_inc(router_ready, 1)
            dve.wait_ge(logits_done, 1)
            dve.wait_ge(inv_ready, 1)
            per_token = lambda v: v[:].unsqueeze(2).broadcast_to([P, TILES, E0])
            nc.vector.tensor_tensor(logits[:], k.ps[:, 0, 0:TILES * E0].rearrange("p (i e) -> p i e", i=TILES),
                                    per_token(inv), ALU.mult).then_inc(step.sem, step.one())
            dve.wait_ge(step.sem, step.n)
            nc.vector.tensor_reduce(top[:], logits[:], AX.X, ALU.max).then_inc(step.sem, step.one())
            mine = logits[:].unsqueeze(3).broadcast_to([P, TILES, E0, E0])
            other = logits[:].unsqueeze(2).broadcast_to([P, TILES, E0, E0])
            nc.vector.tensor_tensor(above[:], other, mine, ALU.is_gt).then_inc(step.sem, step.one())
            nc.vector.tensor_tensor(tied[:], other, mine, ALU.is_equal).then_inc(step.sem, step.one())
            dve.wait_ge(step.sem, step.n)
            nc.vector.tensor_tensor(prob[:], logits[:], per_token(top), ALU.subtract).then_inc(shifted, 1)
            nc.vector.tensor_tensor(tied[:], tied[:], k.lower[:].rearrange("p (e j) -> p e j", e=E0).unsqueeze(1)
                                    .broadcast_to([P, TILES, E0, E0]), ALU.mult).then_inc(step.sem, step.one())
            dve.wait_ge(step.sem, step.n)
            nc.vector.tensor_tensor(above[:], above[:], tied[:], ALU.add).then_inc(step.sem, step.one())
            dve.wait_ge(step.sem, step.n)
            nc.vector.tensor_reduce(before[:], above[:], AX.X, ALU.add).then_inc(step.sem, step.one())
            dve.wait_ge(step.sem, step.n)
            dve.wait_ge(exp_ready, 1)
            nc.vector.scalar_tensor_tensor(out=k.mix[:], in0=before[:], scalar=1.5, in1=prob[:],
                                           op0=ALU.is_lt, op1=ALU.mult).then_inc(step.sem, step.one())
            dve.wait_ge(step.sem, step.n)
            nc.vector.tensor_reduce(total[:], k.mix[:], AX.X, ALU.add).then_inc(step.sem, step.one())
            dve.wait_ge(step.sem, step.n)
            nc.vector.reciprocal(total[:], total[:]).then_inc(step.sem, step.one())
            dve.wait_ge(step.sem, step.n)
            nc.vector.tensor_tensor(k.mix[:], k.mix[:], per_token(total), ALU.mult).then_inc(step.sem, step.one())
            dve.wait_ge(step.sem, step.n)
            nc.vector.tensor_tensor(k.mix[:], k.mix[:], k.escale[:].unsqueeze(1).broadcast_to([P, TILES, E0]),
                                    ALU.mult)


def moe_experts_0(nc, k):
    with ExitStack() as ctx:
        sem = lambda n: k.semaphore(f"me_{n}")
        sb = lambda n, s: ctx.enter_context(nc.sbuf_tensor(f"me_{n}", s, F32))
        HALVES = TOK // BANK
        HT = H0 // P
        UNITS = E0 * HALVES
        gated, act_out = sb("gated", [P, 2, HT, BANK]), sb("hidden", [P, 2, HT, BANK])
        gate_up_ready, gelu_ready, hidden_ready, out_ready, added = (
            sem("gate_up"), sem("gelu"), sem("hidden_s"), sem("out"), sem("added"))
        block = ctx.enter_context(nc.Block())
        OUT_SLOTS = 4

        @block.tensor
        def _(pe):
            pe.wait_ge(k.gate_loaded, 16)
            pe.wait_ge(k.linear_loaded, 16)

            def gate_up(u):
                e, g = divmod(u, HALVES)
                for h in range(HT):
                    if u:
                        pe.wait_ge(hidden_ready, HT * (u - 1) + h + 1)
                    for part in range(2):
                        for c in range(KT):
                            at = part * H0 + h * P
                            last = nc.tensor.matmul(k.ps[:, 2 * h + part, :], k.gate[:, c, e, at:at + P],
                                                    k.xT[:, c, g * BANK:(g + 1) * BANK], start=c == 0, stop=c == KT - 1)
                    last.then_inc(gate_up_ready, 1)

            def down(u):
                e, g = divmod(u, HALVES)
                pe.wait_ge(hidden_ready, HT * (u + 1))
                for pair in range(2):
                    n = 2 * u + pair
                    if n >= OUT_SLOTS:
                        pe.wait_ge(added, 2 * (n - OUT_SLOTS + 1))
                    for j in range(2):
                        t = 2 * pair + j
                        for h in range(HT):
                            last = nc.tensor.matmul(k.ps[:, 4 + n % OUT_SLOTS, j * C:(j + 1) * C],
                                                    act_out[:, u % 2, h, t * P:(t + 1) * P], k.linear[:, h, e, :],
                                                    start=h == 0, stop=h == HT - 1)
                    last.then_inc(out_ready, 1)

            for u in range(UNITS + 1):
                if u < UNITS:
                    gate_up(u)
                if u:
                    down(u - 1)

        @block.scalar
        def _(act):
            for u in range(UNITS):
                for h in range(HT):
                    n = HT * u + h
                    act.wait_ge(gate_up_ready, n + 1)
                    if u >= 2:
                        act.wait_ge(hidden_ready, n - 2 * HT + 1)
                    nc.scalar.activation(gated[:, u % 2, h, :], k.ps[:, 2 * h, :], ACT.Gelu_apprx_tanh).then_inc(gelu_ready, 1)

        @block.vector
        def _(dve):
            def hidden(u):
                for h in range(HT):
                    dve.wait_ge(gelu_ready, HT * u + h + 1)
                    if u >= 2 and h == 0:
                        dve.wait_ge(out_ready, 2 * (u - 1))
                    nc.vector.tensor_tensor(act_out[:, u % 2, h, :], gated[:, u % 2, h, :], k.ps[:, 2 * h + 1, :],
                                            ALU.mult).then_inc(hidden_ready, 1)

            def add(u):
                e, g = divmod(u, HALVES)
                for pair in range(2):
                    n = 2 * u + pair
                    dve.wait_ge(out_ready, n + 1)
                    for j in range(2):
                        t = 4 * g + 2 * pair + j
                        if e:
                            dve.wait_ge(added, 4 * (u - HALVES) + 2 * pair + j + 1)
                        nc.vector.scalar_tensor_tensor(out=k.x[:, t, :], in0=k.ps[:, 4 + n % OUT_SLOTS, j * C:(j + 1) * C],
                                                       scalar=k.mix[:, t, e:e + 1], in1=k.x[:, t, :],
                                                       op0=ALU.mult, op1=ALU.add).then_inc(added, 1)

            for u in range(UNITS + 1):
                if u < UNITS:
                    hidden(u)
                if u:
                    add(u - 1)


H1, HKV, DH = 16, 4, 16
GROUP = H1 // HKV
WINDOW = 32
ROT = (GROUP + 1) * HKV
PAD = 32


def windowed_qkv(nc, k):
    with ExitStack() as ctx:
        sem = lambda n: k.semaphore(f"wq_{n}")
        sb = lambda n, s: ctx.enter_context(nc.sbuf_tensor(f"wq_{n}", s, F32))
        RC = ROT * DH
        HALF = DH // 2
        rot, cross = sb("rot", [P, TILES, ROT, 2, HALF]), sb("cross", [P, 2, ROT, 2, HALF])
        square, ss, inv = sb("square", [P, 2, RC]), sb("ss", [P, TILES, ROT]), sb("inv", [P, TILES, ROT])
        padded = sb("padded", [P, 2, ROT, PAD])
        projected, raw_used, ss_ready, norm_ready = sem("projected"), sem("raw_used"), sem("ss"), sem("norm_s")
        padded_ready, turned, copied, pads_clear, v_ready = sem("padded_s"), sem("turned"), sem("copied"), sem("clear"), sem("v")
        step, floored = Steps(sem("step")), sem("floored")
        shift_done = k.shift_done
        block = ctx.enter_context(nc.Block())

        @block.tensor
        def _(pe):
            pe.wait_ge(k.wqkv_loaded, 16)
            for i in range(TILES):
                if i >= 4:
                    pe.wait_ge(raw_used, i - 3)
                for c in range(KT):
                    last = nc.tensor.matmul(k.ps[:, i % 4, 0:RC + HKV * DH], k.xT[:, c, i * P:(i + 1) * P], k.wqkv[:, c, :],
                                            start=c == 0, stop=c == KT - 1)
                last.then_inc(projected, 1)
            for i in range(TILES):
                pe.wait_ge(padded_ready, i + 1)
                if i >= 2:
                    pe.wait_ge(copied, 2 * (i - 1))
                for g in range(GROUP + 1):
                    last = nc.tensor.transpose(k.ps[:, 4 + 2 * (i % 2) + g // GROUP, (g % GROUP) * P:(g % GROUP + 1) * P],
                                               padded[:, i % 2, g * HKV:(g + 1) * HKV, :].rearrange("p h d -> p (h d)"), k.ident[:])
                last.then_inc(turned, 1)

        @block.vector
        def _(dve):
            dve.wait_ge(k.rope_loaded, 16)
            for i in range(TILES):
                dve.wait_ge(projected, i + 1)
                raw = k.ps[:, i % 4, 0:RC].rearrange("p (h s d) -> p h s d", s=2, d=HALF)
                wave = lambda n: k.rope[:, i % 2, n, :].unsqueeze(1).broadcast_to([P, ROT, HALF])
                nc.vector.tensor_tensor(rot[:, i].rearrange("p h s d -> p (h s) d"), raw.rearrange("p h s d -> p (h s) d"),
                                        k.rope[:, i % 2, 0, :].unsqueeze(1).broadcast_to([P, 2 * ROT, HALF]), ALU.mult).then_inc(step.sem, step.one())
                for half in range(2):
                    nc.vector.tensor_tensor(cross[:, i % 2, :, half, :], raw[:, :, 1 - half, :], wave(1 + half),
                                            ALU.mult).then_inc(step.sem, step.one())
                nc.vector.tensor_copy(k.v[:, i, :], k.ps[:, i % 4, RC:RC + HKV * DH]).then_inc(raw_used, 1)
                dve.wait_ge(step.sem, step.n)
                nc.vector.tensor_tensor(rot[:, i], rot[:, i], cross[:, i % 2], ALU.add).then_inc(step.sem, step.one())
                dve.wait_ge(step.sem, step.n)
                flat = rot[:, i].rearrange("p h s d -> p (h s d)")
                nc.vector.tensor_tensor(square[:, i % 2, :], flat, flat, ALU.mult).then_inc(step.sem, step.one())
                dve.wait_ge(step.sem, step.n)
                nc.vector.tensor_reduce(ss[:, i, :], square[:, i % 2, :].rearrange("p (h d) -> p h d", d=DH), AX.X,
                                        ALU.add).then_inc(ss_ready, 1)
            dve.wait_ge(ss_ready, TILES)
            nc.vector.tensor_scalar(ss[:], ss[:], 1e-24, None, ALU.max).then_inc(floored, 1)
            dve.wait_ge(norm_ready, 1)
            nc.vector.reciprocal(inv[:], inv[:]).then_inc(step.sem, step.one())
            dve.wait_ge(step.sem, step.n)
            dve.wait_ge(k.temp_loaded, 16)
            nc.vector.tensor_tensor(inv[:, :, 0:H1], inv[:, :, 0:H1], k.temp[:].unsqueeze(1).broadcast_to([P, TILES, H1]),
                                    ALU.mult).then_inc(step.sem, step.one())
            dve.wait_ge(step.sem, step.n)
            dve.wait_ge(pads_clear, 1)
            for i in range(TILES):
                if i >= 2:
                    dve.wait_ge(turned, i - 1)
                nc.vector.tensor_tensor(padded[:, i % 2, :, 0:DH], rot[:, i].rearrange("p h s d -> p h (s d)"),
                                        inv[:, i, :].unsqueeze(2).broadcast_to([P, ROT, DH]), ALU.mult).then_inc(padded_ready, 1)

        @block.gpsimd
        def _(pool):
            nc.gpsimd.memset(padded[:], 0.0).then_inc(pads_clear, 1)

        @block.scalar
        def _(act):
            act.wait_ge(floored, 1)
            nc.scalar.activation(inv[:], ss[:], ACT.Sqrt).then_inc(norm_ready, 1)
            for i in range(TILES):
                act.wait_ge(turned, i + 1)
                bank = 4 + 2 * (i % 2)
                nc.scalar.copy(k.qT[:, :, i * P:(i + 1) * P], k.ps[:, bank, :].rearrange("p (g t) -> p g t", g=GROUP)).then_inc(copied, 1)
                nc.scalar.copy(k.kT[:, i * P:(i + 1) * P], k.ps[:, bank + 1, 0:P]).then_inc(copied, 1)

        @block.sync
        def _(sp):
            sp.wait_ge(raw_used, TILES)
            sp.dma_start(k.vprev[:], k.v[P - WINDOW:P, 0:TILES:2, :]).then_inc(shift_done, 16)


def windowed_attention(nc, k):
    with ExitStack() as ctx:
        sem = lambda n: k.semaphore(f"wa_{n}")
        sb = lambda n, s: ctx.enter_context(nc.sbuf_tensor(f"wa_{n}", s, F32))
        KEYS = WINDOW + P
        UNITS = TILES * GROUP
        masked, probs = sb("masked", [P, 2, HKV, KEYS]), sb("probs", [P, 2, HKV, KEYS])
        top, ntop, total = sb("top", [P, 2, HKV]), sb("ntop", [P, 2, HKV]), sb("total", [P, TILES, HKV, GROUP])
        own, prev = sb("own", [P, 2, HKV, P]), sb("prev", [WINDOW, 2, HKV, P])
        rtotal, mixed, mixedT = sb("rtotal", [P, TILES, HKV * GROUP]), sb("mixed", [P, 2, C]), sb("mixedT", [P, 2, KT, P])
        scored, maxed, ntop_ready, exp_ready = sem("scored"), sem("maxed"), sem("ntop_s"), sem("exp")
        turned, own_ready, prev_ready, weighed = sem("turned"), sem("own_s"), sem("prev_s"), sem("weighed")
        rtotal_ready, mixed_ready, mixed_turned, mixedT_ready, projected, added = (
            sem("rtotal_s"), sem("mixed_s"), sem("mixed_turned"), sem("mixedT_s"), sem("projected"), sem("added"))
        block = ctx.enter_context(nc.Block())
        first = lambda i: 0 if i % 2 else WINDOW

        def prevs(n):
            i, g = divmod(n, GROUP)
            return (i // 2) * GROUP + (g if i % 2 else 0)

        @block.tensor
        def _(pe):
            pe.wait_ge(k.shift_done, 16)
            pe.wait_ge(k.wo_loaded, 16)

            def scores(n):
                i, g = divmod(n, GROUP)
                for j in range(HKV):
                    if n:
                        pe.wait_ge(maxed, HKV * (n - 1) + j + 1)
                    rows = slice(PAD * j, PAD * j + DH)
                    nc.tensor.matmul(k.ps[:, j, first(i):KEYS], k.qT[rows, g, i * P:(i + 1) * P],
                                     k.kT[rows, i * P + first(i) - WINDOW:(i + 1) * P],
                                     start=True, stop=True).then_inc(scored, 1)

            def turn(n):
                i, g = divmod(n, GROUP)
                pe.wait_ge(exp_ready, HKV * (n + 1))
                if n:
                    pe.wait_ge(own_ready, n)
                for j in range(HKV):
                    last = nc.tensor.transpose(k.ps[:, 4, j * P:(j + 1) * P], probs[:, n % 2, j, WINDOW:KEYS], k.ident[:])
                if i % 2:
                    if prevs(n):
                        pe.wait_ge(prev_ready, prevs(n))
                    for j in range(HKV):
                        last = nc.tensor.transpose(k.ps[0:WINDOW, 5, j * P:(j + 1) * P], probs[:, n % 2, j, 0:WINDOW], k.ident[:])
                last.then_inc(turned, 1)

            def weigh(n):
                i, g = divmod(n, GROUP)
                pe.wait_ge(own_ready, n + 1)
                if i % 2:
                    pe.wait_ge(prev_ready, prevs(n) + 1)
                if g == 0 and i:
                    pe.wait_ge(mixed_ready, i)
                for j in range(HKV):
                    h = j * GROUP + g
                    out = k.ps[:, 6, h * DH:(h + 1) * DH]
                    last = nc.tensor.matmul(out, own[:, n % 2, j, :], k.v[:, i, j * DH:(j + 1) * DH], start=True, stop=i % 2 == 0)
                    if i % 2:
                        last = nc.tensor.matmul(out, prev[:, n % 2, j, :], k.vprev[:, i // 2, j * DH:(j + 1) * DH], start=False, stop=True)
                last.then_inc(weighed, 1)

            def project(i):
                pe.wait_ge(mixed_ready, i + 1)
                if i:
                    pe.wait_ge(added, i)
                for c in range(KT):
                    last = nc.tensor.transpose(k.ps[:, 7, c * P:(c + 1) * P], mixed[:, i % 2, c * P:(c + 1) * P], k.ident[:])
                last.then_inc(mixed_turned, 1)
                pe.wait_ge(mixedT_ready, i + 1)
                for c in range(KT):
                    last = nc.tensor.matmul(k.ps[:, 7, C:2 * C], mixedT[:, i % 2, c, :], k.wo[:, c, :], start=c == 0, stop=c == KT - 1)
                last.then_inc(projected, 1)

            for n in range(UNITS + 2):
                if n < UNITS:
                    scores(n)
                if 1 <= n <= UNITS:
                    turn(n - 1)
                if n >= 2:
                    weigh(n - 2)
                if n >= 6 and n % GROUP == 2:
                    project(n // GROUP - 1 if n < UNITS + 2 else TILES - 1)
            project(TILES - 1)

        @block.vector
        def _(dve):
            dve.wait_ge(k.wmask_loaded, 16)

            def mask(n):
                i, g = divmod(n, GROUP)
                if n >= 2:
                    dve.wait_ge(exp_ready, HKV * (n - 1))
                f = first(i)
                for j in range(HKV):
                    dve.wait_ge(scored, HKV * n + j + 1)
                    nc.vector.tensor_tensor_reduce(masked[:, n % 2, j, f:KEYS],
                                                   k.ps[:, j, f:KEYS],
                                                   k.wmask[:, f:KEYS], 1.0, -3e38, ALU.add, ALU.max,
                                                   top[:, n % 2, j:j + 1]).then_inc(maxed, 1)
                dve.wait_ge(maxed, HKV * (n + 1))
                nc.vector.tensor_scalar(ntop[:, n % 2, :], top[:, n % 2, :], -1.0, None, ALU.mult).then_inc(ntop_ready, 1)

            def copy_own(n):
                i, g = divmod(n, GROUP)
                dve.wait_ge(turned, n + 1)
                if n >= 2:
                    dve.wait_ge(weighed, n - 1)
                nc.vector.tensor_copy(own[:, n % 2].rearrange("p j t -> p (j t)"), k.ps[:, 4, :]).then_inc(own_ready, 1)

            def finish(i):
                dve.wait_ge(weighed, GROUP * (i + 1))
                nc.vector.reciprocal(rtotal[:, i, :], total[:, i].rearrange("p j g -> p (j g)")).then_inc(rtotal_ready, 1)
                dve.wait_ge(rtotal_ready, i + 1)
                nc.vector.tensor_tensor(mixed[:, i % 2, :].rearrange("p (h d) -> p h d", d=DH), k.ps[:, 6, 0:C].rearrange("p (h d) -> p h d", d=DH),
                                        rtotal[:, i, :].unsqueeze(2).broadcast_to([P, H1, DH]), ALU.mult).then_inc(mixed_ready, 1)
                dve.wait_ge(projected, i + 1)
                nc.vector.tensor_tensor(k.x[:, i, :], k.ps[:, 7, C:2 * C], k.x[:, i, :], ALU.add).then_inc(added, 1)

            for n in range(UNITS + 2):
                if n < UNITS:
                    mask(n)
                if 1 <= n <= UNITS:
                    copy_own(n - 1)
                if n >= 6 and n % GROUP == 2:
                    finish(n // GROUP - 1)
            finish(TILES - 1)

        @block.scalar
        def _(act):
            def exponentials(n):
                i, g = divmod(n, GROUP)
                act.wait_ge(ntop_ready, n + 1)
                if n >= 2:
                    act.wait_ge(turned, n - 1)
                f = first(i)
                for j in range(HKV):
                    nc.scalar.activation(probs[:, n % 2, j, f:KEYS], masked[:, n % 2, j, f:KEYS], ACT.Exp,
                                         bias=ntop[:, n % 2, j:j + 1], accum_out=total[:, i, j, g:g + 1]).then_inc(exp_ready, 1)

            def copy_prev(n):
                i, g = divmod(n, GROUP)
                if i % 2:
                    act.wait_ge(turned, n + 1)
                    if prevs(n) >= 2:
                        act.wait_ge(weighed, n - 1 if g >= 2 else n - GROUP - 1 if g < 2 else 0)
                    nc.scalar.copy(prev[:, n % 2].rearrange("p j t -> p (j t)"), k.ps[0:WINDOW, 5, :]).then_inc(prev_ready, 1)

            def copy_mixed(i):
                act.wait_ge(mixed_turned, i + 1)
                nc.scalar.copy(mixedT[:, i % 2].rearrange("p c t -> p (c t)"), k.ps[:, 7, 0:C]).then_inc(mixedT_ready, 1)

            for n in range(UNITS + 2):
                if n < UNITS:
                    exponentials(n)
                if 1 <= n <= UNITS:
                    copy_prev(n - 1)
                if n >= 6 and n % GROUP == 2:
                    copy_mixed(n // GROUP - 1)
            copy_mixed(TILES - 1)


def cross_attention_1(nc, k):
    with ExitStack() as ctx:
        sem = lambda n: k.semaphore(f"xa1_{n}")
        sb = lambda n, s: ctx.enter_context(nc.sbuf_tensor(f"xa1_{n}", s, F32))
        ALPHA, D = 5.0, 32
        HEADS = P // D
        PAIRS = TILES * HEADS
        square, norm = sb("square", [P, 2, BANK]), sb("norm", [P, 2, BANK])
        floored = sb("floored", [P, 2, BANK])
        qn, kn = sb("qn", [P, TILES, C]), sb("kn", [P, TILES, C])
        expd, vT = sb("expd", [P, 2, KT, C]), sb("vT", [P, B * KT, TILES // B * HEADS, D + 1])
        outT, rden = sb("outT", [P, 2, KT, HEADS, D]), sb("rden", [P, 2, KT, HEADS])
        square_ready, summed, floor_ready, norm_ready, scaled = (
            sem("square_s"), sem("summed"), sem("floor"), sem("norm_s"), sem("scaled"))
        inv_ready = sem("inv")
        scored, exp_ready, weighed, rden_ready, outT_ready, turned, added, vT_ready = (
            sem("scored"), sem("exp_s"), sem("weighed"), sem("rden_s"), sem("outT_s"), sem("turned"), sem("added"), sem("vT_s"))
        block = ctx.enter_context(nc.Block())
        GROUPS = 2 * TILES // 2

        tile_of = lambda n: 2 * (n // 2)
        SETS = GROUPS // 2
        HEADS_OF_SET = 2 * HEADS

        def in_order(norms, heads):
            for s in range(-2, SETS):
                if s >= 0:
                    heads(s)
                if s + 2 < SETS:
                    norms(2 * (s + 2))
                    norms(2 * (s + 2) + 1)

        @block.tensor
        def _(pe):
            pe.wait_ge(k.diag_loaded, 16)

            def norms(n):
                pe.wait_ge(square_ready, n + 1)
                if n >= 2:
                    pe.wait_ge(floor_ready, n - 1)
                nc.tensor.matmul(k.ps[:, 2 + n % 2, :], k.diag[:], square[:, n % 2, :], start=True, stop=True).then_inc(summed, 1)

            def scores(n):
                i, j = divmod(n, HEADS)
                if n >= 2:
                    pe.wait_ge(exp_ready, n - 1)
                for half in range(KT):
                    last = nc.tensor.matmul(k.ps[:, n % 2, half * C:(half + 1) * C], kn[D * j:D * (j + 1), i, half * P:(half + 1) * P],
                                            qn[D * j:D * (j + 1), i, :], start=True, stop=True)
                last.then_inc(scored, 1)

            def weigh(n):
                i, j = divmod(n, HEADS)
                pe.wait_ge(exp_ready, n + 1)
                if n == 0:
                    pe.wait_ge(vT_ready, 2)
                if j == 0 and i >= 2:
                    pe.wait_ge(outT_ready, i - 1)
                for q in range(KT):
                    for half in range(KT):
                        last = nc.tensor.matmul(k.ps[:, 4 + i % 2, (q * HEADS + j) * (D + 1):(q * HEADS + j + 1) * (D + 1)],
                                                expd[:, n % 2, half, q * P:(q + 1) * P], vT[:, (i // 2) * KT + half, (i % 2) * HEADS + j, :],
                                                start=half == 0, stop=half == KT - 1)
                last.then_inc(weighed, 1)

            def turn(i):
                pe.wait_ge(outT_ready, i + 1)
                if i >= 2:
                    pe.wait_ge(added, i - 1)
                for q in range(KT):
                    last = nc.tensor.transpose(k.ps[:, 6 + i % 2, q * P:(q + 1) * P], outT[:, i % 2, q].rearrange("p h d -> p (h d)"), k.ident[:])
                last.then_inc(turned, 1)

            def heads(s):
                pe.wait_ge(scaled, 2 * (s + 1))
                for n in range(HEADS_OF_SET * s, HEADS_OF_SET * (s + 1)):
                    scores(n)
                    if n:
                        weigh(n - 1)
                    if n >= 5 and n % HEADS == 1:
                        turn(n // HEADS - 1)

            in_order(norms, heads)
            weigh(PAIRS - 1)
            turn(TILES - 1)

        @block.vector
        def _(dve):
            dve.wait_ge(k.ctxT_loaded, 16)
            nc.vector.tensor_copy(vT[:, :, :, 0:D], k.ctxT[:].rearrange("p b (g d) -> p b g d", d=D)).then_inc(vT_ready, 1)
            nc.vector.memset(vT[:, :, :, D:D + 1], 1.0).then_inc(vT_ready, 1)

            def norms(n):
                dve.wait_ge(summed, n + 1)
                if n >= 2:
                    dve.wait_ge(norm_ready, n - 1)
                nc.vector.tensor_scalar(floored[:, n % 2, :], k.ps[:, 2 + n % 2, :], 1e-24, None, ALU.max).then_inc(floor_ready, 1)
                dve.wait_ge(norm_ready, n + 1)
                nc.vector.reciprocal(norm[:, n % 2, :], norm[:, n % 2, :]).then_inc(inv_ready, 1)
                dve.wait_ge(inv_ready, n + 1)
                src, dst = (k.xn, qn) if n % 2 == 0 else (k.ctx, kn)
                i = tile_of(n)
                nc.vector.tensor_tensor(dst[:, i:i + 2, :], src[:, i:i + 2, :], norm[:, n % 2, :].rearrange("p (i c) -> p i c", i=2),
                                        ALU.mult).then_inc(scaled, 1)

            def finish(i):
                dve.wait_ge(weighed, HEADS * (i + 1))
                out = k.ps[:, 4 + i % 2, 0:KT * HEADS * (D + 1)].rearrange("p (q d) -> p q d", d=D + 1)
                nc.vector.reciprocal(rden[:, i % 2].rearrange("p q h -> p (q h)"), out[:, :, D]).then_inc(rden_ready, 1)
                dve.wait_ge(rden_ready, i + 1)
                if i >= 2:
                    dve.wait_ge(turned, i - 1)
                nc.vector.tensor_tensor(outT[:, i % 2].rearrange("p q h d -> p (q h) d"), out[:, :, 0:D],
                                        rden[:, i % 2].rearrange("p q h -> p (q h)").unsqueeze(2).broadcast_to([P, KT * HEADS, D]),
                                        ALU.mult).then_inc(outT_ready, 1)
                dve.wait_ge(turned, i + 1)
                nc.vector.tensor_tensor(k.x[:, i, :], k.ps[:, 6 + i % 2, 0:C], k.x[:, i, :], ALU.add).then_inc(added, 1)

            def heads(s):
                for i in range(2 * s, 2 * s + 2):
                    if i:
                        finish(i - 1)

            in_order(norms, heads)
            finish(TILES - 1)

        @block.scalar
        def _(act):
            act.wait_ge(k.ctx_loaded, 16)

            def norms(n):
                if n >= 2:
                    act.wait_ge(summed, n - 1)
                src = k.xn if n % 2 == 0 else k.ctx
                i = tile_of(n)
                nc.scalar.activation(square[:, n % 2, :].rearrange("p (i c) -> p i c", i=2), src[:, i:i + 2, :], ACT.Square).then_inc(square_ready, 1)
                act.wait_ge(floor_ready, n + 1)
                if n >= 2:
                    act.wait_ge(scaled, n - 1)
                nc.scalar.activation(norm[:, n % 2, :], floored[:, n % 2, :], ACT.Sqrt).then_inc(norm_ready, 1)
            def heads(s):
                for n in range(HEADS_OF_SET * s, HEADS_OF_SET * (s + 1)):
                    act.wait_ge(scored, n + 1)
                    if n >= 2:
                        act.wait_ge(weighed, n - 1)
                    nc.scalar.activation(expd[:, n % 2].rearrange("p h q -> p (h q)"), k.ps[:, n % 2, :], ACT.Exp, scale=ALPHA).then_inc(exp_ready, 1)

            in_order(norms, heads)


E1 = 8


def soft_router_1(nc, k):
    with ExitStack() as ctx:
        sem = lambda n: k.semaphore(f"sr_{n}")
        sb = lambda n, s: ctx.enter_context(nc.sbuf_tensor(f"sr_{n}", s, F32))
        OT = C // P
        UNITS = B * OT
        PAIRS = E1 // 2
        logits, shifted = sb("logits", [P, 2, E1, T]), sb("shifted", [P, 2, E1, T])
        high, low, mixed = sb("high", [P, 7, T]), sb("low", [P, 7, T]), sb("mid", [P, 3, T])
        first, second = sb("first", [P, 2, T]), sb("second", [P, 2, T])
        lse, chosen = sb("lse", [P, 2, T]), sb("chosen", [P, E1, T])
        weight, pick = sb("weight", [P, 2, OT, E1, T]), sb("pick", [P, E1, E1])
        scored, logits_ready, gap_ready, log_ready = sem("scored"), sem("logits_s"), sem("gap"), sem("log")
        lse_ready, shifted_ready, exp_ready, weight_ready = sem("lse_s"), sem("shifted_s"), sem("exp"), sem("weight_s")
        summed, share_ready, turned, shareT_ready, pick_ready = sem("summed"), sem("share"), sem("turned"), sem("shareT"), sem("pick_s")
        step, log_step = Steps(sem("step")), sem("log_step")
        block = ctx.enter_context(nc.Block())

        @block.tensor
        def _(pe):
            pe.wait_ge(k.rw1_loaded, 16)

            def scores(n):
                b, o = divmod(n, OT)
                for p in range(PAIRS):
                    if n:
                        pe.wait_ge(logits_ready, E1 * (n - 1) + 2 * p + 2)
                    for j in range(2):
                        for c in range(KT):
                            last = nc.tensor.matmul(k.ps[:, p, j * T:(j + 1) * T], k.rw1[:, c, 2 * p + j, o * P:(o + 1) * P],
                                                    k.xT[:, c, b * T:(b + 1) * T], start=c == 0, stop=c == KT - 1)
                    last.then_inc(scored, 1)

            def sums(b):
                pe.wait_ge(weight_ready, OT * (b + 1))
                if b >= 2:
                    pe.wait_ge(shareT_ready, b - 1)
                for e in range(E1):
                    for o in range(OT):
                        last = nc.tensor.matmul(k.ps[0:E1, 4 + b % 2, 0:T], pick[:, e, :], weight[:, b % 2, o, e, :],
                                                start=e == 0 and o == 0, stop=e == E1 - 1 and o == OT - 1)
                last.then_inc(summed, 1)

            def turn(b):
                pe.wait_ge(shareT_ready, b + 1)
                if b >= 2:
                    pe.wait_ge(share_ready, b - 1)
                for t in range(2):
                    last = nc.tensor.transpose(k.ps[:, 6 + b % 2, t * E1:(t + 1) * E1], k.shareT[:, b * T + t * P:b * T + (t + 1) * P], k.ident[0:E1, 0:E1])
                last.then_inc(turned, 1)

            pe.wait_ge(pick_ready, 2)
            for n in range(UNITS + 1):
                if n < UNITS:
                    scores(n)
                if n >= 3 and n % 2:
                    sums(n // 2 - 1)
            sums(B - 1)
            for b in range(B):
                turn(b)

        @block.scalar
        def _(act):
            act.wait_ge(k.rb1_loaded, 16)

            def logit(n):
                b, o = divmod(n, OT)
                for p in range(PAIRS):
                    act.wait_ge(scored, PAIRS * n + p + 1)
                    if n >= 2 and p == 0:
                        act.wait_ge(weight_ready, n - 1)
                    for j in range(2):
                        nc.scalar.activation(logits[:, n % 2, 2 * p + j, :], k.ps[:, p, j * T:(j + 1) * T], ACT.Identity,
                                             bias=k.rb1[:, o, 2 * p + j:2 * p + j + 1]).then_inc(logits_ready, 1)

            def log_of_sum(n):
                act.wait_ge(gap_ready, n + 1)
                nc.scalar.activation(lse[:, n % 2, :], lse[:, n % 2, :], ACT.Exp).then_inc(log_step, 1)
                act.wait_ge(log_step, n + 1)
                nc.scalar.activation(lse[:, n % 2, :], lse[:, n % 2, :], ACT.Ln, bias=1.0).then_inc(log_ready, 1)

            def exponentials(n):
                act.wait_ge(shifted_ready, n + 1)
                nc.scalar.activation(shifted[:, n % 2].rearrange("p e t -> p (e t)"), shifted[:, n % 2].rearrange("p e t -> p (e t)"),
                                     ACT.Exp).then_inc(exp_ready, 1)

            for n in range(UNITS + 1):
                if n:
                    log_of_sum(n - 1)
                if n < UNITS:
                    logit(n)
                if n:
                    exponentials(n - 1)

        @block.gpsimd
        def _(pool):
            for n in range(UNITS):
                pool.wait_ge(lse_ready, n + 1)
                if n >= 2:
                    pool.wait_ge(weight_ready, n - 1)
                nc.gpsimd.tensor_tensor(shifted[:, n % 2], logits[:, n % 2], lse[:, n % 2, :].unsqueeze(1).broadcast_to([P, E1, T]),
                                        ALU.subtract).then_inc(shifted_ready, 1)

        @block.vector
        def _(dve):
            nc.vector.memset(pick[:], 0.0).then_inc(pick_ready, 1)
            dve.wait_ge(pick_ready, 1)
            nc.vector.memset(pick[:].rearrange("p e m -> p (e m)")[:, 0:E1 * E1:E1 + 1], 1.0).then_inc(pick_ready, 1)

            def both(level, out, a, b_, op):
                nc.vector.tensor_tensor(out, a, b_, op).then_inc(step.sem, step.one())

            def top_two(n):
                lg = logits[:, n % 2]
                dve.wait_ge(logits_ready, E1 * (n + 1))
                both(0, high[:, 0:4], lg[:, 0:4], lg[:, 4:8], ALU.max)
                both(0, low[:, 0:4], lg[:, 0:4], lg[:, 4:8], ALU.min)
                dve.wait_ge(step.sem, step.n)
                both(1, high[:, 4:6], high[:, 0:2], high[:, 2:4], ALU.max)
                both(1, mixed[:, 0:2], high[:, 0:2], high[:, 2:4], ALU.min)
                both(1, low[:, 4:6], low[:, 0:2], low[:, 2:4], ALU.max)
                dve.wait_ge(step.sem, step.n)
                both(1, low[:, 4:6], low[:, 4:6], mixed[:, 0:2], ALU.max)
                both(2, first[:, n % 2, :], high[:, 4, :], high[:, 5, :], ALU.max)
                both(2, mixed[:, 2, :], high[:, 4, :], high[:, 5, :], ALU.min)
                dve.wait_ge(step.sem, step.n)
                both(2, low[:, 6, :], low[:, 4, :], low[:, 5, :], ALU.max)
                dve.wait_ge(step.sem, step.n)
                if n >= 2:
                    dve.wait_ge(shifted_ready, n - 1)
                both(2, second[:, n % 2, :], low[:, 6, :], mixed[:, 2, :], ALU.max)
                dve.wait_ge(step.sem, step.n)
                nc.vector.tensor_tensor(lse[:, n % 2, :], second[:, n % 2, :], first[:, n % 2, :], ALU.subtract).then_inc(gap_ready, 1)

            def add_first(n):
                dve.wait_ge(log_ready, n + 1)
                nc.vector.tensor_tensor(lse[:, n % 2, :], lse[:, n % 2, :], first[:, n % 2, :], ALU.add).then_inc(lse_ready, 1)

            def choose(n):
                b, o = divmod(n, OT)
                if n:
                    dve.wait_ge(weight_ready, n)
                nc.vector.tensor_tensor(chosen[:], logits[:, n % 2], second[:, n % 2, :].unsqueeze(1).broadcast_to([P, E1, T]),
                                        ALU.is_ge).then_inc(step.sem, step.one())
                dve.wait_ge(step.sem, step.n)
                dve.wait_ge(exp_ready, n + 1)
                if b >= 2:
                    dve.wait_ge(summed, b - 1)
                nc.vector.tensor_tensor(weight[:, b % 2, o], chosen[:], shifted[:, n % 2], ALU.mult).then_inc(weight_ready, 1)

            def collect(b):
                dve.wait_ge(summed, b + 1)
                nc.vector.tensor_copy(k.shareT[:, b * T:(b + 1) * T], k.ps[0:E1, 4 + b % 2, 0:T]).then_inc(shareT_ready, 1)

            for n in range(UNITS + 1):
                if n < UNITS:
                    top_two(n)
                if n:
                    choose(n - 1)
                if n < UNITS:
                    add_first(n)
                if n >= 4 and n % 2 == 0:
                    collect(n // 2 - 2)
            collect(B - 1)
            for b in range(B):
                dve.wait_ge(turned, b + 1)
                nc.vector.tensor_copy(k.share[:, 2 * b:2 * b + 2, :], k.ps[:, 6 + b % 2, 0:2 * E1].rearrange("p (t e) -> p t e", t=2)).then_inc(share_ready, 1)


def soft_experts_1(nc, k):
    with ExitStack() as ctx:
        sem = lambda n: k.semaphore(f"se_{n}")
        PAIRS = E1 // 2
        UNITS = (PAIRS + 1) * TILES
        BANKS = 8
        out_ready, added = sem("out"), sem("added")
        block = ctx.enter_context(nc.Block())

        @block.tensor
        def _(pe):
            pe.wait_ge(k.we1_loaded, 16)
            pe.wait_ge(k.be1_loaded, 16)
            for n in range(UNITS):
                p, t = divmod(n, TILES)
                if n >= BANKS:
                    pe.wait_ge(added, 2 * (n - BANKS + 1))
                if p < PAIRS:
                    for c in range(KT):
                        last = nc.tensor.matmul(k.ps[:, n % BANKS, :], k.xT[:, c, t * P:(t + 1) * P],
                                                k.we1[:, c, 2 * p:2 * p + 2, :].rearrange("p e o -> p (e o)"), start=c == 0, stop=c == KT - 1)
                else:
                    last = nc.tensor.matmul(k.ps[:, n % BANKS, 0:C], k.shareT[:, t * P:(t + 1) * P], k.be1[:], start=True, stop=True)
                last.then_inc(out_ready, 1)

        @block.vector
        def _(dve):
            for n in range(UNITS):
                p, t = divmod(n, TILES)
                dve.wait_ge(out_ready, n + 1)
                if p:
                    dve.wait_ge(added, 2 * (n - TILES + 1))
                if p == PAIRS:
                    nc.vector.tensor_tensor(k.x[:, t, :], k.ps[:, n % BANKS, 0:C], k.x[:, t, :], ALU.add).then_inc(k.x_final, 1)
                    continue
                for j in range(2):
                    if j:
                        dve.wait_ge(added, 2 * n + 1)
                    nc.vector.scalar_tensor_tensor(out=k.x[:, t, :], in0=k.ps[:, n % BANKS, j * C:(j + 1) * C],
                                                   scalar=k.share[:, t, 2 * p + j:2 * p + j + 1], in1=k.x[:, t, :],
                                                   op0=ALU.mult, op1=ALU.add).then_inc(added, 1)


I32 = mybir.dt.int32
NK, DK, NV, DV = 16, 128, 32, 128
PV = NV // NK
TAPS = 4
BLK = 32
GB = P // BLK
UNITS = TILES * PV
NEG = -1e30
FRONT = 1 + 2 * PV
RMS_EPS, NORM_EPS2 = 1e-6, 1e-24


def decays(nc, k):
    with ExitStack() as ctx:
        sem = lambda n: k.semaphore(f"dc_{n}")
        sb = lambda n, s: ctx.enter_context(nc.sbuf_tensor(f"dc_{n}", s, F32))
        eb, a, mag, soft, rate = sb("eb", [P, TILES, NV]), sb("a", [P, TILES, NV]), sb("mag", [P, TILES, NV]), sb("soft", [P, TILES, NV]), sb("rate", [P, NV])
        ld, rows = sb("ld", [P, TILES, NV]), sb("rows", [NV, 2, TOK])
        projected, eb_ready, mag_ready, rate_ready, exp_ready, soft_ready = (
            sem("projected"), sem("eb_s"), sem("mag_s"), sem("rate_s"), sem("exp"), sem("soft_s"))
        ld_ready, summed, ccol_ready, beta_ready, turned, rows_ready, stored = (
            sem("ld_s"), sem("summed"), sem("ccol"), sem("beta"), sem("turned"), sem("rows_s"), sem("stored"))
        step = Steps(sem("step"))
        block = ctx.enter_context(nc.Block())
        W2 = 2 * NV

        @block.tensor
        def _(pe):
            pe.wait_ge(k.wba_loaded, 16)
            for i in range(TILES):
                for c in range(KT):
                    last = nc.tensor.matmul(k.ps[:, 0, i * W2:(i + 1) * W2], k.xT[:, c, i * P:(i + 1) * P], k.wba[:, c, :],
                                            start=c == 0, stop=c == KT - 1)
            last.then_inc(projected, 1)
            pe.wait_ge(ld_ready, 1)
            for i in range(TILES):
                out = k.ps[:, 1, i * NV:(i + 1) * NV]
                last = nc.tensor.matmul(out, k.upto[:], ld[:, i, :], start=True, stop=i % 2 == 0)
                if i % 2:
                    last = nc.tensor.matmul(out, k.ones[:], ld[:, i - 1, :], start=False, stop=True)
            last.then_inc(summed, 1)
            pe.wait_ge(ccol_ready, 1)
            pe.wait_ge(beta_ready, 1)
            for n, src in enumerate((k.ccol, k.beta)):
                for i in range(TILES):
                    last = nc.tensor.transpose(k.ps[0:NV, 2 + 2 * n + i // 4, (i % 4) * P:(i % 4 + 1) * P], src[:, i, :], k.ident[:])
            last.then_inc(turned, 1)

        @block.scalar
        def _(act):
            act.wait_ge(projected, 1)
            raw = k.ps[:, 0, :].rearrange("p (i n h) -> p i n h", n=2, h=NV)
            nc.scalar.activation(eb[:], raw[:, :, 0, :], ACT.Exp, scale=-1.0).then_inc(eb_ready, 1)
            act.wait_ge(k.alog_loaded, 16)
            nc.scalar.activation(rate[:], k.alog[:], ACT.Exp).then_inc(rate_ready, 1)
            act.wait_ge(mag_ready, 1)
            nc.scalar.activation(soft[:], mag[:], ACT.Exp, scale=-1.0).then_inc(exp_ready, 1)
            act.wait_ge(exp_ready, 1)
            nc.scalar.activation(soft[:], soft[:], ACT.Ln, bias=1.0).then_inc(soft_ready, 1)

        @block.vector
        def _(dve):
            dve.wait_ge(eb_ready, 1)
            dve.wait_ge(k.dtb_loaded, 16)
            raw = k.ps[:, 0, :].rearrange("p (i n h) -> p i n h", n=2, h=NV)
            nc.vector.tensor_tensor(a[:], raw[:, :, 1, :], k.dtb[:].unsqueeze(1).broadcast_to([P, TILES, NV]), ALU.add).then_inc(step.sem, step.one())
            nc.vector.tensor_scalar(eb[:], eb[:], 1.0, None, ALU.add).then_inc(step.sem, step.one())
            dve.wait_ge(step.sem, step.n)
            nc.vector.scalar_tensor_tensor(out=mag[:], in0=a[:], scalar=-1.0, in1=a[:], op0=ALU.mult, op1=ALU.max).then_inc(mag_ready, 1)
            nc.vector.reciprocal(k.beta[:], eb[:]).then_inc(beta_ready, 1)
            dve.wait_ge(soft_ready, 1)
            nc.vector.scalar_tensor_tensor(out=soft[:], in0=a[:], scalar=0.0, in1=soft[:], op0=ALU.max, op1=ALU.add).then_inc(step.sem, step.one())
            dve.wait_ge(step.sem, step.n)
            dve.wait_ge(rate_ready, 1)
            nc.vector.scalar_tensor_tensor(out=ld[:], in0=soft[:], scalar=-1.0, in1=rate[:].unsqueeze(1).broadcast_to([P, TILES, NV]),
                                           op0=ALU.mult, op1=ALU.mult).then_inc(ld_ready, 1)
            dve.wait_ge(summed, 1)
            nc.vector.tensor_copy(k.ccol[:].rearrange("p i h -> p (i h)"), k.ps[:, 1, 0:TILES * NV]).then_inc(ccol_ready, 1)
            dve.wait_ge(turned, 1)
            for n in range(2):
                for g in range(2):
                    nc.vector.tensor_copy(rows[:, n, g * BANK:(g + 1) * BANK], k.ps[0:NV, 2 + 2 * n + g, :]).then_inc(rows_ready, 1)

        @block.sync
        def _(sp):
            sp.wait_ge(rows_ready, 4)
            sp.dma_start(k.crow_d, rows[:, 0, :]).then_inc(stored, 16)
            sp.dma_start(k.brow_d, rows[:, 1, :]).then_inc(stored, 16)
            sp.wait_ge(stored, 32)


def conv_taps(nc, dve, bank, out, taps, done):
    raw, acc = bank.rearrange("p (b t) -> p b t", b=2), out.rearrange("p (b t) -> p b t", b=2)
    for n in range(TAPS - 1):
        back = n + 1
        done(n, nc.vector.scalar_tensor_tensor(out=acc[:, :, back:T], in0=raw[:, :, 0:T - back], scalar=taps[:, TAPS - 1 - back:TAPS - back],
                                               in1=acc[:, :, back:T], op0=ALU.mult, op1=ALU.add))


def is_first(n, of=1):
    return isinstance(n, int) and n < of


class BlockInverse:

    def __init__(self, nc, k, ctx, name):
        sem = lambda n: k.semaphore(f"{name}_{n}")
        sb = lambda n, s: ctx.enter_context(nc.sbuf_tensor(f"{name}_{n}", s, F32))
        self.nc, self.k = nc, k
        self.gram, self.c, self.b = sb("gram", [P, BLK, BLK]), sb("c", [P, BLK]), sb("b", [P, BLK])
        self.low, self.inv = sb("low", [P, BLK, BLK]), sb("inv", [P, BLK, BLK])
        self.invT = self.gram
        self.w, self.prod = sb("w", [P, BLK]), sb("prod", [P, 256])
        self.loaded, self.w_step, self.w_ready, self.gap_ready, self.floor_ready = sem("loaded"), sem("w_step"), sem("w_s"), sem("gap"), sem("floor")
        self.exp_ready, self.seeded, self.times, self.product, self.updated = sem("exp"), sem("seeded"), sem("times"), sem("product"), sem("updated")
        self.done, self.invT_ready, self.stored = sem("done"), sem("invT_s"), sem("stored")

    def load(self, sp, m, n):
        k = self.k
        if not is_first(n):
            sp.wait_ge(self.done, n)
        for e in range(2):
            for v in range(PV):
                at = (2 * e + v) * BLK
                sp.dma_start(self.gram[at:at + BLK].rearrange("p s t -> p (s t)"), k.gram_d[bass.ds(2 * m + e, 1)].rearrange("o q f -> (o q) f")).then_inc(self.loaded, 16)
        for dst, src in ((self.c, k.crow_d), (self.b, k.brow_d)):
            sp.dma_start(dst[:], src[bass.ds(4 * m, 4)].rearrange("h (q t) -> (h q) t", t=BLK)).then_inc(self.loaded, 16)

    def vector_weights(self, dve, n):
        nc = self.nc
        dve.wait_ge(self.loaded, 96 * (n + 1))
        if not is_first(n):
            dve.wait_ge(self.done, n)
        diag = self.gram[:].rearrange("p s t -> p (s t)")[:, 0:BLK * BLK:BLK + 1]
        nc.vector.tensor_scalar(self.w[:], diag, NORM_EPS2, None, ALU.max).then_inc(self.w_step, 1)
        dve.wait_ge(self.w_step, 2 * n + 1)
        nc.vector.reciprocal(self.w[:], self.w[:]).then_inc(self.w_step, 1)
        dve.wait_ge(self.w_step, 2 * n + 2)
        nc.vector.tensor_tensor(self.w[:], self.w[:], self.b[:], ALU.mult).then_inc(self.w_ready, 1)

    def vector_floor(self, dve, n):
        dve.wait_ge(self.gap_ready, n + 1)
        self.nc.vector.tensor_scalar(self.low[:, :, 1:], self.low[:, :, 1:], 0.0, None, ALU.min).then_inc(self.floor_ready, 1)

    def scalar_exp(self, act, n):
        act.wait_ge(self.floor_ready, n + 1)
        self.nc.scalar.activation(self.low[:, :, 1:], self.low[:, :, 1:], ACT.Exp).then_inc(self.exp_ready, 1)

    def vector_transpose(self, dve, n):
        dve.wait_ge(self.done, n + 1)
        if not is_first(n):
            dve.wait_ge(self.stored, 32 * n)
        self.nc.vector.tensor_copy(self.invT[:].rearrange("p k i -> p i k"), self.inv[:]).then_inc(self.invT_ready, 1)

    def store(self, sp, n):
        sp.wait_ge(self.invT_ready, n + 1)
        sp.dma_start(self.k.inv_d, self.inv[:].rearrange("p i k -> p (i k)")).then_inc(self.stored, 16)
        sp.dma_start(self.k.invT_d, self.invT[:].rearrange("p i k -> p (i k)")).then_inc(self.stored, 16)
        sp.wait_ge(self.stored, 32 * (n + 1))

    def invert(self, pool, n):
        nc, low, inv = self.nc, self.low, self.inv
        pool.wait_ge(self.loaded, 96 * (n + 1))
        if not is_first(n):
            pool.wait_ge(self.done, n)
            pool.wait_ge(self.stored, 32 * n)
        full = [P, BLK, BLK - 1]
        nc.gpsimd.tensor_tensor(low[:, :, 1:], self.c[:, 0:BLK - 1].unsqueeze(1).broadcast_to(full), self.c[:].unsqueeze(2).broadcast_to(full),
                                ALU.subtract).then_inc(self.gap_ready, 1)
        nc.gpsimd.memset(inv[:], 0.0).then_inc(self.seeded, 1)
        pool.wait_ge(self.exp_ready, n + 1)
        nc.gpsimd.tensor_tensor(low[:, :, 1:], low[:, :, 1:], self.gram[:, :, 1:], ALU.mult).then_inc(self.times, 1)
        pool.wait_ge(self.times, 2 * n + 1)
        pool.wait_ge(self.w_ready, n + 1)
        pool.wait_ge(self.seeded, 2 * n + 1)
        nc.gpsimd.tensor_tensor(low[:, :, 1:], low[:, :, 1:], self.w[:].unsqueeze(2).broadcast_to(full), ALU.mult).then_inc(self.times, 1)
        nc.gpsimd.memset(inv[:].rearrange("p i k -> p (i k)")[:, 0:BLK * BLK:BLK + 1], 1.0).then_inc(self.seeded, 1)
        pool.wait_ge(self.times, 2 * n + 2)
        pool.wait_ge(self.seeded, 2 * n + 2)
        for j in range(BLK - 1):
            rows, cols = BLK - 1 - j, j + 1
            prod = self.prod[:, 0:rows * cols].rearrange("p (i k) -> p i k", k=cols)
            if j:
                pool.wait_ge(self.updated, (BLK - 2) * n + j)
            nc.gpsimd.tensor_tensor(prod, low[:, j, j + 1:].unsqueeze(2).broadcast_to([P, rows, cols]),
                                    inv[:, j, 0:cols].unsqueeze(1).broadcast_to([P, rows, cols]), ALU.mult).then_inc(self.product, 1)
            pool.wait_ge(self.product, (BLK - 1) * n + j + 1)
            nc.gpsimd.tensor_tensor(inv[:, j + 1:, 0:cols], inv[:, j + 1:, 0:cols], prod, ALU.subtract).then_inc(
                self.updated if j < BLK - 2 else self.done, 1)


def keys(nc, k):
    with ExitStack() as ctx:
        sem = lambda n: k.semaphore(f"ks_{n}")
        sb = lambda n, s: ctx.enter_context(nc.sbuf_tensor(f"ks_{n}", s, F32))
        wk = [sb(f"wk{e}", [P, KT * DK + TAPS]) for e in range(2)]
        kc = [sb(f"kc{e}", [P, TOK]) for e in range(2)]
        gd = [sb(f"gd{e}", [P, TILES, BLK]) for e in range(2)]
        square, ssk = sb("square", [P, TOK]), sb("ssk", [P, NK, TILES])
        loaded = [sem(f"loaded{e}") for e in range(2)]
        kT_stored = [sem(f"kT_stored{e}") for e in range(2)]
        gd_stored = [sem(f"gd_stored{e}") for e in range(2)]
        projected, last_tap, tap, conv_done = sem("projected"), sem("last_tap"), sem("tap"), sem("conv_done")
        square_ready, norms, ssk_ready, grams, gd_ready = sem("square_s"), sem("norms"), sem("ssk_s"), sem("grams"), sem("gd_s")
        root, w_step = sem("root"), sem("w_step")
        inverse = BlockInverse(nc, k, ctx, "k_inv")
        block = ctx.enter_context(nc.Block())
        G = 2
        EARLY = 3

        @block.sync
        def _(sp):
            def head(m, e, h, first=False):
                if not first:
                    sp.wait_ge(conv_done, G * (h - 1))
                sp.dma_start(wk[e][:], k.wk_d[bass.ds(h, 1)].rearrange("o p f -> (o p) f")).then_inc(loaded[e], 16)

            def store(m, e, h):
                sp.wait_ge(conv_done, G * (h + 1))
                sp.dma_start(k.kT_d[bass.ds(h, 1)].rearrange("o p f -> (o p) f"), kc[e][:]).then_inc(kT_stored[e], 16)
                sp.wait_ge(gd_ready, GB * (h + 1))
                sp.dma_start(k.gram_d[bass.ds(h, 1)].rearrange("o (i g) (s t) -> (o g s) i t", g=GB, t=BLK), gd[e][:]).then_inc(gd_stored[e], 16)

            head(0, 0, 0, True)
            head(0, 1, 1, True)
            for e in range(2):
                head(1, e, 2 + e)
                store(0, e, e)
            for e in range(2):
                sp.wait_ge(gd_stored[e], 16)
            inverse.load(sp, 0, 0)
            with sp.Fori(1, NK // 2 - 1) as m:
                for e in range(2):
                    head(m + 1, e, 2 * m + 2 + e)
                    store(m, e, 2 * m + e)
            for e in range(2):
                store(NK // 2 - 1, e, NK - 2 + e)
            inverse.store(sp, 0)
            for e in range(2):
                sp.wait_ge(kT_stored[e], 16 * NK // 2)
                sp.wait_ge(gd_stored[e], 16 * NK // 2)

        @block.tensor
        def _(pe):
            def project(m, e, h):
                pe.wait_ge(loaded[e], 16 * (m + 1))
                for g in range(G):
                    if not is_first(h, 2):
                        pe.wait_ge(conv_done, G * (h - 2) + g + 1)
                    for c in range(KT):
                        last = nc.tensor.matmul(k.ps[:, 2 * e + g, :], wk[e][:, c * DK:(c + 1) * DK], k.xT[:, c, g * BANK:(g + 1) * BANK],
                                                start=c == 0, stop=c == KT - 1)
                    last.then_inc(projected, 1)

            def measure(m, e, h):
                pe.wait_ge(conv_done, G * (h + 1))
                if not is_first(h):
                    pe.wait_ge(gd_ready, GB * h)
                for i in range(TILES):
                    tile = kc[e][:, i * P:(i + 1) * P]
                    last = nc.tensor.matmul(k.ps[:, 4 + i // 4, (i % 4) * P:(i % 4 + 1) * P], tile, tile, start=True, stop=True)
                last.then_inc(grams, 1)
                pe.wait_ge(square_ready, h + 1)
                if not is_first(h, 2):
                    pe.wait_ge(ssk_ready, h - 1)
                for i in range(TILES):
                    last = nc.tensor.matmul(k.ps[:, 6 + e, i:i + 1], square[:, i * P:(i + 1) * P], k.ones[:, 0:1], start=True, stop=True)
                last.then_inc(norms, 1)

            project(0, 0, 0)
            project(0, 1, 1)
            measure(0, 0, 0)
            project(1, 0, 2)
            measure(0, 1, 1)
            project(1, 1, 3)
            measure(1, 0, 2)
            with pe.Fori(2, NK // 2) as m:
                project(m, 0, 2 * m)
                measure(m - 1, 1, 2 * m - 1)
                project(m, 1, 2 * m + 1)
                measure(m, 0, 2 * m)
            measure(NK // 2 - 1, 1, NK - 1)

        @block.scalar
        def _(act):
            def tap(m, e, h, first=False):
                if not first:
                    act.wait_ge(kT_stored[e], 16 * m)
                    act.wait_ge(grams, h - 1)
                    act.wait_ge(square_ready, h - 1)
                for g in range(G):
                    act.wait_ge(projected, G * h + g + 1)
                    nc.scalar.activation(kc[e][:, g * BANK:(g + 1) * BANK], k.ps[:, 2 * e + g, :], ACT.Copy,
                                         scale=wk[e][:, KT * DK + TAPS - 1:KT * DK + TAPS]).then_inc(last_tap, 1)

            def rest(m, e, h):
                act.wait_ge(conv_done, G * (h + 1))
                if not is_first(h):
                    act.wait_ge(norms, h)
                nc.scalar.activation(square[:], kc[e][:], ACT.Square).then_inc(square_ready, 1)
                act.wait_ge(grams, h + 1)
                if not is_first(h, 2):
                    act.wait_ge(gd_stored[e], 16 * m)
                for g in range(GB):
                    rows = slice(g * BLK, (g + 1) * BLK)
                    nc.scalar.copy(gd[e][rows, :, :], k.ps[rows, 4:6, :].rearrange("p a (i t) -> p (a i) t", t=P)[:, :, g * BLK:(g + 1) * BLK]).then_inc(gd_ready, 1)

            tap(0, 0, 0, True)
            tap(0, 1, 1, True)
            rest(0, 0, 0)
            for m in range(1, EARLY):
                tap(m, 0, 2 * m)
                rest(m - 1, 1, 2 * m - 1)
                tap(m, 1, 2 * m + 1)
                rest(m, 0, 2 * m)
            inverse.scalar_exp(act, 0)
            with act.Fori(EARLY, NK // 2) as m:
                tap(m, 0, 2 * m)
                rest(m - 1, 1, 2 * m - 1)
                tap(m, 1, 2 * m + 1)
                rest(m, 0, 2 * m)
            rest(NK // 2 - 1, 1, NK - 1)

        @block.vector
        def _(dve):
            def convolve(m, e, h):
                for g in range(G):
                    dve.wait_ge(last_tap, G * h + g + 1)
                    u = G * h + g

                    def done(n, ins):
                        if n < TAPS - 2:
                            ins.then_inc(tap, 1)
                            dve.wait_ge(tap, (TAPS - 2) * u + n + 1)
                        else:
                            ins.then_inc(conv_done, 1)
                    conv_taps(nc, dve, k.ps[:, 2 * e + g, :], kc[e][:, g * BANK:(g + 1) * BANK], wk[e][:, KT * DK:KT * DK + TAPS], done)

            def keep(m, e, h):
                dve.wait_ge(norms, h + 1)
                nc.vector.tensor_scalar(ssk[:, h, :] if isinstance(h, int) else ssk[:, bass.ds(h, 1), :].rearrange("p o i -> p (o i)"),
                                        k.ps[:, 6 + e, 0:TILES], NORM_EPS2, None, ALU.max).then_inc(ssk_ready, 1)

            def pair(m):
                convolve(m - 1, 1, 2 * m - 1)
                keep(m - 1, 0, 2 * m - 2)
                convolve(m, 0, 2 * m)
                keep(m - 1, 1, 2 * m - 1)

            convolve(0, 0, 0)
            for m in range(1, EARLY):
                pair(m)
            inverse.vector_weights(dve, 0)
            inverse.vector_floor(dve, 0)
            with dve.Fori(EARLY, NK // 2) as m:
                pair(m)
            convolve(NK // 2 - 1, 1, NK - 1)
            keep(NK // 2 - 1, 0, NK - 2)
            keep(NK // 2 - 1, 1, NK - 1)
            dve.wait_ge(ssk_ready, NK)
            nc.vector.reciprocal(k.rk[:], ssk[:]).then_inc(w_step, 1)
            dve.wait_ge(w_step, 1)
            for v in range(PV):
                nc.vector.tensor_tensor(k.w[:, :, v:NV:PV], k.beta[:, :, v:NV:PV], k.rk[:].rearrange("p h i -> p i h"), ALU.mult).then_inc(w_step, 1)
            dve.wait_ge(w_step, 1 + PV)
            fast_rsqrt(nc, dve, ssk[:].rearrange("p h i -> p (h i)"), k.rk[:].rearrange("p h i -> p (h i)"), k.root_tmp[:, 0:NK * TILES], root, 0)
            nc.vector.tensor_tensor(k.kabs[:], ssk[:], k.rk[:], ALU.mult)
            inverse.vector_transpose(dve, 0)

        @block.gpsimd
        def _(pool):
            inverse.invert(pool, 0)


NEWTON = 3
RSQRT_STEPS = 1 + 3 * NEWTON


def fast_rsqrt(nc, dve, x, y, tmp, step, n):
    at = [RSQRT_STEPS * n]

    def then(ins):
        at[0] = at[0] + 1
        ins.then_inc(step, 1)
        dve.wait_ge(step, at[0])
    then(nc.vector.tensor_scalar(y.bitcast(I32), x.bitcast(I32), -0.5, float(0x5F3759DF), ALU.mult, ALU.add))
    for _ in range(NEWTON):
        then(nc.vector.tensor_tensor(tmp, y, y, ALU.mult))
        then(nc.vector.scalar_tensor_tensor(out=tmp, in0=tmp, scalar=-0.5, in1=x, op0=ALU.mult, op1=ALU.mult))
        then(nc.vector.scalar_tensor_tensor(out=y, in0=tmp, scalar=1.5, in1=y, op0=ALU.add, op1=ALU.mult))


def heads(nc, k):
    with ExitStack() as ctx:
        sem = lambda n: k.semaphore(f"hd_{n}")
        sb = lambda n, s: ctx.enter_context(nc.sbuf_tensor(f"hd_{n}", s, F32))
        two = lambda n, s: [sb(f"{n}{e}", s) for e in range(2)]
        two_sems = lambda n: [sem(f"{n}{e}") for e in range(2)]
        EC, E1, EW = 1, 2 + T, 2 + T + P
        wf, wo, cbc, kT, qT = two("wf", [P, KT * FRONT * P + 12]), two("wo", [P, PV, C]), two("cbc", [P, PV, B, T]), two("kT", [P, TOK]), sb("qT", [P, TOK])
        vT, th, sz = sb("vT", [P, PV, TOK]), two("th", [P, BANK]), two("sz", [P, PV, TOK])
        E = [sb(f"E{b}", [P, PV, EW]) for b in range(B)]
        bp0, bp1 = sb("bp0", [P, B, PV, 2, T]), sb("bp1", [P, B, PV, 2, P])
        Z, M = two("Z", [P, UNITS, P]), two("M", [P, UNITS, 2 * BLK])
        t1, square = sb("t1", [P, UNITS, BLK]), sb("square", [P, TOK])
        t2 = square[:].rearrange("p (u k) -> p u k", k=2 * BLK)
        R, U, gT = sb("R", [P, B, 2, PV, P]), sb("U", [P, B, 2, PV, P]), two("gT", [P, PV, 2 * P])
        O = k.xn[:].rearrange("p i (c d) -> p (i c) d", d=P).rearrange("p (b v c) d -> p b v c d", b=B, v=PV)
        osq = U[:].rearrange("p b c v d -> p (b c v) d")
        ssq, ms, inv, tmp, floor, nwh = two("ssq", [P, TILES]), sb("ms", [P, 16]), sb("rms", [P, 16]), sb("tmp", [P, 16]), sb("floor", [P, TILES]), sb("nwh", [P, 1])
        wf_loaded, wo_loaded, in_loaded, zm_loaded = two_sems("wf_l"), two_sems("wo_l"), two_sems("in_l"), two_sems("zm_l")
        cleared, pads, nwh_ready = sem("cleared"), sem("pads"), sem("nwh_s")
        g_ready, q_proj, v_proj, z_proj, v_turned = sem("g"), sem("q_proj"), sem("v_proj"), sem("z_proj"), sem("v_turned")
        t1_ready, l1_ready, t2_ready, l2_ready, u0_ready, x1_ready, u1_ready, o_ready = (sem(n) for n in ("t1_p", "l1_p", "t2_p", "l2_p", "u0_p", "x1_p", "u1_p", "o_p"))
        qn_ready, turned, y_ready = sem("qn"), sem("turned"), sem("y")
        bp_ready, r_ready, q_tap, q_conv, v_tap, v_conv, sz_ready, x1_done, gT_ready, added, arg_ready, q_kept, scaled = (
            sem(n) for n in ("bp", "r", "q_tap", "q_conv", "v_tap", "v_conv", "sz_s", "x1_d", "gT_s", "added", "arg_s", "q_kept", "scaled"))
        e_ready, q_last, v_last, th_ready, t1_out, l1_out, t2_out, l2_out, u0_out, u1_out, q_square, o_out, o_square = (
            sem(n) for n in ("e", "q_last", "v_last", "th_s", "t1_o", "l1_o", "t2_o", "l2_o", "u0_o", "u1_o", "q_square", "o_o", "o_sq"))
        chain, root = sem("chain"), sem("root")
        passed, weights_used = sem("passed"), sem("weights_used")
        inverse = BlockInverse(nc, k, ctx, "h_inv")
        block = ctx.enter_context(nc.Block())
        G = 2
        TAP0 = KT * FRONT * P
        LAST = NK // 2 - 1
        taps_of = lambda e, part: wf[e][:, TAP0 + part * TAPS:TAP0 + (part + 1) * TAPS]

        def after(m, e):
            return (m, 1, 2 * m + 1) if e == 0 else (m + 1, 0, 2 * m + 2)

        def every_head(eng, body):
            body(0, 0, False, True)
            body(0, 1, True, True)
            with eng.Fori(1, LAST) as m:
                body(m, 0, True, True)
                body(m, 1, True, True)
            body(LAST, 0, True, True)
            body(LAST, 1, True, False)

        unit = lambda b, c, v: v * TILES + 2 * b + c
        pick = lambda t, h: t[:, h, :] if isinstance(h, int) else t[:, bass.ds(h, 1), :].rearrange("p o i -> p (o i)")
        col = lambda t, i, h: t[:, i, h:h + 1] if isinstance(h, int) else t[:, i, bass.ds(h, 1)]

        @block.gpsimd
        def _(pool):
            for e in range(2):
                nc.gpsimd.memset(Z[e][:], 0.0).then_inc(cleared, 1)
                nc.gpsimd.memset(M[e][:], 0.0).then_inc(cleared, 1)
            for b in range(B):
                nc.gpsimd.memset(E[b][:], 0.0).then_inc(pads, 1)
            inverse.invert(pool, 0)
            with pool.Fori(1, LAST) as n:
                inverse.invert(pool, n)

        @block.sync
        def _(sp):
            def front_weights(e, h):
                sp.dma_start(wf[e][:], k.wf_d[bass.ds(h, 1)].rearrange("o p f -> (o p) f")).then_inc(wf_loaded[e], 16)

            def inputs(e, h):
                sp.dma_start(cbc[e][:].rearrange("p v b t -> p (v b t)"), k.crow_d[bass.ds(PV * h, PV)].rearrange("v f -> (v f)").unsqueeze(0)
                             .broadcast_to([P, PV * TOK])).then_inc(in_loaded[e], 16)
                sp.dma_start(kT[e][:], k.kT_d[bass.ds(h, 1)].rearrange("o p f -> (o p) f")).then_inc(in_loaded[e], 16)

            def blocks(e):
                for src, dst, n in ((k.invT_d, Z[e], GB), (k.inv_d, M[e], GB - 1)):
                    src = src.rearrange("(e u g) (i k) -> e g i u k", e=2, g=GB, k=BLK)
                    for g in range(n):
                        at = g * BLK if n == GB else (g % 2) * BLK
                        sp.dma_start(dst[g * BLK:(g + 1) * BLK, :, at:at + BLK], src[e, g]).then_inc(zm_loaded[e], 16)

            def body(m, e, prev, nxt):
                h = 2 * m + e
                m1, e1, h1 = after(m, e)
                if nxt and not (m is LAST and e == 0):
                    sp.wait_ge(z_proj, 2 * PV * (h + 1))
                    sp.sem_inc(weights_used, 1)
                    sp.wait_ge(v_conv, PV * G * (h + 1))
                    front_weights(e, h + 2)
                if not is_first(h, 2):
                    sp.wait_ge(y_ready, B * (h - 1))
                sp.dma_start(wo[e][:].rearrange("p v c -> p (v c)"), k.wo_d[bass.ds(h, 1)].rearrange("o p f -> (o p) f")).then_inc(wo_loaded[e], 16)
                if nxt and not is_first(h):
                    sp.wait_ge(g_ready, B * h)
                    sp.wait_ge(arg_ready, B * h)
                if nxt:
                    inputs(e1, h1)
                if nxt and e == 0 and m is not LAST:
                    inverse.load(sp, m + 1, m)
                if nxt and e == 1:
                    for x in range(2):
                        sp.wait_ge(zm_loaded[x], 16 * (2 * GB - 1) * (m + 1))
                    inverse.store(sp, m)
                if nxt and not is_first(h):
                    sp.wait_ge(u1_ready, 2 * h)
                if nxt:
                    blocks(e1)

            front_weights(0, 0)
            front_weights(1, 1)
            inputs(0, 0)
            sp.wait_ge(cleared, 4)
            blocks(0)
            every_head(sp, body)

        @block.tensor
        def _(pe):
            def project(part, e, g, done):
                for c in range(KT):
                    at = (c * FRONT + part) * P
                    last = nc.tensor.matmul(k.ps[:, g, :], wf[e][:, at:at + P], k.xT[:, c, g * BANK:(g + 1) * BANK], start=c == 0, stop=c == KT - 1)
                last.then_inc(done, 1)

            def project_q(m, e, h, first=False):
                pe.wait_ge(wf_loaded[e], 16 * (m + 1))
                for g in range(G):
                    if not first:
                        pe.wait_ge(sz_ready, 4 * h - 2 + g + 1)
                    project(0, e, g, q_proj)

            def project_v(v, e, h, halves=range(2)):
                for g in halves:
                    if v == 0:
                        pe.wait_ge(q_conv, G * h + g + 1)
                    else:
                        pe.wait_ge(v_conv, 4 * h + g + 1)
                    project(1 + v, e, g, v_proj)

            def project_z(v, e, h, halves=range(2)):
                for g in halves:
                    if v == 0:
                        pe.wait_ge(v_conv, 4 * h + 2 + g + 1)
                    else:
                        pe.wait_ge(sz_ready, 4 * h + g + 1)
                    project(1 + PV + v, e, g, z_proj)

            def norms_q(e, h, first=False):
                pe.wait_ge(q_square, h + 1)
                for i in range(TILES):
                    last = nc.tensor.matmul(k.ps[:, 6, i:i + 1], square[:, i * P:(i + 1) * P], k.ones[:, 0:1], start=True, stop=True)
                last.then_inc(qn_ready, 1)

            def grams(m, e, h, b):
                if b == 0:
                    pe.wait_ge(in_loaded[e], 32 * (m + 1))
                    pe.wait_ge(q_conv, G * (h + 1))
                if b >= 2:
                    pe.wait_ge(bp_ready, B * h + b - 1)
                elif not is_first(h):
                    pe.wait_ge(o_out, B * h - 2 + 2 * b)
                bank = 2 + 2 * (b % 2)
                first, seq, second = slice(b * T, b * T + P), slice(b * T, (b + 1) * T), slice(b * T + P, (b + 1) * T)
                for n, src in enumerate((kT[e], qT)):
                    nc.tensor.matmul(k.ps[:, bank, n * T:(n + 1) * T], kT[e][:, first], src[:, seq], start=True, stop=True)
                    last = nc.tensor.matmul(k.ps[:, bank + 1, n * P:(n + 1) * P], kT[e][:, second], src[:, second], start=True, stop=True)
                last.then_inc(g_ready, 1)

            def turn_v(h, b):
                if b == 0:
                    pe.wait_ge(v_conv, 4 * (h + 1))
                    pe.wait_ge(q_kept, h + 1)
                elif b == 1:
                    if not is_first(h):
                        pe.wait_ge(l2_out, 2 * h)
                    if not is_first(h, 2):
                        pe.wait_ge(added, B * (h - 1))
                else:
                    pe.wait_ge(r_ready, B * h + b - 1)
                for c in range(2):
                    for v in range(PV):
                        at = (c * PV + v) * P
                        tokens = b * T + c * P
                        last = nc.tensor.transpose(k.ps[:, 6 + b % 2, at:at + P], vT[:, v, tokens:tokens + P], k.ident[:])
                last.then_inc(v_turned, 1)

            def turn(h, q, bank_free):
                pe.wait_ge(*bank_free)
                pe.wait_ge(scaled, B * h + q + 1)
                for v in range(PV):
                    for c in range(2):
                        at = (v * 2 + c) * P
                        last = nc.tensor.transpose(k.ps[:, 6, at:at + P], O[:, q, v, c, :], k.ident[:])
                last.then_inc(turned, 1)

            def output(e, m, h, q, bank_free):
                pe.wait_ge(*bank_free)
                pe.wait_ge(gT_ready, B * h + q + 1)
                if q == 0:
                    pe.wait_ge(wo_loaded[e], 16 * (m + 1))
                for c in range(2):
                    for v in range(PV):
                        last = nc.tensor.matmul(k.ps[:, 7, c * C:(c + 1) * C], gT[q % 2][:, v, c * P:(c + 1) * P], wo[e][:, v, :], start=v == 0, stop=v == PV - 1)
                last.then_inc(y_ready, 1)

            def turn_outputs(h, q, bank_free=None):
                turn(h, q, bank_free or (gT_ready, B * h + q))

            def project_outputs(m, e, h, q, bank_free=None):
                output(e, m, h, q, bank_free or (added, B * h + q))

            def body(m, e, prev, nxt):
                h = 2 * m + e
                m1, e1, h1 = after(m, e)
                before = (m if e else m - 1, 1 - e, h - 1)
                grams(m, e, h, 0)
                grams(m, e, h, 1)
                turn_v(h, 0)
                turn_v(h, 1)
                if nxt:
                    project_q(m1, e1, h1)
                turn_v(h, 2)
                turn_v(h, 3)
                grams(m, e, h, 2)
                grams(m, e, h, 3)
                pe.wait_ge(bp_ready, B * (h + 1))
                pe.wait_ge(zm_loaded[e], 16 * (2 * GB - 1) * (m + 1))
                pe.sem_inc(passed, 1)
                chunk = lambda b, c, v: (bp0[:, b, v, 0, 0:P], bp1[:, b, v, 0, :])[c]
                every = [(b, c, v) for b in range(B) for c in range(2) for v in range(PV)]
                for g in (0, 2):
                    for b, c, v in every:
                        at, to = slice(g * BLK, (g + 1) * BLK), slice((g + 1) * BLK, (g + 2) * BLK)
                        u = unit(b, c, v)
                        m_at = slice(0, BLK)
                        last = nc.tensor.matmul(k.ps[to, 2, u * BLK:(u + 1) * BLK], chunk(b, c, v)[at, to], M[e][at, u, m_at], start=True, stop=True)
                last.then_inc(t1_ready, 1)
                pe.wait_ge(t1_out, 2 * (h + 1))
                pe.sem_inc(passed, 1)
                for g in (0, 2):
                    for b, c, v in every:
                        at, to = slice(g * BLK, (g + 1) * BLK), slice((g + 1) * BLK, (g + 2) * BLK)
                        u = unit(b, c, v)
                        last = nc.tensor.matmul(k.ps[at, 3, u * BLK:(u + 1) * BLK], t1[to, u, :], Z[e][to, u, to], start=True, stop=True)
                for b, c, v in every:
                    u = unit(b, c, v)
                    to = slice(BLK, 2 * BLK)
                    last = nc.tensor.matmul(k.ps[to, 3, u * BLK:(u + 1) * BLK], Z[e][to, u, to], t1[to, u, :], start=True, stop=True)
                last.then_inc(l1_ready, 1)
                pe.wait_ge(l1_out, 3 * (h + 1))
                pe.sem_inc(passed, 1)
                HALF = 2 * BLK
                for a in range(2):
                    for b, c, v in every:
                        u = unit(b, c, v)
                        if u // TILES == a:
                            last = nc.tensor.matmul(k.ps[HALF:P, 4 + a, (u % TILES) * HALF:(u % TILES + 1) * HALF], chunk(b, c, v)[0:HALF, HALF:P], M[e][0:HALF, u, :],
                                                    start=True, stop=True)
                    last.then_inc(t2_ready, 1)
                pe.wait_ge(r_ready, B * (h + 1))
                for a in range(2):
                    pe.wait_ge(t2_out, 2 * h + a + 1)
                    pe.sem_inc(passed, 1)
                    for i in range(TILES):
                        u = a * TILES + i
                        last = nc.tensor.matmul(k.ps[0:HALF, 6 + a, i * HALF:(i + 1) * HALF], t2[HALF:P, u, :], Z[e][HALF:P, u, HALF:P], start=True, stop=True)
                    last.then_inc(l2_ready, 1)
                pe.wait_ge(l2_out, 2 * (h + 1))
                for a in range(2):
                    for b in (2 * a, 2 * a + 1):
                        for v in range(PV):
                            at = ((b % 2) * PV + v) * P
                            last = nc.tensor.matmul(k.ps[:, 2 + a, at:at + P], Z[e][:, unit(b, 0, v), :], R[:, b, 0, v, :], start=True, stop=True)
                    last.then_inc(u0_ready, 1)
                if prev:
                    turn_outputs(h - 1, 0, (l2_out, 2 * (h + 1)))
                if nxt:
                    project_v(0, e1, h1, (0,))
                for a in range(2):
                    pe.wait_ge(u0_out, 2 * h + a + 1)
                    for b in (2 * a, 2 * a + 1):
                        for v in range(PV):
                            at = ((b % 2) * PV + v) * P
                            last = nc.tensor.matmul(k.ps[:, 4 + a, at:at + P], bp0[:, b, v, 0, P:T], U[:, b, 0, v, :], start=True, stop=True)
                    last.then_inc(x1_ready, 1)
                if nxt:
                    project_v(0, e1, h1, (1,))
                if prev:
                    turn_outputs(h - 1, 1)
                    project_outputs(*before, 0, (l2_out, 2 * (h + 1)))
                for a in range(2):
                    pe.wait_ge(x1_done, 2 * h + a + 1)
                    for b in (2 * a, 2 * a + 1):
                        for v in range(PV):
                            at = ((b % 2) * PV + v) * P
                            last = nc.tensor.matmul(k.ps[:, 2 + a, at:at + P], Z[e][:, unit(b, 1, v), :], R[:, b, 1, v, :], start=True, stop=True)
                    last.then_inc(u1_ready, 1)
                if nxt:
                    project_v(1, e1, h1)
                if prev:
                    turn_outputs(h - 1, 2)
                    project_outputs(*before, 1)
                for b in range(B):
                    pe.wait_ge(u1_out, 2 * h + (1 if b == 0 else 2))
                    for v in range(PV):
                        at = v * 2 * P
                        nc.tensor.matmul(k.ps[:, 2 + b, at:at + P], bp0[:, b, v, 1, 0:P], U[:, b, 0, v, :], start=True, stop=True)
                        nc.tensor.matmul(k.ps[:, 2 + b, at + P:at + 2 * P], bp0[:, b, v, 1, P:T], U[:, b, 0, v, :], start=True, stop=False)
                        last = nc.tensor.matmul(k.ps[:, 2 + b, at + P:at + 2 * P], bp1[:, b, v, 1, :], U[:, b, 1, v, :], start=False, stop=True)
                    last.then_inc(o_ready, 1)
                if prev:
                    turn_outputs(h - 1, 3)
                if nxt:
                    project_z(0, e1, h1)
                if prev:
                    project_outputs(*before, 2)
                if nxt:
                    project_z(1, e1, h1)
                if prev:
                    project_outputs(*before, 3)
                if nxt:
                    if prev:
                        pe.wait_ge(gT_ready, B * h)
                    norms_q(e1, h1)

            project_q(0, 0, 0, True)
            project_v(0, 0, 0)
            project_v(1, 0, 0)
            project_z(0, 0, 0)
            project_z(1, 0, 0)
            norms_q(0, 0)
            every_head(pe, body)
            for q in range(B + 1):
                if q < B:
                    turn_outputs(NK - 1, q, None if q else (l2_out, 2 * NK))
                if q:
                    project_outputs(LAST, 1, NK - 1, q - 1, None if q > 1 else (l2_out, 2 * NK))

        @block.scalar
        def _(act):
            def decay(h, b):
                act.wait_ge(arg_ready, B * h + b + 1)
                nc.scalar.activation(E[b][:, :, EC:EC + T], E[b][:, :, EC:EC + T], ACT.Exp)
                nc.scalar.activation(E[b][:, :, E1:E1 + P], E[b][:, :, E1:E1 + P], ACT.Exp).then_inc(e_ready, 1)

            def last_tap_q(m, e, h):
                if not is_first(h):
                    act.wait_ge(g_ready, B * h)
                    act.wait_ge(q_square, h)
                act.wait_ge(wf_loaded[e], 16 * (m + 1))
                for g in range(G):
                    act.wait_ge(q_proj, G * h + g + 1)
                    nc.scalar.activation(qT[:, g * BANK:(g + 1) * BANK], k.ps[:, g, :], ACT.Copy,
                                         scale=taps_of(e, 0)[:, TAPS - 1:TAPS]).then_inc(q_last, 1)

            def last_tap_v(v, e, h):
                if v == 0 and not is_first(h):
                    act.wait_ge(v_turned, B * h)
                for g in range(G):
                    act.wait_ge(v_proj, 4 * h + 2 * v + g + 1)
                    nc.scalar.activation(vT[:, v, g * BANK:(g + 1) * BANK], k.ps[:, g, :], ACT.Copy,
                                         scale=taps_of(e, 1 + v)[:, TAPS - 1:TAPS]).then_inc(v_last, 1)

            def tanh_z(v, h, halves=range(2)):
                for g in halves:
                    z = 4 * h + 2 * v + g
                    act.wait_ge(z_proj, z + 1)
                    if not is_first(z, 2):
                        act.wait_ge(sz_ready, z - 1)
                    nc.scalar.activation(th[g][:], k.ps[:, g, :], ACT.Tanh, scale=0.5).then_inc(th_ready, 1)

            def square_q(e, h):
                act.wait_ge(q_conv, G * (h + 1))
                if not is_first(h):
                    act.wait_ge(qn_ready, h)
                nc.scalar.activation(square[:], qT[:], ACT.Square).then_inc(q_square, 1)

            def minus(out, src, done):
                nc.scalar.activation(out, src, ACT.Copy, scale=-1.0).then_inc(done, 1)

            def square_o(h):
                act.wait_ge(o_out, B * (h + 1))
                if not is_first(h):
                    act.wait_ge(scaled, B * h)
                nc.scalar.activation(osq.rearrange("p u d -> p (u d)"), k.xn[:].rearrange("p i c -> p (i c)"), ACT.Square).then_inc(o_square, 1)

            def body(m, e, prev, nxt):
                h = 2 * m + e
                m1, e1, h1 = after(m, e)
                if nxt:
                    last_tap_q(m1, e1, h1)
                if nxt and e == 0 and m is not LAST:
                    inverse.scalar_exp(act, m)
                act.wait_ge(t1_ready, h + 1)
                for g in (1, 3):
                    rows = slice(g * BLK, (g + 1) * BLK)
                    nc.scalar.copy(t1[rows].rearrange("p u k -> p (u k)"), k.ps[rows, 2, :]).then_inc(t1_out, 1)
                act.wait_ge(l1_ready, h + 1)
                lvl1 = lambda g: k.ps[g * BLK:(g + 1) * BLK, 3, :].rearrange("p (u k) -> p u k", k=BLK)
                minus(Z[e][0:BLK, :, BLK:2 * BLK], lvl1(0), l1_out)
                minus(Z[e][2 * BLK:3 * BLK, :, 3 * BLK:P], lvl1(2), l1_out)
                minus(M[e][BLK:2 * BLK, :, 0:BLK], lvl1(1), l1_out)
                act.wait_ge(qn_ready, h + 1)
                for a in range(2):
                    act.wait_ge(t2_ready, 2 * h + a + 1)
                    nc.scalar.copy(t2[2 * BLK:P, a * TILES:(a + 1) * TILES, :], k.ps[2 * BLK:P, 4 + a, :].rearrange("p (u k) -> p u k", k=2 * BLK)).then_inc(t2_out, 1)
                for a in range(2):
                    act.wait_ge(l2_ready, 2 * h + a + 1)
                    minus(Z[e][0:2 * BLK, a * TILES:(a + 1) * TILES, 2 * BLK:P], k.ps[0:2 * BLK, 6 + a, :].rearrange("p (u k) -> p u k", k=2 * BLK), l2_out)
                if prev:
                    act.wait_ge(scaled, B * h)
                for c, ready, out in ((0, u0_ready, u0_out), (1, u1_ready, u1_out)):
                    for a in range(2):
                        act.wait_ge(ready, 2 * h + a + 1)
                        nc.scalar.copy(U[:, 2 * a:2 * a + 2, c], k.ps[:, 2 + a, :].rearrange("p (b v d) -> p b v d", b=2, v=PV)).then_inc(out, 1)
                    if nxt:
                        last_tap_v(c, e1, h1)
                if nxt:
                    decay(h1, 0)
                    decay(h1, 1)
                for b in range(B):
                    act.wait_ge(o_ready, B * h + b + 1)
                    if prev:
                        act.wait_ge(turned, B * (h - 1) + b + 1)
                    nc.scalar.copy(O[:, b].rearrange("p v c d -> p (v c d)"), k.ps[:, 2 + b, :]).then_inc(o_out, 1)
                if nxt:
                    tanh_z(0, h1)
                square_o(h)
                if nxt:
                    square_q(e1, h1)
                    tanh_z(1, h1)
                    decay(h1, 2)
                    decay(h1, 3)

            act.wait_ge(pads, B)
            last_tap_q(0, 0, 0)
            last_tap_v(0, 0, 0)
            last_tap_v(1, 0, 0)
            tanh_z(0, 0)
            tanh_z(1, 0)
            square_q(0, 0)
            for b in range(B):
                decay(0, b)
            every_head(act, body)

        @block.vector
        def _(dve):
            def exponent(m, e, h, b):
                if b == 0:
                    dve.wait_ge(in_loaded[e], 32 * (m + 1))
                if not is_first(h):
                    dve.wait_ge(bp_ready, B * (h - 1) + b + 1)
                for v in range(PV):
                    nc.vector.scalar_tensor_tensor(out=E[b][:, v, EC:EC + T], in0=cbc[e][:, v, b, :], scalar=col(k.ccol, 2 * b, PV * h + v),
                                                   in1=k.bound[:], op0=ALU.subtract, op1=ALU.min)
                    last = nc.vector.scalar_tensor_tensor(out=E[b][:, v, E1:E1 + P], in0=cbc[e][:, v, b, P:T], scalar=col(k.ccol, 2 * b + 1, PV * h + v),
                                                          in1=k.bound[:, 0:P], op0=ALU.subtract, op1=ALU.min)
                last.then_inc(arg_ready, 1)

            def weigh(e, h, b):
                dve.wait_ge(e_ready, B * h + b + 1)
                dve.wait_ge(g_ready, B * h + b + 1)
                if not is_first(h):
                    dve.wait_ge(o_ready, B * (h - 1) + b + 1)
                bank = 2 + 2 * (b % 2)
                for v in range(PV):
                    for c, out, at, n in ((0, bp0, EC, T), (1, bp1, E1, P)):
                        decays_of = E[b][:, v, at - 1:at + n]
                        two_steps = bass.AP(tensor=decays_of.tensor, offset=decays_of.offset, ap=[list(decays_of.ap[0]), [1, 2], [1, n]])
                        last = nc.vector.scalar_tensor_tensor(out=out[:, b, v], in0=k.ps[:, bank + c, 0:2 * n].rearrange("p (n t) -> p n t", n=2),
                                                              scalar=col(k.w, 2 * b + c, PV * h + v), in1=two_steps, op0=ALU.mult, op1=ALU.mult)
                last.then_inc(bp_ready, 1)

            def scale_v(h, b):
                dve.wait_ge(v_turned, B * h + b + 1)
                if not is_first(h):
                    dve.wait_ge(u1_ready, 2 * h)
                per_token = pick(k.kabs, h)[:, 2 * b:2 * b + 2].unsqueeze(2).broadcast_to([P, 2, PV * P])
                nc.vector.tensor_tensor(R[:, b].rearrange("p c v d -> p c (v d)"), k.ps[:, 6 + b % 2, :].rearrange("p (c f) -> p c f", c=2), per_token,
                                        ALU.mult).then_inc(r_ready, 1)

            def convolve(part, e, h, last_tap, tap, conv, of_head):
                out = qT[:] if part == 0 else vT[:, part - 1, :]
                for g in range(G):
                    u = of_head * h + max(part - 1, 0) * G + g
                    dve.wait_ge(last_tap, u + 1)

                    def done(n, ins):
                        if n < TAPS - 2:
                            ins.then_inc(tap, 1)
                            dve.wait_ge(tap, (TAPS - 2) * u + n + 1)
                        else:
                            ins.then_inc(conv, 1)
                    conv_taps(nc, dve, k.ps[:, g, :], out[:, g * BANK:(g + 1) * BANK], taps_of(e, part), done)

            def convolve_q(e, h):
                convolve(0, e, h, q_last, q_tap, q_conv, G)

            def convolve_v(v, e, h):
                convolve(1 + v, e, h, v_last, v_tap, v_conv, PV * G)

            def gate(v, e, h, halves=range(2)):
                if v == 0 and not is_first(h, 2):
                    dve.wait_ge(gT_ready, B * (h - 1))
                for g in halves:
                    dve.wait_ge(th_ready, 4 * h + 2 * v + g + 1)
                    nc.vector.scalar_tensor_tensor(out=sz[e][:, v, g * BANK:(g + 1) * BANK], in0=th[g][:], scalar=1.0, in1=k.ps[:, g, :],
                                                   op0=ALU.add, op1=ALU.mult).then_inc(sz_ready, 1)

            def keep_q(e, h):
                dve.wait_ge(qn_ready, h + 1)
                nc.vector.tensor_scalar(ssq[e][:], k.ps[:, 6, 0:TILES], NORM_EPS2, None, ALU.max).then_inc(q_kept, 1)

            def normalise(e, h):
                CH = 2
                dve.wait_ge(o_square, h + 1)
                dve.wait_ge(q_kept, h + 1)
                nc.vector.tensor_reduce(ms[:], osq, AX.X, ALU.add).then_inc(chain, 1)
                nc.vector.tensor_scalar(floor[:], ssq[e][:], RMS_EPS, None, ALU.mult).then_inc(chain, 1)
                dve.wait_ge(chain, 4 * h + CH)
                nc.vector.scalar_tensor_tensor(out=ms[:].rearrange("p (b v c) -> p b v c", v=PV, c=2)[:, :, 0], in0=ms[:].rearrange("p (b v c) -> p b v c", v=PV, c=2)[:, :, 0],
                                               scalar=1.0 / DV, in1=floor[:].rearrange("p (b c) -> p b c", c=2), op0=ALU.mult, op1=ALU.add).then_inc(chain, 1)
                nc.vector.scalar_tensor_tensor(out=ms[:].rearrange("p (b v c) -> p b v c", v=PV, c=2)[:, :, 1], in0=ms[:].rearrange("p (b v c) -> p b v c", v=PV, c=2)[:, :, 1],
                                               scalar=1.0 / DV, in1=floor[:].rearrange("p (b c) -> p b c", c=2), op0=ALU.mult, op1=ALU.add).then_inc(chain, 1)
                dve.wait_ge(chain, 4 * h + CH + 2)
                fast_rsqrt(nc, dve, ms[:], inv[:], tmp[:], root, h)
                for q in range(B):
                    nc.vector.tensor_tensor(O[:, q].rearrange("p v c d -> p (v c) d"), O[:, q].rearrange("p v c d -> p (v c) d"),
                                            inv[:, 4 * q:4 * q + 4].unsqueeze(2).broadcast_to([P, 4, P]), ALU.mult).then_inc(scaled, 1)

            def gate_outputs(e, h, q):
                dve.wait_ge(turned, B * h + q + 1)
                if not (is_first(h) and q < 2):
                    dve.wait_ge(y_ready, B * h + q - 1)
                nc.vector.scalar_tensor_tensor(out=gT[q % 2][:], in0=k.ps[:, 6, :].rearrange("p (v t) -> p v t", v=PV), scalar=nwh[:, 0:1],
                                               in1=sz[e][:, :, q * T:(q + 1) * T], op0=ALU.mult, op1=ALU.mult).then_inc(gT_ready, 1)

            def add_outputs(h, q):
                dve.wait_ge(y_ready, B * h + q + 1)
                if not is_first(h):
                    dve.wait_ge(added, B * (h - 1) + q + 1)
                nc.vector.tensor_tensor(k.x[:, 2 * q:2 * q + 2, :], k.ps[:, 7, :].rearrange("p (i c) -> p i c", i=2), k.x[:, 2 * q:2 * q + 2, :],
                                        ALU.add).then_inc(added, 1)

            def body(m, e, prev, nxt):
                h = 2 * m + e
                m1, e1, h1 = after(m, e)
                weigh(e, h, 0)
                scale_v(h, 0)
                scale_v(h, 1)
                weigh(e, h, 1)
                scale_v(h, 2)
                scale_v(h, 3)
                if nxt and e == 0 and m is not LAST:
                    inverse.vector_weights(dve, m)
                    inverse.vector_floor(dve, m)
                weigh(e, h, 2)
                weigh(e, h, 3)
                if prev:
                    normalise(1 - e, h - 1)
                if nxt:
                    convolve_q(e1, h1)
                    for b in range(B):
                        exponent(m1, e1, h1, b)
                if prev:
                    gate_outputs(1 - e, h - 1, 0)
                for a in range(2):
                    dve.wait_ge(x1_ready, 2 * h + a + 1)
                    nc.vector.tensor_tensor(R[:, 2 * a:2 * a + 2, 1], R[:, 2 * a:2 * a + 2, 1], k.ps[:, 4 + a, :].rearrange("p (b v d) -> p b v d", b=2, v=PV),
                                            ALU.subtract).then_inc(x1_done, 1)
                if prev:
                    gate_outputs(1 - e, h - 1, 1)
                if nxt and e == 1:
                    inverse.vector_transpose(dve, m)
                for v in range(PV):
                    if nxt:
                        convolve_v(v, e1, h1)
                    if prev:
                        add_outputs(h - 1, v)
                        gate_outputs(1 - e, h - 1, 2 + v)
                if nxt:
                    gate(0, e1, h1)
                if prev:
                    add_outputs(h - 1, 2)
                if nxt:
                    gate(1, e1, h1)
                if prev:
                    add_outputs(h - 1, 3)
                if nxt:
                    keep_q(e1, h1)

            dve.wait_ge(k.nw_loaded, 16)
            nc.vector.tensor_scalar(nwh[:], k.nw[:], 0.5, None, ALU.mult).then_inc(nwh_ready, 1)
            dve.wait_ge(nwh_ready, 1)
            dve.wait_ge(pads, B)
            convolve_q(0, 0)
            for v in range(PV):
                convolve_v(v, 0, 0)
            gate(0, 0, 0)
            gate(1, 0, 0)
            keep_q(0, 0)
            for b in range(B):
                exponent(0, 0, 0, b)
            every_head(dve, body)
            normalise(1, NK - 1)
            for q in range(B + 1):
                if q < B:
                    gate_outputs(1, NK - 1, q)
                if q:
                    add_outputs(NK - 1, q - 1)




def constants(nc, k, pool):
    nc.gpsimd.memset(k.neghalf[:], -0.5).then_inc(k.const_ready, 1)
    nc.gpsimd.memset(k.ident[:], 0.0).then_inc(k.ident_ready, 1)
    pool.wait_ge(k.ident_ready, 1)
    nc.gpsimd.affine_select(out=k.ident[:], in_=k.ident[:], compare_op=ALU.not_equal, fill=1.0, base=0, pattern=[[-1, P]],
                            channel_multiplier=1).then_inc(k.ident_ready, 1)
    nc.gpsimd.memset(k.ones[:], 1.0).then_inc(k.const_ready, 1)
    nc.gpsimd.memset(k.bound[:], 0.0).then_inc(k.const_ready, 1)
    pool.wait_ge(k.const_ready, 3)
    nc.gpsimd.affine_select(out=k.upto[:], in_=k.ones[:], compare_op=ALU.is_ge, fill=0.0, base=0, pattern=[[1, P]], channel_multiplier=-1)
    nc.gpsimd.affine_select(out=k.bound[:], in_=k.bound[:], compare_op=ALU.is_ge, fill=NEG, base=0, pattern=[[1, C]], channel_multiplier=-1)


def build(nc, d, out):
    tokens = lambda a: a.rearrange("(i p) c -> p i c", p=P)
    with ExitStack() as whole:
        k = Names()
        sb = lambda n, s: whole.enter_context(nc.sbuf_tensor(n, s, F32))
        sem = lambda n: whole.enter_context(nc.semaphore(n))

        def semaphore(name):
            k.taken.append(nc.alloc_semaphore(name))
            return k.taken[-1]

        k.taken, k.semaphore = [], semaphore
        scratch = lambda n, s: nc.dram_tensor(n, s, F32, kind="Internal").ap()
        k.x, k.xn, k.xT, k.ident, k.neghalf = sb("x", [P, TILES, C]), sb("xn", [P, TILES, C]), sb("xT", [P, KT, TOK]), sb("ident", [P, P]), sb("neghalf", [P, TILES])
        k.ps = whole.enter_context(nc.psum_tensor("ps", [P, 8, BANK], F32))
        k.x_loaded, k.ident_ready, k.const_ready = sem("x_loaded"), sem("ident_ready"), sem("const_ready")

        def load(eng, dst, src, loaded):
            eng.dma_start(dst, src).then_inc(loaded, 16)

        with ExitStack() as layer:
            sb = lambda n, s: layer.enter_context(nc.sbuf_tensor(n, s, F32))
            k.ones, k.upto, k.bound = sb("ones", [P, P]), sb("upto", [P, P]), sb("bound", [P, C])
            k.wba, k.alog, k.dtb, k.nw = sb("wba", [P, KT, 2 * NV]), sb("alog", [P, NV]), sb("dtb", [P, NV]), sb("nw", [P, 1])
            k.ccol, k.beta, k.w = sb("ccol", [P, TILES, NV]), sb("beta", [P, TILES, NV]), sb("w", [P, TILES, NV])
            k.rk, k.kabs, k.root_tmp = sb("rk", [P, NK, TILES]), sb("kabs", [P, NK, TILES]), sb("root_tmp", [P, NK * TILES])
            k.wba_loaded, k.alog_loaded, k.dtb_loaded, k.nw_loaded = sem("wba_loaded"), sem("alog_loaded"), sem("dtb_loaded"), sem("nw_loaded")
            k.crow_d, k.brow_d = scratch("crow_d", (NV, TOK)), scratch("brow_d", (NV, TOK))
            k.kT_d, k.gram_d = scratch("kT_d", (NK, DK, TOK)), scratch("gram_d", (NK, BLK, TOK))
            k.inv_d, k.invT_d = scratch("inv_d", (P, BLK * BLK)), scratch("invT_d", (P, BLK * BLK))
            k.wk_d, k.wf_d, k.wo_d = d["wk"], d["wf"], d["wo"]

            with nc.Block() as block:
                @block.sync
                def _(sp):
                    load(sp, k.x[:], tokens(d["x"]), k.x_loaded)
                    load(sp, k.wba[:], d["wba"].rearrange("k p e -> p k e"), k.wba_loaded)
                    load(sp, k.alog[:], d["alog"].broadcast_to([P, NV]), k.alog_loaded)
                    load(sp, k.dtb[:], d["dtb"].broadcast_to([P, NV]), k.dtb_loaded)
                    load(sp, k.nw[:], d["nw"], k.nw_loaded)

                @block.gpsimd
                def _(pool):
                    constants(nc, k, pool)

            layernorm(nc, k, "ln0")
            decays(nc, k)
            keys(nc, k)
            heads(nc, k)
        nc.clear_and_free_semaphores(k.taken)
        nc.all_engine_barrier()

        sb = lambda n, s: whole.enter_context(nc.sbuf_tensor(n, s, F32))
        k.ctx, k.ctxT, k.diag = sb("ctx", [P, TILES, C]), sb("ctxT", [P, TILES, T]), sb("diag", [P, P])
        k.router, k.rscale, k.escale = sb("router", [P, KT, E0]), sb("rscale", [P, KT]), sb("escale", [P, E0])
        k.lower, k.mix = sb("lower", [P, E0 * E0]), sb("mix", [P, TILES, E0])
        k.wqkv, k.wo, k.rope, k.temp, k.wmask = sb("wqkv", [P, KT, 384]), sb("wo", [P, KT, C]), sb("rope", [P, 2, 3, 8]), sb("temp", [P, H1]), sb("wmask", [P, 160])
        (k.ctx_loaded, k.ctxT_loaded, k.diag_loaded, k.router_loaded, k.rscale_loaded, k.escale_loaded, k.lower_loaded, k.gate_loaded, k.linear_loaded,
         k.wqkv_loaded, k.wo_loaded, k.rope_loaded, k.temp_loaded, k.wmask_loaded, k.rw1_loaded, k.rb1_loaded, k.we1_loaded, k.be1_loaded) = (
            sem(n + "_loaded") for n in ("ctx", "ctxT", "diag", "router", "rscale", "escale", "lower", "gate", "linear",
                                         "wqkv", "wo1", "rope", "temp", "wmask", "rw1", "rb1", "we1", "be1"))
        k.shift_done, k.x_final, stored = sem("shift_done"), sem("x_final"), sem("stored")
        k.rw1, k.rb1 = sb("rw1", [P, KT, E1, C]), sb("rb1", [P, 2, E1])
        k.we1, k.be1 = sb("we1", [P, KT, E1, C]), sb("be1", [E1, C])

        with ExitStack() as layer:
            sb = lambda n, s: layer.enter_context(nc.sbuf_tensor(n, s, F32))
            k.gate, k.linear = sb("gate", [P, KT, E0, 2 * H0]), sb("linear", [P, KT, E0, C])

            with nc.Block() as block:
                @block.sync
                def _(sp):
                    load(sp, k.ctx[:], tokens(d["ctx"]), k.ctx_loaded)
                    load(sp, k.ctxT[:], tokens(d["ctxT"]), k.ctxT_loaded)
                    load(sp, k.router[:], d["router"].rearrange("k p e -> p k e"), k.router_loaded)
                    load(sp, k.rscale[:], d["rscale"], k.rscale_loaded)
                    load(sp, k.escale[:], d["escale"].broadcast_to([P, E0]), k.escale_loaded)
                    load(sp, k.lower[:], d["lower"].broadcast_to([P, E0 * E0]), k.lower_loaded)
                    load(sp, k.gate[:], d["gate"].rearrange("k p e h -> p k e h"), k.gate_loaded)
                    load(sp, k.linear[:], d["linear"].rearrange("k p e h -> p k e h"), k.linear_loaded)
                    load(sp, k.wqkv[:], d["wqkv"].rearrange("k p e -> p k e"), k.wqkv_loaded)
                    load(sp, k.rope[:], d["rope"].rearrange("h p a b -> p h a b"), k.rope_loaded)
                    load(sp, k.temp[:], d["temp"].broadcast_to([P, H1]), k.temp_loaded)
                    load(sp, k.wmask[:], d["wmask"], k.wmask_loaded)
                    load(sp, k.wo[:], d["wo1"].rearrange("k p e -> p k e"), k.wo_loaded)
                    load(sp, k.diag[:], d["diag"], k.diag_loaded)
                    load(sp, k.rw1[:], d["rw1"].rearrange("k p e o -> p k e o"), k.rw1_loaded)
                    load(sp, k.rb1[:], d["rb1"].rearrange("k p e -> p k e"), k.rb1_loaded)
                    load(sp, k.we1[:], d["we1"].rearrange("k p e o -> p k e o"), k.we1_loaded)
                    load(sp, k.be1[:], d["be1"], k.be1_loaded)

            layernorm(nc, k, "ln1", False)
            cross_attention_0(nc, k)
            layernorm(nc, k, "ln2")
            moe_router_0(nc, k)
            moe_experts_0(nc, k)

        with ExitStack() as layer:
            sb = lambda n, s: layer.enter_context(nc.sbuf_tensor(n, s, F32))
            k.qT, k.kT, k.v, k.vprev = sb("qT", [P, GROUP, TOK]), sb("kT", [P, TOK]), sb("v", [P, TILES, 64]), sb("vprev", [WINDOW, B, 64])
            layernorm(nc, k, "ln3")
            windowed_qkv(nc, k)
            windowed_attention(nc, k)

        layernorm(nc, k, "ln4", False)
        cross_attention_1(nc, k)

        sb = lambda n, s: whole.enter_context(nc.sbuf_tensor(n, s, F32))
        k.share, k.shareT = sb("share", [P, TILES, E1]), sb("shareT", [E1, TOK])
        layernorm(nc, k, "ln5")
        soft_router_1(nc, k)
        soft_experts_1(nc, k)

        with nc.Block() as block:
            @block.sync
            def _(sp):
                sp.dma_start(tokens(out), k.x[:]).then_inc(stored, 16)
                sp.wait_ge(stored, 16)


def kernel(**inputs):
    import concourse.bacc as bacc
    from concourse.bass_utils import run_bass_kernel_spmd

    a = {n: np.asarray(v) for n, v in inputs.items()}
    QW, KW = NK * DK, 2 * NK * DK
    taps = a["L0_attn_conv_w"]
    wT = a["L0_attn_W_qkv"].T.reshape(KT, P, -1)
    by_head = lambda w, n: w.reshape(KT, P, NK, n, P)
    wk = np.concatenate([wT[:, :, QW:KW].reshape(KT, P, NK, DK).transpose(2, 1, 0, 3).reshape(NK, P, KT * DK), taps[QW:KW].reshape(NK, DK, TAPS)], 2)
    front = np.concatenate([by_head(wT[:, :, :QW], 1), by_head(wT[:, :, KW:], PV), by_head(a["L0_attn_W_z"].T, PV)], 3)
    front_taps = np.concatenate([taps[:QW].reshape(NK, 1, P, TAPS), taps[KW:].reshape(NK, PV, P, TAPS)], 1).transpose(0, 2, 1, 3)
    q_of_group = a["L1_attn_Wq"].reshape(H1 // GROUP, GROUP, 16, C).transpose(1, 0, 2, 3).reshape(C, C)
    angle = np.arange(T, dtype=np.float32)[:, None] * (1.0 / 10000.0 ** (np.arange(0, 16, 2, dtype=np.float32) / 16)).astype(np.float32)
    q_at, k_at = np.arange(P)[:, None], np.arange(P + WINDOW)[None]
    arrays = {
        "x": a["x"].reshape(TOK, C),
        "wk": wk,
        "wf": np.concatenate([front.transpose(2, 1, 0, 3, 4).reshape(NK, P, -1), front_taps.reshape(NK, P, -1)], 2),
        "wo": a["L0_attn_W_out"].T.reshape(NK, PV, P, C).transpose(0, 2, 1, 3).reshape(NK, P, PV * C),
        "wba": np.concatenate([a["L0_attn_W_b"], a["L0_attn_W_a"]], 0).T.reshape(KT, P, 2 * NV),
        "alog": a["L0_attn_A_log"].reshape(1, NV),
        "dtb": a["L0_attn_dt_bias"].reshape(1, NV),
        "nw": a["L0_attn_norm_w"].reshape(DV, 1),
        "ctx": a["ctx_2048"].reshape(TOK, C),
        "ctxT": a["ctx_2048"].transpose(0, 2, 1).reshape(B * C, T),
        "router": a["L0_ffn_router_logits"].reshape(KT, P, E0),
        "rscale": a["L0_ffn_router_scale"].reshape(KT, P).T,
        "escale": a["L0_ffn_per_expert_scale"].reshape(1, E0),
        "lower": np.tril(np.ones((E0, E0), np.float32), -1).reshape(1, E0 * E0),
        "gate": a["L0_ffn_gating_einsum"].transpose(3, 0, 1, 2).reshape(KT, P, E0, 2 * H0),
        "linear": a["L0_ffn_linear"].transpose(1, 0, 2).reshape(KT, P, E0, C),
        "wqkv": np.concatenate([q_of_group, a["L1_attn_Wkv"]], 0).T.reshape(KT, P, -1),
        "wo1": a["L1_attn_Wo"].T.reshape(KT, P, C),
        "rope": np.stack([np.cos(angle), -np.sin(angle), np.sin(angle)], 1).astype(np.float32).reshape(KT, P, 3, 8),
        "temp": a["L1_attn_qk_temp"].reshape(H1 // GROUP, GROUP).T.reshape(1, H1),
        "wmask": np.where((k_at > q_at) & (k_at <= q_at + WINDOW), 0, NEG).astype(np.float32),
        "diag": np.kron(np.eye(4), np.ones((32, 32))).astype(np.float32),
        "rw1": a["L1_ffn_router_w"].reshape(C, E1, C).transpose(2, 1, 0).reshape(KT, P, E1, C),
        "rb1": a["L1_ffn_router_b"].reshape(KT, P, E1),
        "we1": a["L1_ffn_expert_w"].transpose(2, 0, 1).reshape(KT, P, E1, C),
        "be1": a["L1_ffn_expert_b"],
    }
    nc = bacc.Bacc("TRN2", target_bir_lowering=False, num_devices=1)
    arrays = {f"in_{n}": np.ascontiguousarray(v) for n, v in arrays.items()}
    d = {n[3:]: nc.dram_tensor(n, v.shape, F32, kind="ExternalInput").ap() for n, v in arrays.items()}
    build(nc, d, nc.dram_tensor("out", (TOK, C), F32, kind="ExternalOutput").ap())
    result = run_bass_kernel_spmd(nc, [arrays], core_ids=[0])
    return result.results[0]["out"].reshape(B, T, C)
```

```python
from contextlib import ExitStack

import concourse.bass as bass
import numpy as np
from concourse import mybir

F32 = mybir.dt.float32
ALU = mybir.AluOpType
ACT = mybir.ActivationFunctionType
AX = mybir.AxisListType
P = 128
BANK = 512
B, T, C = 4, 256, 256
TILES = B * T // P
KT = C // P
TOK = B * T
LN_EPS = 1e-5


class Names:
    pass


class Steps:

    def __init__(self, sem):
        self.sem, self.n = sem, 0

    def one(self):
        self.n += 1
        return 1


def layernorm(nc, k, name, transposed=True, loads=None):
    with ExitStack() as ctx:
        sem = lambda n: k.semaphore(f"{name}_{n}")
        stats = ctx.enter_context(nc.sbuf_tensor(f"{name}_stats", [P, TILES, 6], F32))
        mv = ctx.enter_context(nc.sbuf_tensor(f"{name}_mv", [P, TILES, 2], F32))
        rstd = ctx.enter_context(nc.sbuf_tensor(f"{name}_rstd", [P, TILES], F32))
        vare = ctx.enter_context(nc.sbuf_tensor(f"{name}_vare", [P, TILES], F32))
        vare_done = sem("vare_done")
        stats_done, mv_done, rstd_done = sem("stats_done"), sem("mv_done"), sem("rstd_done")
        xn_done, turned, xT_done = sem("xn_done"), sem("turned"), sem("xT_done")
        block = ctx.enter_context(nc.Block())

        @block.vector
        def _(dve):
            if k.x_loaded is not None:
                dve.wait_ge(k.x_loaded, 16)
            for i in range(TILES):
                nc.vector.bn_stats(stats[:, i, :], k.x[:, i, :]).then_inc(stats_done, 1)
            for i in range(TILES):
                dve.wait_ge(stats_done, i + 1)
                nc.vector.bn_aggr(mv[:, i, :], stats[:, i, :]).then_inc(mv_done, 1)
            dve.wait_ge(rstd_done, 1)
            for i in range(TILES):
                nc.vector.tensor_scalar(k.xn[:, i, :], k.x[:, i, :], mv[:, i, 0:1], rstd[:, i:i + 1],
                                        ALU.subtract, ALU.mult).then_inc(xn_done, 1)

        @block.gpsimd
        def _(pool):
            pool.wait_ge(mv_done, TILES)
            nc.gpsimd.tensor_scalar(vare[:], mv[:, :, 1], LN_EPS, None, ALU.add).then_inc(vare_done, 1)
            pool.wait_ge(vare_done, 1)
            nc.gpsimd.tensor_tensor(rstd[:], vare[:], k.neghalf[:, 0:TILES], ALU.pow).then_inc(rstd_done, 1)

        if loads is not None:
            @block.sync
            def _(sp):
                loads(sp)

        if not transposed:
            return

        @block.tensor
        def _(pe):
            if k.ident_ready is not None:
                pe.wait_ge(k.ident_ready, 2)
            for i in range(TILES):
                pe.wait_ge(xn_done, i + 1)
                for c in range(KT):
                    last = nc.tensor.transpose(k.ps[:, c * 2 + i // 4, (i % 4) * P:(i % 4 + 1) * P],
                                               k.xn[:, i, c * P:(c + 1) * P], k.ident[:])
                if i % 4 == 3:
                    last.then_inc(turned, 1)

        @block.scalar
        def _(act):
            for g in range(TILES // 4):
                act.wait_ge(turned, g + 1)
                for c in range(KT):
                    nc.scalar.copy(k.xT[:, c, g * BANK:(g + 1) * BANK], k.ps[:, c * 2 + g, :]).then_inc(xT_done, 1)


def cross_attention_0(nc, k):
    with ExitStack() as ctx:
        sem = lambda n: k.semaphore(f"xa0_{n}")
        sb = lambda n, s: ctx.enter_context(nc.sbuf_tensor(f"xa0_{n}", s, F32))
        SCALE = float(C) ** -0.5
        probs, top, ntop = sb("probs", [P, B, KT, C]), sb("top", [P, B, KT]), sb("ntop", [P, B, KT])
        total, rtotal = sb("total", [P, B, KT]), sb("rtotal", [P, B, KT])
        scores_ready, top_ready, ntop_ready, exp_ready = sem("scores"), sem("top"), sem("ntop"), sem("exp")
        rtotal_ready, probs_ready, mixed = sem("rtotal"), sem("probs_s"), sem("mixed")
        block = ctx.enter_context(nc.Block())

        @block.tensor
        def _(pe):
            pe.wait_ge(k.ctx_loaded, 16)
            for b in range(B):
                for e in range(KT):
                    for s in range(KT):
                        last = nc.tensor.matmul(k.ps[:, b, e * C:(e + 1) * C], k.ctx[:, 2 * b + s, e * P:(e + 1) * P],
                                                k.xn[:, 2 * b + s, :], start=s == 0, stop=s == KT - 1)
                last.then_inc(scores_ready, 1)
            pe.wait_ge(k.ctxT_loaded, 16)
            for b in range(B):
                pe.wait_ge(probs_ready, KT * (b + 1))
                for t in range(KT):
                    for e in range(KT):
                        last = nc.tensor.matmul(k.ps[:, B + b, t * C:(t + 1) * C], k.ctxT[:, 2 * b + e, t * P:(t + 1) * P],
                                                probs[:, b, e, :], start=e == 0, stop=e == KT - 1)
                last.then_inc(mixed, 1)

        @block.vector
        def _(dve):
            for b in range(B):
                dve.wait_ge(scores_ready, b + 1)
                nc.vector.tensor_reduce(top[:, b, :], k.ps[:, b, :].rearrange("p (e d) -> p e d", e=KT),
                                        AX.X, ALU.max).then_inc(top_ready, 1)
                dve.wait_ge(top_ready, b + 1)
                nc.vector.tensor_scalar(ntop[:, b, :], top[:, b, :], -SCALE, None, ALU.mult).then_inc(ntop_ready, 1)
            for b in range(B):
                dve.wait_ge(exp_ready, KT * (b + 1))
                nc.vector.reciprocal(rtotal[:, b, :], total[:, b, :]).then_inc(rtotal_ready, 1)
                dve.wait_ge(rtotal_ready, b + 1)
                for e in range(KT):
                    nc.vector.tensor_scalar(probs[:, b, e, :], probs[:, b, e, :], rtotal[:, b, e:e + 1], None,
                                            ALU.mult).then_inc(probs_ready, 1)
            for b in range(B):
                dve.wait_ge(mixed, b + 1)
                nc.vector.tensor_tensor(k.x[:, 2 * b:2 * b + 2, :], k.ps[:, B + b, :].rearrange("p (t d) -> p t d", t=KT),
                                        k.x[:, 2 * b:2 * b + 2, :], ALU.add)

        @block.scalar
        def _(act):
            for b in range(B):
                act.wait_ge(ntop_ready, b + 1)
                for e in range(KT):
                    nc.scalar.activation(probs[:, b, e, :], k.ps[:, b, e * C:(e + 1) * C], ACT.Exp, bias=ntop[:, b, e:e + 1],
                                         scale=SCALE, accum_out=total[:, b, e:e + 1]).then_inc(exp_ready, 1)


E0, H0 = 8, 256


def moe_router_0(nc, k):
    with ExitStack() as ctx:
        sem = lambda n: k.semaphore(f"mr_{n}")
        sb = lambda n, s: ctx.enter_context(nc.sbuf_tensor(f"mr_{n}", s, F32))
        router = sb("router", [P, KT, E0])
        square, mean2, inv = sb("square", [P, C]), sb("mean2", [P, TILES]), sb("inv", [P, TILES])
        logits, prob = sb("logits", [P, TILES, E0]), sb("prob", [P, TILES, E0])
        top, total, before = sb("top", [P, TILES]), sb("total", [P, TILES]), sb("before", [P, TILES, E0])
        above, tied = sb("above", [P, TILES, E0, E0]), sb("tied", [P, TILES, E0, E0])
        router_ready, square_done, inv_ready, logits_done = sem("router"), sem("square"), sem("inv"), sem("logits")
        step, shifted, exp_ready = Steps(sem("vector_step")), sem("shifted"), sem("exp")
        pool_step = sem("pool_step")
        block = ctx.enter_context(nc.Block())

        @block.scalar
        def _(act):
            for i in range(TILES):
                if i:
                    act.wait_ge(square_done, i)
                nc.scalar.activation(square[:], k.xn[:, i, :], ACT.Square, accum_out=mean2[:, i:i + 1]).then_inc(square_done, 1)
            act.wait_ge(shifted, 1)
            nc.scalar.activation(prob[:], prob[:], ACT.Exp).then_inc(exp_ready, 1)

        @block.gpsimd
        def _(pool):
            pool.wait_ge(square_done, TILES)
            nc.gpsimd.tensor_scalar(mean2[:], mean2[:], 1.0 / C, 1e-6, ALU.mult, ALU.add).then_inc(pool_step, 1)
            pool.wait_ge(pool_step, 1)
            nc.gpsimd.tensor_tensor(inv[:], mean2[:], k.neghalf[:, 0:TILES], ALU.pow).then_inc(pool_step, 1)
            pool.wait_ge(pool_step, 2)
            nc.gpsimd.tensor_scalar(inv[:], inv[:], float(C) ** -0.5, None, ALU.mult).then_inc(inv_ready, 1)

        @block.tensor
        def _(pe):
            pe.wait_ge(router_ready, KT)
            for i in range(TILES):
                for c in range(KT):
                    last = nc.tensor.matmul(k.ps[:, 0, i * E0:(i + 1) * E0], k.xT[:, c, i * P:(i + 1) * P],
                                            router[:, c, :], start=c == 0, stop=c == KT - 1)
            last.then_inc(logits_done, 1)

        @block.vector
        def _(dve):
            for s in (k.router_loaded, k.rscale_loaded, k.escale_loaded, k.lower_loaded):
                dve.wait_ge(s, 16)
            for c in range(KT):
                nc.vector.tensor_scalar(router[:, c, :], k.router[:, c, :], k.rscale[:, c:c + 1], None,
                                        ALU.mult).then_inc(router_ready, 1)
            dve.wait_ge(logits_done, 1)
            dve.wait_ge(inv_ready, 1)
            per_token = lambda v: v[:].unsqueeze(2).broadcast_to([P, TILES, E0])
            nc.vector.tensor_tensor(logits[:], k.ps[:, 0, 0:TILES * E0].rearrange("p (i e) -> p i e", i=TILES),
                                    per_token(inv), ALU.mult).then_inc(step.sem, step.one())
            dve.wait_ge(step.sem, step.n)
            nc.vector.tensor_reduce(top[:], logits[:], AX.X, ALU.max).then_inc(step.sem, step.one())
            mine = logits[:].unsqueeze(3).broadcast_to([P, TILES, E0, E0])
            other = logits[:].unsqueeze(2).broadcast_to([P, TILES, E0, E0])
            nc.vector.tensor_tensor(above[:], other, mine, ALU.is_gt).then_inc(step.sem, step.one())
            nc.vector.tensor_tensor(tied[:], other, mine, ALU.is_equal).then_inc(step.sem, step.one())
            dve.wait_ge(step.sem, step.n)
            nc.vector.tensor_tensor(prob[:], logits[:], per_token(top), ALU.subtract).then_inc(shifted, 1)
            nc.vector.tensor_tensor(tied[:], tied[:], k.lower[:].rearrange("p (e j) -> p e j", e=E0).unsqueeze(1)
                                    .broadcast_to([P, TILES, E0, E0]), ALU.mult).then_inc(step.sem, step.one())
            dve.wait_ge(step.sem, step.n)
            nc.vector.tensor_tensor(above[:], above[:], tied[:], ALU.add).then_inc(step.sem, step.one())
            dve.wait_ge(step.sem, step.n)
            nc.vector.tensor_reduce(before[:], above[:], AX.X, ALU.add).then_inc(step.sem, step.one())
            dve.wait_ge(step.sem, step.n)
            dve.wait_ge(exp_ready, 1)
            nc.vector.scalar_tensor_tensor(out=k.mix[:], in0=before[:], scalar=1.5, in1=prob[:],
                                           op0=ALU.is_lt, op1=ALU.mult).then_inc(step.sem, step.one())
            dve.wait_ge(step.sem, step.n)
            nc.vector.tensor_reduce(total[:], k.mix[:], AX.X, ALU.add).then_inc(step.sem, step.one())
            dve.wait_ge(step.sem, step.n)
            nc.vector.reciprocal(total[:], total[:]).then_inc(step.sem, step.one())
            dve.wait_ge(step.sem, step.n)
            nc.vector.tensor_tensor(k.mix[:], k.mix[:], per_token(total), ALU.mult).then_inc(step.sem, step.one())
            dve.wait_ge(step.sem, step.n)
            nc.vector.tensor_tensor(k.mix[:], k.mix[:], k.escale[:].unsqueeze(1).broadcast_to([P, TILES, E0]),
                                    ALU.mult)


def moe_experts_0(nc, k):
    with ExitStack() as ctx:
        sem = lambda n: k.semaphore(f"me_{n}")
        sb = lambda n, s: ctx.enter_context(nc.sbuf_tensor(f"me_{n}", s, F32))
        HALVES = TOK // BANK
        HT = H0 // P
        UNITS = E0 * HALVES
        gated, act_out = sb("gated", [P, 2, HT, BANK]), sb("hidden", [P, 2, HT, BANK])
        gate_up_ready, gelu_ready, hidden_ready, out_ready, added = (
            sem("gate_up"), sem("gelu"), sem("hidden_s"), sem("out"), sem("added"))
        block = ctx.enter_context(nc.Block())
        OUT_SLOTS = 4

        @block.tensor
        def _(pe):
            pe.wait_ge(k.gate_loaded, 16)
            pe.wait_ge(k.linear_loaded, 16)

            def gate_up(u):
                e, g = divmod(u, HALVES)
                for h in range(HT):
                    if u:
                        pe.wait_ge(hidden_ready, HT * (u - 1) + h + 1)
                    for part in range(2):
                        for c in range(KT):
                            at = part * H0 + h * P
                            last = nc.tensor.matmul(k.ps[:, 2 * h + part, :], k.gate[:, c, e, at:at + P],
                                                    k.xT[:, c, g * BANK:(g + 1) * BANK], start=c == 0, stop=c == KT - 1)
                    last.then_inc(gate_up_ready, 1)

            def down(u):
                e, g = divmod(u, HALVES)
                pe.wait_ge(hidden_ready, HT * (u + 1))
                for pair in range(2):
                    n = 2 * u + pair
                    if n >= OUT_SLOTS:
                        pe.wait_ge(added, 2 * (n - OUT_SLOTS + 1))
                    for j in range(2):
                        t = 2 * pair + j
                        for h in range(HT):
                            last = nc.tensor.matmul(k.ps[:, 4 + n % OUT_SLOTS, j * C:(j + 1) * C],
                                                    act_out[:, u % 2, h, t * P:(t + 1) * P], k.linear[:, h, e, :],
                                                    start=h == 0, stop=h == HT - 1)
                    last.then_inc(out_ready, 1)

            for u in range(UNITS + 1):
                if u < UNITS:
                    gate_up(u)
                if u:
                    down(u - 1)

        @block.scalar
        def _(act):
            for u in range(UNITS):
                for h in range(HT):
                    n = HT * u + h
                    act.wait_ge(gate_up_ready, n + 1)
                    if u >= 2:
                        act.wait_ge(hidden_ready, n - 2 * HT + 1)
                    nc.scalar.activation(gated[:, u % 2, h, :], k.ps[:, 2 * h, :], ACT.Gelu_apprx_tanh).then_inc(gelu_ready, 1)

        @block.vector
        def _(dve):
            def hidden(u):
                for h in range(HT):
                    dve.wait_ge(gelu_ready, HT * u + h + 1)
                    if u >= 2 and h == 0:
                        dve.wait_ge(out_ready, 2 * (u - 1))
                    nc.vector.tensor_tensor(act_out[:, u % 2, h, :], gated[:, u % 2, h, :], k.ps[:, 2 * h + 1, :],
                                            ALU.mult).then_inc(hidden_ready, 1)

            def add(u):
                e, g = divmod(u, HALVES)
                for pair in range(2):
                    n = 2 * u + pair
                    dve.wait_ge(out_ready, n + 1)
                    for j in range(2):
                        t = 4 * g + 2 * pair + j
                        if e:
                            dve.wait_ge(added, 4 * (u - HALVES) + 2 * pair + j + 1)
                        nc.vector.scalar_tensor_tensor(out=k.x[:, t, :], in0=k.ps[:, 4 + n % OUT_SLOTS, j * C:(j + 1) * C],
                                                       scalar=k.mix[:, t, e:e + 1], in1=k.x[:, t, :],
                                                       op0=ALU.mult, op1=ALU.add).then_inc(added, 1)

            for u in range(UNITS + 1):
                if u < UNITS:
                    hidden(u)
                if u:
                    add(u - 1)


H1, HKV, DH = 16, 4, 16
GROUP = H1 // HKV
WINDOW = 32
ROT = (GROUP + 1) * HKV
PAD = 32


def windowed_qkv(nc, k):
    with ExitStack() as ctx:
        sem = lambda n: k.semaphore(f"wq_{n}")
        sb = lambda n, s: ctx.enter_context(nc.sbuf_tensor(f"wq_{n}", s, F32))
        RC = ROT * DH
        HALF = DH // 2
        rot, cross = sb("rot", [P, TILES, ROT, 2, HALF]), sb("cross", [P, 2, ROT, 2, HALF])
        square, ss, inv = sb("square", [P, 2, RC]), sb("ss", [P, TILES, ROT]), sb("inv", [P, TILES, ROT])
        padded = sb("padded", [P, 2, ROT, PAD])
        projected, raw_used, ss_ready, norm_ready = sem("projected"), sem("raw_used"), sem("ss"), sem("norm_s")
        padded_ready, turned, copied, pads_clear = sem("padded_s"), sem("turned"), sem("copied"), sem("clear")
        step, floored = Steps(sem("step")), sem("floored")
        shift_done = k.shift_done
        block = ctx.enter_context(nc.Block())

        @block.tensor
        def _(pe):
            pe.wait_ge(k.wqkv_loaded, 16)
            for i in range(TILES):
                if i >= 4:
                    pe.wait_ge(raw_used, i - 3)
                for c in range(KT):
                    last = nc.tensor.matmul(k.ps[:, i % 4, 0:RC + HKV * DH], k.xT[:, c, i * P:(i + 1) * P], k.wqkv[:, c, :],
                                            start=c == 0, stop=c == KT - 1)
                last.then_inc(projected, 1)
            for i in range(TILES):
                pe.wait_ge(padded_ready, i + 1)
                if i >= 2:
                    pe.wait_ge(copied, 2 * (i - 1))
                for g in range(GROUP + 1):
                    last = nc.tensor.transpose(k.ps[:, 4 + 2 * (i % 2) + g // GROUP, (g % GROUP) * P:(g % GROUP + 1) * P],
                                               padded[:, i % 2, g * HKV:(g + 1) * HKV, :].rearrange("p h d -> p (h d)"), k.ident[:])
                last.then_inc(turned, 1)

        @block.vector
        def _(dve):
            dve.wait_ge(k.rope_loaded, 16)
            for i in range(TILES):
                dve.wait_ge(projected, i + 1)
                raw = k.ps[:, i % 4, 0:RC].rearrange("p (h s d) -> p h s d", s=2, d=HALF)
                wave = lambda n: k.rope[:, i % 2, n, :].unsqueeze(1).broadcast_to([P, ROT, HALF])
                nc.vector.tensor_tensor(rot[:, i].rearrange("p h s d -> p (h s) d"), raw.rearrange("p h s d -> p (h s) d"),
                                        k.rope[:, i % 2, 0, :].unsqueeze(1).broadcast_to([P, 2 * ROT, HALF]), ALU.mult).then_inc(step.sem, step.one())
                for half in range(2):
                    nc.vector.tensor_tensor(cross[:, i % 2, :, half, :], raw[:, :, 1 - half, :], wave(1 + half),
                                            ALU.mult).then_inc(step.sem, step.one())
                nc.vector.tensor_copy(k.v[:, i, :], k.ps[:, i % 4, RC:RC + HKV * DH]).then_inc(raw_used, 1)
                dve.wait_ge(step.sem, step.n)
                nc.vector.tensor_tensor(rot[:, i], rot[:, i], cross[:, i % 2], ALU.add).then_inc(step.sem, step.one())
                dve.wait_ge(step.sem, step.n)
                flat = rot[:, i].rearrange("p h s d -> p (h s d)")
                nc.vector.tensor_tensor(square[:, i % 2, :], flat, flat, ALU.mult).then_inc(step.sem, step.one())
                dve.wait_ge(step.sem, step.n)
                nc.vector.tensor_reduce(ss[:, i, :], square[:, i % 2, :].rearrange("p (h d) -> p h d", d=DH), AX.X,
                                        ALU.add).then_inc(ss_ready, 1)
            dve.wait_ge(ss_ready, TILES)
            nc.vector.tensor_scalar(ss[:], ss[:], 1e-24, None, ALU.max).then_inc(floored, 1)
            dve.wait_ge(norm_ready, 1)
            nc.vector.reciprocal(inv[:], inv[:]).then_inc(step.sem, step.one())
            dve.wait_ge(step.sem, step.n)
            dve.wait_ge(k.temp_loaded, 16)
            nc.vector.tensor_tensor(inv[:, :, 0:H1], inv[:, :, 0:H1], k.temp[:].unsqueeze(1).broadcast_to([P, TILES, H1]),
                                    ALU.mult).then_inc(step.sem, step.one())
            dve.wait_ge(step.sem, step.n)
            dve.wait_ge(pads_clear, 1)
            for i in range(TILES):
                if i >= 2:
                    dve.wait_ge(turned, i - 1)
                nc.vector.tensor_tensor(padded[:, i % 2, :, 0:DH], rot[:, i].rearrange("p h s d -> p h (s d)"),
                                        inv[:, i, :].unsqueeze(2).broadcast_to([P, ROT, DH]), ALU.mult).then_inc(padded_ready, 1)

        @block.gpsimd
        def _(pool):
            nc.gpsimd.memset(padded[:], 0.0).then_inc(pads_clear, 1)

        @block.scalar
        def _(act):
            act.wait_ge(floored, 1)
            nc.scalar.activation(inv[:], ss[:], ACT.Sqrt).then_inc(norm_ready, 1)
            for i in range(TILES):
                act.wait_ge(turned, i + 1)
                bank = 4 + 2 * (i % 2)
                nc.scalar.copy(k.qT[:, :, i * P:(i + 1) * P], k.ps[:, bank, :].rearrange("p (g t) -> p g t", g=GROUP)).then_inc(copied, 1)
                nc.scalar.copy(k.kT[:, i * P:(i + 1) * P], k.ps[:, bank + 1, 0:P]).then_inc(copied, 1)

        @block.sync
        def _(sp):
            sp.wait_ge(raw_used, TILES)
            sp.dma_start(k.vprev[:], k.v[P - WINDOW:P, 0:TILES:2, :]).then_inc(shift_done, 16)


def windowed_attention(nc, k):
    with ExitStack() as ctx:
        sem = lambda n: k.semaphore(f"wa_{n}")
        sb = lambda n, s: ctx.enter_context(nc.sbuf_tensor(f"wa_{n}", s, F32))
        KEYS = WINDOW + P
        UNITS = TILES * GROUP
        masked, probs = sb("masked", [P, 2, HKV, KEYS]), sb("probs", [P, 2, HKV, KEYS])
        top, ntop, total = sb("top", [P, 2, HKV]), sb("ntop", [P, 2, HKV]), sb("total", [P, TILES, HKV, GROUP])
        own, prev = sb("own", [P, 2, HKV, P]), sb("prev", [WINDOW, 2, HKV, P])
        rtotal, mixedT = sb("rtotal", [P, 2, HKV]), sb("mixedT", [P, 2, KT, P])
        v_pad, vprev_pad = sb("v_pad", [P, 2, TILES * HKV, 2 * DH]), sb("vprev_pad", [WINDOW, 2, B * HKV, 2 * DH])
        scored, maxed, ntop_ready, exp_ready = sem("scored"), sem("maxed"), sem("ntop_s"), sem("exp")
        turned, own_ready, prev_ready, weighed = sem("turned"), sem("own_s"), sem("prev_s"), sem("weighed")
        rtotal_ready, probs_ready, mixedT_ready, projected, added = sem("rtotal_s"), sem("probs_s"), sem("mixedT_s"), sem("projected"), sem("added")
        cleared, pad_ready = sem("cleared"), sem("pad_s")
        block = ctx.enter_context(nc.Block())
        first = lambda i: 0 if i % 2 else WINDOW

        def prevs(n):
            i, g = divmod(n, GROUP)
            return (i // 2) * GROUP + (g if i % 2 else 0)

        @block.tensor
        def _(pe):
            pe.wait_ge(k.wo_loaded, 16)

            def scores(n):
                i, g = divmod(n, GROUP)
                for j in range(HKV):
                    if n:
                        pe.wait_ge(maxed, HKV * (n - 1) + j + 1)
                    rows = slice(PAD * j, PAD * j + DH)
                    nc.tensor.matmul(k.ps[:, j, first(i):KEYS], k.qT[rows, g, i * P:(i + 1) * P],
                                     k.kT[rows, i * P + first(i) - WINDOW:(i + 1) * P],
                                     start=True, stop=True).then_inc(scored, 1)

            def turn(n):
                i, g = divmod(n, GROUP)
                pe.wait_ge(probs_ready, n + 1)
                if n:
                    pe.wait_ge(own_ready, n)
                for j in range(HKV):
                    last = nc.tensor.transpose(k.ps[:, 4, j * P:(j + 1) * P], probs[:, n % 2, j, WINDOW:KEYS], k.ident[:])
                if i % 2:
                    if prevs(n):
                        pe.wait_ge(prev_ready, prevs(n))
                    for j in range(HKV):
                        last = nc.tensor.transpose(k.ps[0:WINDOW, 5, j * P:(j + 1) * P], probs[:, n % 2, j, 0:WINDOW], k.ident[:])
                last.then_inc(turned, 1)

            def weigh(n):
                i, g = divmod(n, GROUP)
                pe.wait_ge(own_ready, n + 1)
                if i % 2:
                    pe.wait_ge(prev_ready, prevs(n) + 1)
                if n == 0:
                    pe.wait_ge(pad_ready, 4)
                if g == 0 and i >= 2:
                    pe.wait_ge(added, i - 1)
                for j in range(HKV):
                    opens, closes = g % 2 == 0 and j < 2, g % 2 == 1 and j >= 2
                    rows = P // 2 * (j % 2) + 2 * DH * (g // 2)
                    out = k.ps[rows:rows + 2 * DH, 6 + i % 2, (j // 2) * P:(j // 2 + 1) * P]
                    last = nc.tensor.matmul(out, v_pad[:, g % 2, i * HKV + j, :], own[:, n % 2, j, :], start=opens, stop=closes and i % 2 == 0)
                    if i % 2:
                        last = nc.tensor.matmul(out, vprev_pad[:, g % 2, (i // 2) * HKV + j, :], prev[:, n % 2, j, :], start=False, stop=closes)
                last.then_inc(weighed, 1)

            def project(i):
                pe.wait_ge(mixedT_ready, i + 1)
                for c in range(KT):
                    last = nc.tensor.matmul(k.ps[:, 6 + i % 2, C:2 * C], mixedT[:, i % 2, c, :], k.wo[:, c, :], start=c == 0, stop=c == KT - 1)
                last.then_inc(projected, 1)

            for n in range(UNITS + 2):
                if n < UNITS:
                    scores(n)
                if 1 <= n <= UNITS:
                    turn(n - 1)
                if n >= 2:
                    weigh(n - 2)
                if n >= 6 and n % GROUP == 2:
                    project(n // GROUP - 1)
            project(TILES - 1)

        @block.vector
        def _(dve):
            dve.wait_ge(cleared, 2)
            dve.wait_ge(k.shift_done, 16)
            for half in range(2):
                at = slice(half * DH, (half + 1) * DH)
                nc.vector.tensor_copy(v_pad[:, half, :, at], k.v[:].rearrange("p i (j d) -> p (i j) d", d=DH)).then_inc(pad_ready, 1)
                nc.vector.tensor_copy(vprev_pad[:, half, :, at], k.vprev[:].rearrange("p i (j d) -> p (i j) d", d=DH)).then_inc(pad_ready, 1)
            dve.wait_ge(k.wmask_loaded, 16)

            def mask(n):
                i, g = divmod(n, GROUP)
                if n >= 2:
                    dve.wait_ge(exp_ready, HKV * (n - 1))
                f = first(i)
                for j in range(HKV):
                    dve.wait_ge(scored, HKV * n + j + 1)
                    nc.vector.tensor_tensor_reduce(masked[:, n % 2, j, f:KEYS],
                                                   k.ps[:, j, f:KEYS],
                                                   k.wmask[:, f:KEYS], 1.0, -3e38, ALU.add, ALU.max,
                                                   top[:, n % 2, j:j + 1]).then_inc(maxed, 1)
                dve.wait_ge(maxed, HKV * (n + 1))
                nc.vector.tensor_scalar(ntop[:, n % 2, :], top[:, n % 2, :], -1.0, None, ALU.mult).then_inc(ntop_ready, 1)

            def copy_own(n):
                i, g = divmod(n, GROUP)
                dve.wait_ge(turned, n + 1)
                if n >= 2:
                    dve.wait_ge(weighed, n - 1)
                nc.vector.tensor_copy(own[:, n % 2].rearrange("p j t -> p (j t)"), k.ps[:, 4, :]).then_inc(own_ready, 1)

            def normalise(n):
                i, g = divmod(n, GROUP)
                dve.wait_ge(exp_ready, HKV * (n + 1))
                nc.vector.reciprocal(rtotal[:, n % 2, :], total[:, i, :, g]).then_inc(rtotal_ready, 1)
                dve.wait_ge(rtotal_ready, n + 1)
                f = first(i)
                nc.vector.tensor_tensor(probs[:, n % 2, :, f:KEYS], probs[:, n % 2, :, f:KEYS], rtotal[:, n % 2, :].unsqueeze(2).broadcast_to([P, HKV, KEYS - f]),
                                        ALU.mult).then_inc(probs_ready, 1)

            def add(i):
                dve.wait_ge(projected, i + 1)
                nc.vector.tensor_tensor(k.x[:, i, :], k.ps[:, 6 + i % 2, C:2 * C], k.x[:, i, :], ALU.add).then_inc(added, 1)

            for n in range(UNITS + 2):
                if 1 <= n <= UNITS:
                    normalise(n - 1)
                if n < UNITS:
                    mask(n)
                if 1 <= n <= UNITS:
                    copy_own(n - 1)
                if n >= 7 and n % GROUP == 3:
                    add(n // GROUP - 1)
            add(TILES - 1)

        @block.gpsimd
        def _(pool):
            nc.gpsimd.memset(v_pad[:], 0.0).then_inc(cleared, 1)
            nc.gpsimd.memset(vprev_pad[:], 0.0).then_inc(cleared, 1)

        @block.scalar
        def _(act):
            def exponentials(n):
                i, g = divmod(n, GROUP)
                act.wait_ge(ntop_ready, n + 1)
                if n >= 2:
                    act.wait_ge(turned, n - 1)
                f = first(i)
                for j in range(HKV):
                    nc.scalar.activation(probs[:, n % 2, j, f:KEYS], masked[:, n % 2, j, f:KEYS], ACT.Exp,
                                         bias=ntop[:, n % 2, j:j + 1], accum_out=total[:, i, j, g:g + 1]).then_inc(exp_ready, 1)

            def copy_prev(n):
                i, g = divmod(n, GROUP)
                if i % 2:
                    act.wait_ge(turned, n + 1)
                    if prevs(n) >= 2:
                        act.wait_ge(weighed, n - 1 if g >= 2 else n - GROUP - 1 if g < 2 else 0)
                    nc.scalar.copy(prev[:, n % 2].rearrange("p j t -> p (j t)"), k.ps[0:WINDOW, 5, :]).then_inc(prev_ready, 1)

            def copy_mixed(i):
                act.wait_ge(weighed, GROUP * (i + 1))
                if i >= 2:
                    act.wait_ge(projected, i - 1)
                nc.scalar.copy(mixedT[:, i % 2].rearrange("p c t -> p (c t)"), k.ps[:, 6 + i % 2, 0:C]).then_inc(mixedT_ready, 1)

            for n in range(UNITS + 2):
                if n < UNITS:
                    exponentials(n)
                if 1 <= n <= UNITS:
                    copy_prev(n - 1)
                if n >= 6 and n % GROUP == 2:
                    copy_mixed(n // GROUP - 1)
            copy_mixed(TILES - 1)


def cross_attention_1(nc, k):
    with ExitStack() as ctx:
        sem = lambda n: k.semaphore(f"xa1_{n}")
        sb = lambda n, s: ctx.enter_context(nc.sbuf_tensor(f"xa1_{n}", s, F32))
        ALPHA, D = 5.0, 32
        HEADS = P // D
        square, norm = sb("square", [P, 2, BANK]), sb("norm", [P, 2, BANK])
        floored = sb("floored", [P, 2, BANK])
        qn, kn = sb("qn", [P, TILES, C]), sb("kn", [P, TILES, C])
        expd, ones = sb("expd", [P, 2, HEADS, KT, C]), sb("ones", [P, D])
        rden, out = sb("rden", [P, 2, C]), sb("out", [P, 2, C])
        square_ready, summed, floor_ready, norm_ready, scaled = (
            sem("square_s"), sem("summed"), sem("floor"), sem("norm_s"), sem("scaled"))
        inv_ready = sem("inv")
        scored, exp_ready, weighed, rden_ready, out_ready, added, ones_ready = (
            sem("scored"), sem("exp_s"), sem("weighed"), sem("rden_s"), sem("out_s"), sem("added"), sem("ones_s"))
        block = ctx.enter_context(nc.Block())
        GROUPS = TILES
        tile_of = lambda n: 2 * (n // 2)
        SETS = GROUPS // 2

        def in_order(norms, tile):
            for s in range(-2, SETS):
                if s >= 0:
                    tile(2 * s)
                    tile(2 * s + 1)
                if s + 2 < SETS:
                    norms((2 * (s + 2), 2 * (s + 2) + 1))

        @block.tensor
        def _(pe):
            pe.wait_ge(k.diag_loaded, 16)

            def norms(pair):
                for n in pair:
                    pe.wait_ge(square_ready, n + 1)
                    if n >= 2:
                        pe.wait_ge(floor_ready, n - 1)
                    nc.tensor.matmul(k.ps[:, 6 + n % 2, :], k.diag[:], square[:, n % 2, :], start=True, stop=True).then_inc(summed, 1)

            def scores(i):
                pe.wait_ge(scaled, 2 * (i // 2 + 1))
                for half in range(KT):
                    for j in range(HEADS):
                        if i and half == 0:
                            pe.wait_ge(exp_ready, HEADS * (i - 1) + j + 1)
                        last = nc.tensor.matmul(k.ps[:, j, half * C:(half + 1) * C], kn[D * j:D * (j + 1), i, half * P:(half + 1) * P],
                                                qn[D * j:D * (j + 1), i, :], start=True, stop=True)
                        if half == KT - 1:
                            last.then_inc(scored, 1)

            def weigh(i):
                pe.wait_ge(exp_ready, HEADS * (i + 1))
                if i == 0:
                    pe.wait_ge(ones_ready, 1)
                    pe.wait_ge(k.ctxT_loaded, 16)
                if i >= 2:
                    pe.wait_ge(out_ready, i - 1)
                for part in range(2):
                    for half in range(KT):
                        for j in range(HEADS):
                            at = (i % 2) * P + D * j
                            weights = ones[:] if part else k.ctxT[:, (i // 2) * KT + half, at:at + D]
                            last = nc.tensor.matmul(k.ps[D * j:D * (j + 1), 4 + i % 2, part * C:(part + 1) * C], weights, expd[:, i % 2, j, half, :],
                                                    start=half == 0, stop=half == KT - 1)
                last.then_inc(weighed, 1)

            def tile(i):
                scores(i)
                if i:
                    weigh(i - 1)

            in_order(norms, tile)
            weigh(TILES - 1)

        @block.vector
        def _(dve):
            nc.vector.memset(ones[:], 1.0).then_inc(ones_ready, 1)

            def norms(pair):
                for n in pair:
                    dve.wait_ge(summed, n + 1)
                    if n >= 2:
                        dve.wait_ge(norm_ready, n - 1)
                    nc.vector.tensor_scalar(floored[:, n % 2, :], k.ps[:, 6 + n % 2, :], 1e-24, None, ALU.max).then_inc(floor_ready, 1)
                for n in pair:
                    dve.wait_ge(norm_ready, n + 1)
                    nc.vector.reciprocal(norm[:, n % 2, :], norm[:, n % 2, :]).then_inc(inv_ready, 1)
                    dve.wait_ge(inv_ready, n + 1)
                    src, dst = (k.xn, qn) if n % 2 == 0 else (k.ctx, kn)
                    i = tile_of(n)
                    nc.vector.tensor_tensor(dst[:, i:i + 2, :], src[:, i:i + 2, :], norm[:, n % 2, :].rearrange("p (i c) -> p i c", i=2),
                                            ALU.mult).then_inc(scaled, 1)

            def finish(i):
                dve.wait_ge(weighed, i + 1)
                nc.vector.reciprocal(rden[:, i % 2, :], k.ps[:, 4 + i % 2, C:2 * C]).then_inc(rden_ready, 1)
                dve.wait_ge(rden_ready, i + 1)
                if i >= 2:
                    dve.wait_ge(added, i - 1)
                nc.vector.tensor_tensor(out[:, i % 2, :], k.ps[:, 4 + i % 2, 0:C], rden[:, i % 2, :], ALU.mult).then_inc(out_ready, 1)
                dve.wait_ge(out_ready, i + 1)
                nc.vector.tensor_tensor(k.x[:, i, :], out[:, i % 2, :], k.x[:, i, :], ALU.add).then_inc(added, 1)

            def tile(i):
                if i:
                    finish(i - 1)

            in_order(norms, tile)
            finish(TILES - 1)

        @block.scalar
        def _(act):
            act.wait_ge(k.ctx_loaded, 16)

            def norms(pair):
                for n in pair:
                    if n >= 2:
                        act.wait_ge(summed, n - 1)
                    src = k.xn if n % 2 == 0 else k.ctx
                    i = tile_of(n)
                    nc.scalar.activation(square[:, n % 2, :].rearrange("p (i c) -> p i c", i=2), src[:, i:i + 2, :], ACT.Square).then_inc(square_ready, 1)
                for n in pair:
                    act.wait_ge(floor_ready, n + 1)
                    if n >= 2:
                        act.wait_ge(scaled, n - 1)
                    nc.scalar.activation(norm[:, n % 2, :], floored[:, n % 2, :], ACT.Sqrt).then_inc(norm_ready, 1)

            def tile(i):
                if i >= 2:
                    act.wait_ge(weighed, i - 1)
                for j in range(HEADS):
                    act.wait_ge(scored, HEADS * i + j + 1)
                    nc.scalar.activation(expd[:, i % 2, j].rearrange("p h q -> p (h q)"), k.ps[:, j, :], ACT.Exp, scale=ALPHA).then_inc(exp_ready, 1)

            in_order(norms, tile)


E1 = 8


def soft_experts_1(nc, k):
    with ExitStack() as ctx:
        sem = lambda n: k.semaphore(f"sr_{n}")
        sb = lambda n, s: ctx.enter_context(nc.sbuf_tensor(f"sr_{n}", s, F32))
        OT = C // P
        UNITS = B * OT
        PAIRS = E1 // 2
        logits, shifted = sb("logits", [P, 2, E1, T]), sb("shifted", [P, 2, E1, T])
        high, low, mixed = sb("high", [P, 7, T]), sb("low", [P, 7, T]), sb("mid", [P, 3, T])
        first, second = sb("first", [P, 2, T]), sb("second", [P, 2, T])
        lse, chosen = sb("lse", [P, 2, T]), sb("chosen", [P, E1, T])
        weight, pick = sb("weight", [P, 2, OT, E1, T]), sb("pick", [P, E1, E1])
        scored, logits_ready, gap_ready, log_ready = sem("scored"), sem("logits_s"), sem("gap"), sem("log")
        lse_ready, shifted_ready, exp_ready, weight_ready = sem("lse_s"), sem("shifted_s"), sem("exp"), sem("weight_s")
        summed, share_ready, turned, shareT_ready, pick_ready = sem("summed"), sem("share"), sem("turned"), sem("shareT"), sem("pick_s")
        step, log_step = Steps(sem("step")), sem("log_step")
        out_ready, summed_up = sem("out"), sem("summed_up")
        block = ctx.enter_context(nc.Block())
        LAG = 4
        ALL = PAIRS + 1
        sums_until = lambda u: (u // ALL) * (E1 + 1) + min(2 * (u % ALL + 1), E1 + 1)

        def in_order(begin, early, middle, batch_sums, late, batch_end):
            for n in range(TILES + LAG):
                tile, seq = n - LAG, (n - 3) // 2 if n % 2 and n >= 3 and (n - 3) // 2 < B else None
                begin(n, seq)
                if tile >= 0:
                    early(tile)
                middle(n)
                if seq is not None:
                    batch_sums(seq)
                if tile >= 0:
                    late(tile)
                if seq is not None:
                    batch_end(seq)

        @block.tensor
        def _(pe):
            pe.wait_ge(k.rw1_loaded, 16)

            def scores(n):
                b, o = divmod(n, OT)
                for p in range(PAIRS):
                    if n:
                        pe.wait_ge(logits_ready, E1 * (n - 1) + 2 * p + 2)
                    for j in range(2):
                        for c in range(KT):
                            last = nc.tensor.matmul(k.ps[:, p, j * T:(j + 1) * T], k.rw1[:, c, 2 * p + j, o * P:(o + 1) * P],
                                                    k.xT[:, c, b * T:(b + 1) * T], start=c == 0, stop=c == KT - 1)
                    last.then_inc(scored, 1)

            def sums(b):
                pe.wait_ge(weight_ready, OT * (b + 1))
                if b:
                    pe.wait_ge(shareT_ready, b)
                for e in range(E1):
                    for o in range(OT):
                        last = nc.tensor.matmul(k.ps[0:E1, 4, 0:T], pick[:, e, :], weight[:, b % 2, o, e, :],
                                                start=e == 0 and o == 0, stop=e == E1 - 1 and o == OT - 1)
                last.then_inc(summed, 1)

            def turn(b):
                pe.wait_ge(shareT_ready, b + 1)
                if b:
                    pe.wait_ge(share_ready, b)
                for t in range(2):
                    last = nc.tensor.transpose(k.ps[:, 5, t * E1:(t + 1) * E1], k.shareT[:, b * T + t * P:b * T + (t + 1) * P], k.ident[0:E1, 0:E1])
                last.then_inc(turned, 1)

            def expert_outputs(t, p):
                u = t * ALL + p
                if u >= 2:
                    pe.wait_ge(summed_up, sums_until(u - 2))
                if p < PAIRS:
                    for c in range(KT):
                        last = nc.tensor.matmul(k.ps[:, 6 + u % 2, :], k.xT[:, c, t * P:(t + 1) * P],
                                                k.we1[:, c, 2 * p:2 * p + 2, :].rearrange("p e o -> p (e o)"), start=c == 0, stop=c == KT - 1)
                else:
                    last = nc.tensor.matmul(k.ps[:, 6 + u % 2, 0:C], k.shareT[:, t * P:(t + 1) * P], k.be1[:], start=True, stop=True)
                last.then_inc(out_ready, 1)

            def begin(n, seq):
                if seq is not None:
                    sums(seq)

            def early(t):
                expert_outputs(t, 0)
                expert_outputs(t, 1)

            def middle(n):
                if n + 1 < UNITS:
                    scores(n + 1)

            def late(t):
                for p in range(2, ALL):
                    expert_outputs(t, p)

            pe.wait_ge(pick_ready, 2)
            pe.wait_ge(k.we1_loaded, 16)
            pe.wait_ge(k.be1_loaded, 16)
            scores(0)
            in_order(begin, early, middle, lambda seq: None, late, turn)

        @block.scalar
        def _(act):
            act.wait_ge(k.rb1_loaded, 16)

            def logit(n):
                b, o = divmod(n, OT)
                for p in range(PAIRS):
                    act.wait_ge(scored, PAIRS * n + p + 1)
                    if n >= 2 and p == 0:
                        act.wait_ge(weight_ready, n - 1)
                    for j in range(2):
                        nc.scalar.activation(logits[:, n % 2, 2 * p + j, :], k.ps[:, p, j * T:(j + 1) * T], ACT.Identity,
                                             bias=k.rb1[:, o, 2 * p + j:2 * p + j + 1]).then_inc(logits_ready, 1)

            def log_of_sum(n):
                act.wait_ge(gap_ready, n + 1)
                nc.scalar.activation(lse[:, n % 2, :], lse[:, n % 2, :], ACT.Exp).then_inc(log_step, 1)
                act.wait_ge(log_step, n + 1)
                nc.scalar.activation(lse[:, n % 2, :], lse[:, n % 2, :], ACT.Ln, bias=1.0).then_inc(log_ready, 1)

            def exponentials(n):
                act.wait_ge(shifted_ready, n + 1)
                nc.scalar.activation(shifted[:, n % 2].rearrange("p e t -> p (e t)"), shifted[:, n % 2].rearrange("p e t -> p (e t)"),
                                     ACT.Exp).then_inc(exp_ready, 1)

            for n in range(UNITS + 1):
                if n:
                    log_of_sum(n - 1)
                if n < UNITS:
                    logit(n)
                if n:
                    exponentials(n - 1)

        @block.gpsimd
        def _(pool):
            for n in range(UNITS):
                pool.wait_ge(lse_ready, n + 1)
                if n >= 2:
                    pool.wait_ge(weight_ready, n - 1)
                nc.gpsimd.tensor_tensor(shifted[:, n % 2], logits[:, n % 2], lse[:, n % 2, :].unsqueeze(1).broadcast_to([P, E1, T]),
                                        ALU.subtract).then_inc(shifted_ready, 1)

        @block.vector
        def _(dve):
            nc.vector.memset(pick[:], 0.0).then_inc(pick_ready, 1)
            dve.wait_ge(pick_ready, 1)
            nc.vector.memset(pick[:].rearrange("p e m -> p (e m)")[:, 0:E1 * E1:E1 + 1], 1.0).then_inc(pick_ready, 1)

            def both(level, out, a, b_, op):
                nc.vector.tensor_tensor(out, a, b_, op).then_inc(step.sem, step.one())

            def top_two(n):
                lg = logits[:, n % 2]
                dve.wait_ge(logits_ready, E1 * (n + 1))
                both(0, high[:, 0:4], lg[:, 0:4], lg[:, 4:8], ALU.max)
                both(0, low[:, 0:4], lg[:, 0:4], lg[:, 4:8], ALU.min)
                dve.wait_ge(step.sem, step.n)
                both(1, high[:, 4:6], high[:, 0:2], high[:, 2:4], ALU.max)
                both(1, mixed[:, 0:2], high[:, 0:2], high[:, 2:4], ALU.min)
                both(1, low[:, 4:6], low[:, 0:2], low[:, 2:4], ALU.max)
                dve.wait_ge(step.sem, step.n)
                both(1, low[:, 4:6], low[:, 4:6], mixed[:, 0:2], ALU.max)
                both(2, first[:, n % 2, :], high[:, 4, :], high[:, 5, :], ALU.max)
                both(2, mixed[:, 2, :], high[:, 4, :], high[:, 5, :], ALU.min)
                dve.wait_ge(step.sem, step.n)
                both(2, low[:, 6, :], low[:, 4, :], low[:, 5, :], ALU.max)
                dve.wait_ge(step.sem, step.n)
                if n >= 2:
                    dve.wait_ge(shifted_ready, n - 1)
                both(2, second[:, n % 2, :], low[:, 6, :], mixed[:, 2, :], ALU.max)
                dve.wait_ge(step.sem, step.n)
                nc.vector.tensor_tensor(lse[:, n % 2, :], second[:, n % 2, :], first[:, n % 2, :], ALU.subtract).then_inc(gap_ready, 1)

            def add_first(n):
                dve.wait_ge(log_ready, n + 1)
                nc.vector.tensor_tensor(lse[:, n % 2, :], lse[:, n % 2, :], first[:, n % 2, :], ALU.add).then_inc(lse_ready, 1)

            def choose(n):
                b, o = divmod(n, OT)
                if n:
                    dve.wait_ge(weight_ready, n)
                nc.vector.tensor_tensor(chosen[:], logits[:, n % 2], second[:, n % 2, :].unsqueeze(1).broadcast_to([P, E1, T]),
                                        ALU.is_ge).then_inc(step.sem, step.one())
                dve.wait_ge(step.sem, step.n)
                dve.wait_ge(exp_ready, n + 1)
                if b >= 2:
                    dve.wait_ge(summed, b - 1)
                nc.vector.tensor_tensor(weight[:, b % 2, o], chosen[:], shifted[:, n % 2], ALU.mult).then_inc(weight_ready, 1)

            def collect(b):
                dve.wait_ge(summed, b + 1)
                nc.vector.tensor_copy(k.shareT[:, b * T:(b + 1) * T], k.ps[0:E1, 4, 0:T]).then_inc(shareT_ready, 1)

            def share(b):
                dve.wait_ge(turned, b + 1)
                nc.vector.tensor_copy(k.share[:, 2 * b:2 * b + 2, :], k.ps[:, 5, 0:2 * E1].rearrange("p (t e) -> p t e", t=2)).then_inc(share_ready, 1)

            def add_up(t, p):
                u = t * ALL + p
                dve.wait_ge(out_ready, u + 1)
                if p:
                    dve.wait_ge(summed_up, sums_until(u - 1))
                else:
                    dve.wait_ge(share_ready, t // 2 + 1)
                if p == PAIRS:
                    nc.vector.tensor_tensor(k.x[:, t, :], k.ps[:, 6 + u % 2, 0:C], k.x[:, t, :], ALU.add).then_inc(summed_up, 1)
                    return
                for j in range(2):
                    if j:
                        dve.wait_ge(summed_up, sums_until(u) - 1)
                    nc.vector.scalar_tensor_tensor(out=k.x[:, t, :], in0=k.ps[:, 6 + u % 2, j * C:(j + 1) * C],
                                                   scalar=k.share[:, t, 2 * p + j:2 * p + j + 1], in1=k.x[:, t, :],
                                                   op0=ALU.mult, op1=ALU.add).then_inc(summed_up, 1)

            def begin(n, seq):
                if n < UNITS:
                    top_two(n)

            def early(t):
                add_up(t, 0)
                add_up(t, 1)

            def middle(n):
                if 1 <= n <= UNITS:
                    choose(n - 1)
                if n < UNITS:
                    add_first(n)

            def late(t):
                for p in range(2, ALL):
                    add_up(t, p)

            in_order(begin, early, middle, collect, late, share)


I32 = mybir.dt.int32
NK, DK, NV, DV = 16, 128, 32, 128
PV = NV // NK
TAPS = 4
BLK = 32
GB = P // BLK
UNITS = TILES * PV
NEG = -1e30
FRONT = 1 + 2 * PV
RMS_EPS, NORM_EPS2 = 1e-6, 1e-24


def decays(nc, k):
    with ExitStack() as ctx:
        sem = lambda n: k.semaphore(f"dc_{n}")
        sb = lambda n, s: ctx.enter_context(nc.sbuf_tensor(f"dc_{n}", s, F32))
        eb, a, mag, soft, rate = sb("eb", [P, TILES, NV]), sb("a", [P, TILES, NV]), sb("mag", [P, TILES, NV]), sb("soft", [P, TILES, NV]), sb("rate", [P, NV])
        ld, rows = sb("ld", [P, TILES, NV]), sb("rows", [NV, 2, TOK])
        projected, eb_ready, mag_ready, rate_ready, exp_ready, soft_ready = (
            sem("projected"), sem("eb_s"), sem("mag_s"), sem("rate_s"), sem("exp"), sem("soft_s"))
        ld_ready, summed, ccol_ready, beta_ready, turned, rows_ready, stored = (
            sem("ld_s"), sem("summed"), sem("ccol"), sem("beta"), sem("turned"), sem("rows_s"), sem("stored"))
        step = Steps(sem("step"))
        block = ctx.enter_context(nc.Block())
        W2 = 2 * NV

        @block.tensor
        def _(pe):
            pe.wait_ge(k.wba_loaded, 16)
            for i in range(TILES):
                for c in range(KT):
                    last = nc.tensor.matmul(k.ps[:, 0, i * W2:(i + 1) * W2], k.xT[:, c, i * P:(i + 1) * P], k.wba[:, c, :],
                                            start=c == 0, stop=c == KT - 1)
            last.then_inc(projected, 1)
            pe.wait_ge(ld_ready, 1)
            for i in range(TILES):
                out = k.ps[:, 1, i * NV:(i + 1) * NV]
                last = nc.tensor.matmul(out, k.upto[:], ld[:, i, :], start=True, stop=i % 2 == 0)
                if i % 2:
                    last = nc.tensor.matmul(out, k.ones[:], ld[:, i - 1, :], start=False, stop=True)
            last.then_inc(summed, 1)
            pe.wait_ge(ccol_ready, 1)
            pe.wait_ge(beta_ready, 1)
            for n, src in enumerate((k.ccol, k.beta)):
                for i in range(TILES):
                    last = nc.tensor.transpose(k.ps[0:NV, 2 + 2 * n + i // 4, (i % 4) * P:(i % 4 + 1) * P], src[:, i, :], k.ident[:])
            last.then_inc(turned, 1)

        @block.scalar
        def _(act):
            act.wait_ge(projected, 1)
            raw = k.ps[:, 0, :].rearrange("p (i n h) -> p i n h", n=2, h=NV)
            nc.scalar.activation(eb[:], raw[:, :, 0, :], ACT.Exp, scale=-1.0).then_inc(eb_ready, 1)
            act.wait_ge(k.alog_loaded, 16)
            nc.scalar.activation(rate[:], k.alog[:], ACT.Exp).then_inc(rate_ready, 1)
            act.wait_ge(mag_ready, 1)
            nc.scalar.activation(soft[:], mag[:], ACT.Exp, scale=-1.0).then_inc(exp_ready, 1)
            act.wait_ge(exp_ready, 1)
            nc.scalar.activation(soft[:], soft[:], ACT.Ln, bias=1.0).then_inc(soft_ready, 1)

        @block.vector
        def _(dve):
            dve.wait_ge(eb_ready, 1)
            dve.wait_ge(k.dtb_loaded, 16)
            raw = k.ps[:, 0, :].rearrange("p (i n h) -> p i n h", n=2, h=NV)
            nc.vector.tensor_tensor(a[:], raw[:, :, 1, :], k.dtb[:].unsqueeze(1).broadcast_to([P, TILES, NV]), ALU.add).then_inc(step.sem, step.one())
            nc.vector.tensor_scalar(eb[:], eb[:], 1.0, None, ALU.add).then_inc(step.sem, step.one())
            dve.wait_ge(step.sem, step.n)
            nc.vector.scalar_tensor_tensor(out=mag[:], in0=a[:], scalar=-1.0, in1=a[:], op0=ALU.mult, op1=ALU.max).then_inc(mag_ready, 1)
            nc.vector.reciprocal(k.beta[:], eb[:]).then_inc(beta_ready, 1)
            dve.wait_ge(soft_ready, 1)
            nc.vector.scalar_tensor_tensor(out=soft[:], in0=a[:], scalar=0.0, in1=soft[:], op0=ALU.max, op1=ALU.add).then_inc(step.sem, step.one())
            dve.wait_ge(step.sem, step.n)
            dve.wait_ge(rate_ready, 1)
            nc.vector.scalar_tensor_tensor(out=ld[:], in0=soft[:], scalar=-1.0, in1=rate[:].unsqueeze(1).broadcast_to([P, TILES, NV]),
                                           op0=ALU.mult, op1=ALU.mult).then_inc(ld_ready, 1)
            dve.wait_ge(summed, 1)
            nc.vector.tensor_copy(k.ccol[:].rearrange("p i h -> p (i h)"), k.ps[:, 1, 0:TILES * NV]).then_inc(ccol_ready, 1)
            dve.wait_ge(turned, 1)
            for n in range(2):
                for g in range(2):
                    nc.vector.tensor_copy(rows[:, n, g * BANK:(g + 1) * BANK], k.ps[0:NV, 2 + 2 * n + g, :]).then_inc(rows_ready, 1)

        @block.sync
        def _(sp):
            sp.wait_ge(rows_ready, 4)
            sp.dma_start(k.crow_d, rows[:, 0, :]).then_inc(stored, 16)
            sp.dma_start(k.brow_d, rows[:, 1, :]).then_inc(stored, 16)
            sp.wait_ge(stored, 32)


def conv_taps(nc, dve, bank, out, taps, done):
    raw, acc = bank.rearrange("p (b t) -> p b t", b=2), out.rearrange("p (b t) -> p b t", b=2)
    for n in range(TAPS - 1):
        back = n + 1
        done(n, nc.vector.scalar_tensor_tensor(out=acc[:, :, back:T], in0=raw[:, :, 0:T - back], scalar=taps[:, TAPS - 1 - back:TAPS - back],
                                               in1=acc[:, :, back:T], op0=ALU.mult, op1=ALU.add))


def is_first(n, of=1):
    return isinstance(n, int) and n < of


class BlockInverse:

    def __init__(self, nc, k, ctx, name):
        sem = lambda n: k.semaphore(f"{name}_{n}")
        sb = lambda n, s: ctx.enter_context(nc.sbuf_tensor(f"{name}_{n}", s, F32))
        self.nc, self.k = nc, k
        self.gram, self.c, self.b = sb("gram", [P, BLK, BLK]), sb("c", [P, BLK]), sb("b", [P, BLK])
        self.low, self.inv = sb("low", [P, BLK, BLK]), sb("inv", [P, BLK, BLK])
        self.invT = self.gram
        self.w, self.prod = sb("w", [P, BLK]), sb("prod", [P, 256])
        self.loaded, self.w_step, self.w_ready, self.gap_ready, self.floor_ready = sem("loaded"), sem("w_step"), sem("w_s"), sem("gap"), sem("floor")
        self.exp_ready, self.seeded, self.times, self.product, self.updated = sem("exp"), sem("seeded"), sem("times"), sem("product"), sem("updated")
        self.done, self.invT_ready, self.stored = sem("done"), sem("invT_s"), sem("stored")

    def load(self, sp, m, n):
        k = self.k
        if not is_first(n):
            sp.wait_ge(self.done, n)
        for e in range(2):
            for v in range(PV):
                at = (2 * e + v) * BLK
                sp.dma_start(self.gram[at:at + BLK].rearrange("p s t -> p (s t)"), k.gram_d[bass.ds(2 * m + e, 1)].rearrange("o q f -> (o q) f")).then_inc(self.loaded, 16)
        for dst, src in ((self.c, k.crow_d), (self.b, k.brow_d)):
            sp.dma_start(dst[:], src[bass.ds(4 * m, 4)].rearrange("h (q t) -> (h q) t", t=BLK)).then_inc(self.loaded, 16)

    def vector_weights(self, dve, n):
        nc = self.nc
        dve.wait_ge(self.loaded, 96 * (n + 1))
        if not is_first(n):
            dve.wait_ge(self.done, n)
        diag = self.gram[:].rearrange("p s t -> p (s t)")[:, 0:BLK * BLK:BLK + 1]
        nc.vector.tensor_scalar(self.w[:], diag, NORM_EPS2, None, ALU.max).then_inc(self.w_step, 1)
        dve.wait_ge(self.w_step, 2 * n + 1)
        nc.vector.reciprocal(self.w[:], self.w[:]).then_inc(self.w_step, 1)
        dve.wait_ge(self.w_step, 2 * n + 2)
        nc.vector.tensor_tensor(self.w[:], self.w[:], self.b[:], ALU.mult).then_inc(self.w_ready, 1)

    def vector_floor(self, dve, n):
        dve.wait_ge(self.gap_ready, n + 1)
        self.nc.vector.tensor_scalar(self.low[:, :, 1:], self.low[:, :, 1:], 0.0, None, ALU.min).then_inc(self.floor_ready, 1)

    def scalar_exp(self, act, n):
        act.wait_ge(self.floor_ready, n + 1)
        self.nc.scalar.activation(self.low[:, :, 1:], self.low[:, :, 1:], ACT.Exp).then_inc(self.exp_ready, 1)

    def vector_transpose(self, dve, n):
        dve.wait_ge(self.done, n + 1)
        if not is_first(n):
            dve.wait_ge(self.stored, 32 * n)
        self.nc.vector.tensor_copy(self.invT[:].rearrange("p k i -> p i k"), self.inv[:]).then_inc(self.invT_ready, 1)

    def store(self, sp, n):
        sp.wait_ge(self.invT_ready, n + 1)
        sp.dma_start(self.k.inv_d, self.inv[:].rearrange("p i k -> p (i k)")).then_inc(self.stored, 16)
        sp.dma_start(self.k.invT_d, self.invT[:].rearrange("p i k -> p (i k)")).then_inc(self.stored, 16)
        sp.wait_ge(self.stored, 32 * (n + 1))

    def invert(self, pool, n):
        nc, low, inv = self.nc, self.low, self.inv
        pool.wait_ge(self.loaded, 96 * (n + 1))
        if not is_first(n):
            pool.wait_ge(self.done, n)
            pool.wait_ge(self.stored, 32 * n)
        full = [P, BLK, BLK - 1]
        nc.gpsimd.tensor_tensor(low[:, :, 1:], self.c[:, 0:BLK - 1].unsqueeze(1).broadcast_to(full), self.c[:].unsqueeze(2).broadcast_to(full),
                                ALU.subtract).then_inc(self.gap_ready, 1)
        nc.gpsimd.memset(inv[:], 0.0).then_inc(self.seeded, 1)
        pool.wait_ge(self.exp_ready, n + 1)
        nc.gpsimd.tensor_tensor(low[:, :, 1:], low[:, :, 1:], self.gram[:, :, 1:], ALU.mult).then_inc(self.times, 1)
        pool.wait_ge(self.times, 2 * n + 1)
        pool.wait_ge(self.w_ready, n + 1)
        pool.wait_ge(self.seeded, 2 * n + 1)
        nc.gpsimd.tensor_tensor(low[:, :, 1:], low[:, :, 1:], self.w[:].unsqueeze(2).broadcast_to(full), ALU.mult).then_inc(self.times, 1)
        nc.gpsimd.memset(inv[:].rearrange("p i k -> p (i k)")[:, 0:BLK * BLK:BLK + 1], 1.0).then_inc(self.seeded, 1)
        pool.wait_ge(self.times, 2 * n + 2)
        pool.wait_ge(self.seeded, 2 * n + 2)
        for j in range(BLK - 1):
            rows, cols = BLK - 1 - j, j + 1
            prod = self.prod[:, 0:rows * cols].rearrange("p (i k) -> p i k", k=cols)
            if j:
                pool.wait_ge(self.updated, (BLK - 2) * n + j)
            nc.gpsimd.tensor_tensor(prod, low[:, j, j + 1:].unsqueeze(2).broadcast_to([P, rows, cols]),
                                    inv[:, j, 0:cols].unsqueeze(1).broadcast_to([P, rows, cols]), ALU.mult).then_inc(self.product, 1)
            pool.wait_ge(self.product, (BLK - 1) * n + j + 1)
            nc.gpsimd.tensor_tensor(inv[:, j + 1:, 0:cols], inv[:, j + 1:, 0:cols], prod, ALU.subtract).then_inc(
                self.updated if j < BLK - 2 else self.done, 1)


def keys(nc, k):
    with ExitStack() as ctx:
        sem = lambda n: k.semaphore(f"ks_{n}")
        sb = lambda n, s: ctx.enter_context(nc.sbuf_tensor(f"ks_{n}", s, F32))
        wk = [sb(f"wk{e}", [P, KT * DK + TAPS]) for e in range(2)]
        kc = [sb(f"kc{e}", [P, TOK]) for e in range(2)]
        gd = [sb(f"gd{e}", [P, TILES, BLK]) for e in range(2)]
        square, ssk = sb("square", [P, TOK]), sb("ssk", [P, NK, TILES])
        loaded = [sem(f"loaded{e}") for e in range(2)]
        kT_stored = [sem(f"kT_stored{e}") for e in range(2)]
        gd_stored = [sem(f"gd_stored{e}") for e in range(2)]
        projected, last_tap, tap, conv_done = sem("projected"), sem("last_tap"), sem("tap"), sem("conv_done")
        square_ready, norms, ssk_ready, grams, gd_ready = sem("square_s"), sem("norms"), sem("ssk_s"), sem("grams"), sem("gd_s")
        root, w_step = sem("root"), sem("w_step")
        inverse = BlockInverse(nc, k, ctx, "k_inv")
        block = ctx.enter_context(nc.Block())
        G = 2
        EARLY = 3

        @block.sync
        def _(sp):
            def head(m, e, h, first=False):
                if not first:
                    sp.wait_ge(conv_done, G * (h - 1))
                sp.dma_start(wk[e][:], k.wk_d[bass.ds(h, 1)].rearrange("o p f -> (o p) f")).then_inc(loaded[e], 16)

            def store(m, e, h):
                sp.wait_ge(conv_done, G * (h + 1))
                sp.dma_start(k.kT_d[bass.ds(h, 1)].rearrange("o p f -> (o p) f"), kc[e][:]).then_inc(kT_stored[e], 16)
                sp.wait_ge(gd_ready, GB * (h + 1))
                sp.dma_start(k.gram_d[bass.ds(h, 1)].rearrange("o (i g) (s t) -> (o g s) i t", g=GB, t=BLK), gd[e][:]).then_inc(gd_stored[e], 16)

            head(0, 0, 0, True)
            head(0, 1, 1, True)
            for e in range(2):
                sp.dma_start(k.wf[e][:], k.wf_d[e]).then_inc(k.wf_loaded[e], 16)
            for e in range(2):
                head(1, e, 2 + e)
                store(0, e, e)
            for e in range(2):
                sp.wait_ge(gd_stored[e], 16)
            inverse.load(sp, 0, 0)
            with sp.Fori(1, NK // 2 - 1) as m:
                for e in range(2):
                    head(m + 1, e, 2 * m + 2 + e)
                    store(m, e, 2 * m + e)
            for e in range(2):
                store(NK // 2 - 1, e, NK - 2 + e)
            inverse.store(sp, 0)
            for e in range(2):
                sp.wait_ge(kT_stored[e], 16 * NK // 2)
                sp.wait_ge(gd_stored[e], 16 * NK // 2)

        @block.tensor
        def _(pe):
            def project(m, e, h):
                pe.wait_ge(loaded[e], 16 * (m + 1))
                for g in range(G):
                    if not is_first(h, 2):
                        pe.wait_ge(conv_done, G * (h - 2) + g + 1)
                    for c in range(KT):
                        last = nc.tensor.matmul(k.ps[:, 2 * e + g, :], wk[e][:, c * DK:(c + 1) * DK], k.xT[:, c, g * BANK:(g + 1) * BANK],
                                                start=c == 0, stop=c == KT - 1)
                    last.then_inc(projected, 1)

            def measure(m, e, h):
                pe.wait_ge(conv_done, G * (h + 1))
                if not is_first(h):
                    pe.wait_ge(gd_ready, GB * h)
                for i in range(TILES):
                    tile = kc[e][:, i * P:(i + 1) * P]
                    last = nc.tensor.matmul(k.ps[:, 4 + i // 4, (i % 4) * P:(i % 4 + 1) * P], tile, tile, start=True, stop=True)
                last.then_inc(grams, 1)
                pe.wait_ge(square_ready, h + 1)
                if not is_first(h, 2):
                    pe.wait_ge(ssk_ready, h - 1)
                for i in range(TILES):
                    last = nc.tensor.matmul(k.ps[:, 6 + e, i:i + 1], square[:, i * P:(i + 1) * P], k.ones[:, 0:1], start=True, stop=True)
                last.then_inc(norms, 1)

            project(0, 0, 0)
            project(0, 1, 1)
            measure(0, 0, 0)
            project(1, 0, 2)
            measure(0, 1, 1)
            project(1, 1, 3)
            measure(1, 0, 2)
            with pe.Fori(2, NK // 2) as m:
                project(m, 0, 2 * m)
                measure(m - 1, 1, 2 * m - 1)
                project(m, 1, 2 * m + 1)
                measure(m, 0, 2 * m)
            measure(NK // 2 - 1, 1, NK - 1)

        @block.scalar
        def _(act):
            def tap(m, e, h, first=False):
                if not first:
                    act.wait_ge(kT_stored[e], 16 * m)
                    act.wait_ge(grams, h - 1)
                    act.wait_ge(square_ready, h - 1)
                for g in range(G):
                    act.wait_ge(projected, G * h + g + 1)
                    nc.scalar.activation(kc[e][:, g * BANK:(g + 1) * BANK], k.ps[:, 2 * e + g, :], ACT.Copy,
                                         scale=wk[e][:, KT * DK + TAPS - 1:KT * DK + TAPS]).then_inc(last_tap, 1)

            def rest(m, e, h):
                act.wait_ge(conv_done, G * (h + 1))
                if not is_first(h):
                    act.wait_ge(norms, h)
                nc.scalar.activation(square[:], kc[e][:], ACT.Square).then_inc(square_ready, 1)
                act.wait_ge(grams, h + 1)
                if not is_first(h, 2):
                    act.wait_ge(gd_stored[e], 16 * m)
                for g in range(GB):
                    rows = slice(g * BLK, (g + 1) * BLK)
                    nc.scalar.copy(gd[e][rows, :, :], k.ps[rows, 4:6, :].rearrange("p a (i t) -> p (a i) t", t=P)[:, :, g * BLK:(g + 1) * BLK]).then_inc(gd_ready, 1)

            tap(0, 0, 0, True)
            tap(0, 1, 1, True)
            rest(0, 0, 0)
            for m in range(1, EARLY):
                tap(m, 0, 2 * m)
                rest(m - 1, 1, 2 * m - 1)
                tap(m, 1, 2 * m + 1)
                rest(m, 0, 2 * m)
            inverse.scalar_exp(act, 0)
            with act.Fori(EARLY, NK // 2) as m:
                tap(m, 0, 2 * m)
                rest(m - 1, 1, 2 * m - 1)
                tap(m, 1, 2 * m + 1)
                rest(m, 0, 2 * m)
            rest(NK // 2 - 1, 1, NK - 1)

        @block.vector
        def _(dve):
            def convolve(m, e, h):
                for g in range(G):
                    dve.wait_ge(last_tap, G * h + g + 1)
                    u = G * h + g

                    def done(n, ins):
                        if n < TAPS - 2:
                            ins.then_inc(tap, 1)
                            dve.wait_ge(tap, (TAPS - 2) * u + n + 1)
                        else:
                            ins.then_inc(conv_done, 1)
                    conv_taps(nc, dve, k.ps[:, 2 * e + g, :], kc[e][:, g * BANK:(g + 1) * BANK], wk[e][:, KT * DK:KT * DK + TAPS], done)

            def keep(m, e, h):
                dve.wait_ge(norms, h + 1)
                nc.vector.tensor_scalar(ssk[:, h, :] if isinstance(h, int) else ssk[:, bass.ds(h, 1), :].rearrange("p o i -> p (o i)"),
                                        k.ps[:, 6 + e, 0:TILES], NORM_EPS2, None, ALU.max).then_inc(ssk_ready, 1)

            def pair(m):
                convolve(m - 1, 1, 2 * m - 1)
                keep(m - 1, 0, 2 * m - 2)
                convolve(m, 0, 2 * m)
                keep(m - 1, 1, 2 * m - 1)

            convolve(0, 0, 0)
            for m in range(1, EARLY):
                pair(m)
            inverse.vector_weights(dve, 0)
            inverse.vector_floor(dve, 0)
            with dve.Fori(EARLY, NK // 2) as m:
                pair(m)
            convolve(NK // 2 - 1, 1, NK - 1)
            inverse.vector_transpose(dve, 0)
            keep(NK // 2 - 1, 0, NK - 2)
            keep(NK // 2 - 1, 1, NK - 1)
            dve.wait_ge(ssk_ready, NK)
            nc.vector.reciprocal(k.rk[:], ssk[:]).then_inc(w_step, 1)
            dve.wait_ge(w_step, 1)
            for v in range(PV):
                nc.vector.tensor_tensor(k.w[:, :, v:NV:PV], k.beta[:, :, v:NV:PV], k.rk[:].rearrange("p h i -> p i h"), ALU.mult).then_inc(w_step, 1)
            dve.wait_ge(w_step, 1 + PV)
            fast_rsqrt(nc, dve, ssk[:].rearrange("p h i -> p (h i)"), k.rk[:].rearrange("p h i -> p (h i)"), k.root_tmp[:, 0:NK * TILES], root, 0)
            nc.vector.tensor_tensor(k.kabs[:], ssk[:], k.rk[:], ALU.mult)

        @block.gpsimd
        def _(pool):
            inverse.invert(pool, 0)


NEWTON = 3
RSQRT_STEPS = 1 + 3 * NEWTON


def fast_rsqrt(nc, dve, x, y, tmp, step, n):
    at = [RSQRT_STEPS * n]

    def then(ins):
        at[0] = at[0] + 1
        ins.then_inc(step, 1)
        dve.wait_ge(step, at[0])
    then(nc.vector.tensor_scalar(y.bitcast(I32), x.bitcast(I32), -0.5, float(0x5F3759DF), ALU.mult, ALU.add))
    for _ in range(NEWTON):
        then(nc.vector.tensor_tensor(tmp, y, y, ALU.mult))
        then(nc.vector.scalar_tensor_tensor(out=tmp, in0=tmp, scalar=-0.5, in1=x, op0=ALU.mult, op1=ALU.mult))
        then(nc.vector.scalar_tensor_tensor(out=y, in0=tmp, scalar=1.5, in1=y, op0=ALU.add, op1=ALU.mult))


def heads(nc, k):
    with ExitStack() as ctx:
        sem = lambda n: k.semaphore(f"hd_{n}")
        sb = lambda n, s: ctx.enter_context(nc.sbuf_tensor(f"hd_{n}", s, F32))
        two = lambda n, s: [sb(f"{n}{e}", s) for e in range(2)]
        two_sems = lambda n: [sem(f"{n}{e}") for e in range(2)]
        EC, E1, EW = 1, 2 + T, 2 + T + P
        wf, wf_loaded = k.wf, k.wf_loaded
        wo, cbc, kT, qT = two("wo", [P, PV, C]), two("cbc", [P, PV, B, T]), two("kT", [P, TOK]), sb("qT", [P, TOK])
        vT, th, sz = sb("vT", [P, PV, TOK]), two("th", [P, BANK]), two("sz", [P, PV, TOK])
        E = [sb(f"E{b}", [P, PV, EW]) for b in range(B)]
        bp0, bp1 = sb("bp0", [P, B, PV, 2, T]), sb("bp1", [P, B, PV, 2, P])
        Z, M = two("Z", [P, UNITS, P]), two("M", [P, UNITS, 2 * BLK])
        t1, square = sb("t1", [P, UNITS, BLK]), sb("square", [P, TOK])
        t2 = square[:].rearrange("p (u k) -> p u k", k=2 * BLK)
        R, U, gT = sb("R", [P, B, 2, PV, P]), sb("U", [P, B, 2, PV, P]), two("gT", [P, PV, 2 * P])
        O = k.xn[:].rearrange("p i (c d) -> p (i c) d", d=P).rearrange("p (b v c) d -> p b v c d", b=B, v=PV)
        osq = U[:].rearrange("p b c v d -> p (b c v) d")
        kabs, kabs_ready = two("kabs", [P, TILES]), sem("kabs_s")
        ssq, ms, inv, tmp, floor, nwh = two("ssq", [P, TILES]), sb("ms", [P, 16]), sb("rms", [P, 16]), sb("tmp", [P, 16]), sb("floor", [P, TILES]), sb("nwh", [P, 1])
        wo_loaded, in_loaded, zm_loaded = two_sems("wo_l"), two_sems("in_l"), two_sems("zm_l")
        cleared, pads, nwh_ready = sem("cleared"), sem("pads"), sem("nwh_s")
        g_ready, q_proj, v_proj, z_proj, v_turned = sem("g"), sem("q_proj"), sem("v_proj"), sem("z_proj"), sem("v_turned")
        t1_ready, l1_ready, t2_ready, l2_ready, u0_ready, x1_ready, u1_ready, o_ready = (sem(n) for n in ("t1_p", "l1_p", "t2_p", "l2_p", "u0_p", "x1_p", "u1_p", "o_p"))
        qn_ready, turned, y_ready = sem("qn"), sem("turned"), sem("y")
        bp_ready, r_ready, q_tap, q_conv, v_tap, v_conv, sz_ready, x1_done, gT_ready, added, arg_ready, q_kept, scaled = (
            sem(n) for n in ("bp", "r", "q_tap", "q_conv", "v_tap", "v_conv", "sz_s", "x1_d", "gT_s", "added", "arg_s", "q_kept", "scaled"))
        e_ready, q_last, v_last, th_ready, t1_out, l1_out, t2_out, l2_out, u0_out, u1_out, q_square, o_out, o_square = (
            sem(n) for n in ("e", "q_last", "v_last", "th_s", "t1_o", "l1_o", "t2_o", "l2_o", "u0_o", "u1_o", "q_square", "o_o", "o_sq"))
        chain, root = sem("chain"), sem("root")
        passed, weights_used = sem("passed"), sem("weights_used")
        inverse = BlockInverse(nc, k, ctx, "h_inv")
        block = ctx.enter_context(nc.Block())
        G = 2
        TAP0 = KT * FRONT * P
        LAST = NK // 2 - 1
        taps_of = lambda e, part: wf[e][:, TAP0 + part * TAPS:TAP0 + (part + 1) * TAPS]

        def after(m, e):
            return (m, 1, 2 * m + 1) if e == 0 else (m + 1, 0, 2 * m + 2)

        def every_head(eng, body):
            body(0, 0, False, True)
            body(0, 1, True, True)
            with eng.Fori(1, LAST) as m:
                body(m, 0, True, True)
                body(m, 1, True, True)
            body(LAST, 0, True, True)
            body(LAST, 1, True, False)

        unit = lambda b, c, v: v * TILES + 2 * b + c
        pick = lambda t, h: t[:, h, :] if isinstance(h, int) else t[:, bass.ds(h, 1), :].rearrange("p o i -> p (o i)")
        col = lambda t, i, h: t[:, i, h:h + 1] if isinstance(h, int) else t[:, i, bass.ds(h, 1)]

        @block.gpsimd
        def _(pool):
            for e in range(2):
                nc.gpsimd.memset(Z[e][:], 0.0).then_inc(cleared, 1)
                nc.gpsimd.memset(M[e][:], 0.0).then_inc(cleared, 1)
            for b in range(B):
                nc.gpsimd.memset(E[b][:], 0.0).then_inc(pads, 1)
            inverse.invert(pool, 0)
            with pool.Fori(1, LAST) as n:
                inverse.invert(pool, n)

        @block.sync
        def _(sp):
            def front_weights(e, h):
                sp.dma_start(wf[e][:], k.wf_d[bass.ds(h, 1)].rearrange("o p f -> (o p) f")).then_inc(wf_loaded[e], 16)

            def inputs(e, h):
                sp.dma_start(cbc[e][:].rearrange("p v b t -> p (v b t)"), k.crow_d[bass.ds(PV * h, PV)].rearrange("v f -> (v f)").unsqueeze(0)
                             .broadcast_to([P, PV * TOK])).then_inc(in_loaded[e], 16)
                sp.dma_start(kT[e][:], k.kT_d[bass.ds(h, 1)].rearrange("o p f -> (o p) f")).then_inc(in_loaded[e], 16)

            def blocks(e):
                for src, dst, n in ((k.invT_d, Z[e], GB), (k.inv_d, M[e], GB - 1)):
                    src = src.rearrange("(e u g) (i k) -> e g i u k", e=2, g=GB, k=BLK)
                    for g in range(n):
                        at = g * BLK if n == GB else (g % 2) * BLK
                        sp.dma_start(dst[g * BLK:(g + 1) * BLK, :, at:at + BLK], src[e, g]).then_inc(zm_loaded[e], 16)

            def body(m, e, prev, nxt):
                h = 2 * m + e
                m1, e1, h1 = after(m, e)
                if nxt and not (m is LAST and e == 0):
                    sp.wait_ge(z_proj, 2 * PV * (h + 1))
                    sp.sem_inc(weights_used, 1)
                    sp.wait_ge(v_conv, PV * G * (h + 1))
                    front_weights(e, h + 2)
                if not is_first(h, 2):
                    sp.wait_ge(y_ready, B * (h - 1))
                sp.dma_start(wo[e][:].rearrange("p v c -> p (v c)"), k.wo_d[bass.ds(h, 1)].rearrange("o p f -> (o p) f")).then_inc(wo_loaded[e], 16)
                if nxt and not is_first(h):
                    sp.wait_ge(g_ready, B * h)
                    sp.wait_ge(arg_ready, B * h)
                if nxt:
                    inputs(e1, h1)
                if nxt and e == 0 and m is not LAST:
                    inverse.load(sp, m + 1, m)
                if nxt and e == 1:
                    for x in range(2):
                        sp.wait_ge(zm_loaded[x], 16 * (2 * GB - 1) * (m + 1))
                    inverse.store(sp, m)
                if nxt and not is_first(h):
                    sp.wait_ge(u1_ready, 2 * h)
                if nxt:
                    blocks(e1)

            inputs(0, 0)
            sp.wait_ge(cleared, 4)
            blocks(0)
            every_head(sp, body)

        @block.tensor
        def _(pe):
            def project(part, e, g, done):
                for c in range(KT):
                    at = (c * FRONT + part) * P
                    last = nc.tensor.matmul(k.ps[:, g, :], wf[e][:, at:at + P], k.xT[:, c, g * BANK:(g + 1) * BANK], start=c == 0, stop=c == KT - 1)
                last.then_inc(done, 1)

            def project_q(m, e, h, halves=range(2), first=False):
                pe.wait_ge(wf_loaded[e], 16 * (m + 1))
                for g in halves:
                    if not first:
                        pe.wait_ge(sz_ready, 4 * h - 2 + g + 1)
                    project(0, e, g, q_proj)

            def project_v(v, e, h, halves=range(2)):
                for g in halves:
                    if v == 0:
                        pe.wait_ge(q_conv, G * h + g + 1)
                    else:
                        pe.wait_ge(v_conv, 4 * h + g + 1)
                    project(1 + v, e, g, v_proj)

            def project_z(v, e, h, halves=range(2)):
                for g in halves:
                    if v == 0:
                        pe.wait_ge(v_conv, 4 * h + 2 + g + 1)
                    else:
                        pe.wait_ge(sz_ready, 4 * h + g + 1)
                    project(1 + PV + v, e, g, z_proj)

            def norms_q(e, h, first=False):
                pe.wait_ge(q_square, h + 1)
                for i in range(TILES):
                    last = nc.tensor.matmul(k.ps[:, 6, i:i + 1], square[:, i * P:(i + 1) * P], k.ones[:, 0:1], start=True, stop=True)
                last.then_inc(qn_ready, 1)

            def grams(m, e, h, b):
                if b == 0:
                    pe.wait_ge(in_loaded[e], 32 * (m + 1))
                    pe.wait_ge(q_conv, G * (h + 1))
                if b >= 2:
                    pe.wait_ge(bp_ready, B * h + b - 1)
                elif not is_first(h):
                    pe.wait_ge(o_out, B * h - 2 + 2 * b)
                bank = 2 + 2 * (b % 2)
                first, seq, second = slice(b * T, b * T + P), slice(b * T, (b + 1) * T), slice(b * T + P, (b + 1) * T)
                for n, src in enumerate((kT[e], qT)):
                    nc.tensor.matmul(k.ps[:, bank, n * T:(n + 1) * T], kT[e][:, first], src[:, seq], start=True, stop=True)
                    last = nc.tensor.matmul(k.ps[:, bank + 1, n * P:(n + 1) * P], kT[e][:, second], src[:, second], start=True, stop=True)
                last.then_inc(g_ready, 1)

            def turn_v(h, b):
                if b == 0:
                    pe.wait_ge(v_conv, 4 * (h + 1))
                    pe.wait_ge(q_kept, h + 1)
                elif b == 1:
                    if not is_first(h):
                        pe.wait_ge(l2_out, 2 * h)
                    if not is_first(h, 2):
                        pe.wait_ge(added, B * (h - 1))
                else:
                    pe.wait_ge(r_ready, B * h + b - 1)
                for c in range(2):
                    for v in range(PV):
                        at = (c * PV + v) * P
                        tokens = b * T + c * P
                        last = nc.tensor.transpose(k.ps[:, 6 + b % 2, at:at + P], vT[:, v, tokens:tokens + P], k.ident[:])
                last.then_inc(v_turned, 1)

            def turn(h, q, bank_free):
                pe.wait_ge(*bank_free)
                pe.wait_ge(scaled, B * h + q + 1)
                for v in range(PV):
                    for c in range(2):
                        at = (v * 2 + c) * P
                        last = nc.tensor.transpose(k.ps[:, 6, at:at + P], O[:, q, v, c, :], k.ident[:])
                last.then_inc(turned, 1)

            def output(e, m, h, q, bank_free):
                pe.wait_ge(*bank_free)
                pe.wait_ge(gT_ready, B * h + q + 1)
                if q == 0:
                    pe.wait_ge(wo_loaded[e], 16 * (m + 1))
                for c in range(2):
                    for v in range(PV):
                        last = nc.tensor.matmul(k.ps[:, 7, c * C:(c + 1) * C], gT[q % 2][:, v, c * P:(c + 1) * P], wo[e][:, v, :], start=v == 0, stop=v == PV - 1)
                last.then_inc(y_ready, 1)

            def turn_outputs(h, q, bank_free=None):
                turn(h, q, bank_free or (gT_ready, B * h + q))

            def project_outputs(m, e, h, q, bank_free=None):
                output(e, m, h, q, bank_free or (added, B * h + q))

            def body(m, e, prev, nxt):
                h = 2 * m + e
                m1, e1, h1 = after(m, e)
                before = (m if e else m - 1, 1 - e, h - 1)
                grams(m, e, h, 0)
                grams(m, e, h, 1)
                turn_v(h, 0)
                turn_v(h, 1)
                if nxt:
                    project_q(m1, e1, h1, (0,))
                turn_v(h, 2)
                turn_v(h, 3)
                grams(m, e, h, 2)
                grams(m, e, h, 3)
                if nxt:
                    project_q(m1, e1, h1, (1,))
                pe.wait_ge(zm_loaded[e], 16 * (2 * GB - 1) * (m + 1))
                chunk = lambda b, c, v: (bp0[:, b, v, 0, 0:P], bp1[:, b, v, 0, :])[c]
                every = [(b, c, v) for b in range(B) for c in range(2) for v in range(PV)]
                for some in (every[:-2 * PV], every[-2 * PV:]):
                    pe.wait_ge(bp_ready, B * h + some[-1][0] + 1)
                    pe.sem_inc(passed, 1)
                    for g, (b, c, v) in [(g, one) for g in (0, 2) for one in some]:
                        at, to = slice(g * BLK, (g + 1) * BLK), slice((g + 1) * BLK, (g + 2) * BLK)
                        u = unit(b, c, v)
                        m_at = slice(0, BLK)
                        last = nc.tensor.matmul(k.ps[to, 2, u * BLK:(u + 1) * BLK], chunk(b, c, v)[at, to], M[e][at, u, m_at], start=True, stop=True)
                last.then_inc(t1_ready, 1)
                for g in (0, 2):
                    pe.wait_ge(t1_out, 2 * h + g // 2 + 1)
                    pe.sem_inc(passed, 1)
                    at, to = slice(g * BLK, (g + 1) * BLK), slice((g + 1) * BLK, (g + 2) * BLK)
                    for b, c, v in every:
                        u = unit(b, c, v)
                        last = nc.tensor.matmul(k.ps[at, 3, u * BLK:(u + 1) * BLK], t1[to, u, :], Z[e][to, u, to], start=True, stop=True)
                        if g == 0:
                            last = nc.tensor.matmul(k.ps[to, 3, u * BLK:(u + 1) * BLK], Z[e][to, u, to], t1[to, u, :], start=True, stop=True)
                    last.then_inc(l1_ready, 1)
                pe.wait_ge(l1_out, 3 * h + 1)
                pe.sem_inc(passed, 1)
                HALF = 2 * BLK
                for a in range(2):
                    for b, c, v in every:
                        u = unit(b, c, v)
                        if u // TILES == a:
                            last = nc.tensor.matmul(k.ps[HALF:P, 4 + a, (u % TILES) * HALF:(u % TILES + 1) * HALF], chunk(b, c, v)[0:HALF, HALF:P], M[e][0:HALF, u, :],
                                                    start=True, stop=True)
                    last.then_inc(t2_ready, 1)
                pe.wait_ge(r_ready, B * (h + 1))
                pe.wait_ge(l1_out, 3 * (h + 1))
                for a in range(2):
                    pe.wait_ge(t2_out, 2 * h + a + 1)
                    pe.sem_inc(passed, 1)
                    for i in range(TILES):
                        u = a * TILES + i
                        last = nc.tensor.matmul(k.ps[0:HALF, 6 + a, i * HALF:(i + 1) * HALF], t2[HALF:P, u, :], Z[e][HALF:P, u, HALF:P], start=True, stop=True)
                    last.then_inc(l2_ready, 1)
                for v in range(PV):
                    pe.wait_ge(l2_out, 2 * h + v + 1)
                    for b in range(B):
                        at = ((b % 2) * PV + v) * P
                        last = nc.tensor.matmul(k.ps[:, 2 + b // 2, at:at + P], Z[e][:, unit(b, 0, v), :], R[:, b, 0, v, :], start=True, stop=True)
                        if v == PV - 1 and b % 2:
                            last.then_inc(u0_ready, 1)
                if prev:
                    turn_outputs(h - 1, 0, (l2_out, 2 * (h + 1)))
                if nxt:
                    project_v(0, e1, h1, (0,))
                for a in range(2):
                    pe.wait_ge(u0_out, 2 * h + a + 1)
                    for b in (2 * a, 2 * a + 1):
                        for v in range(PV):
                            at = ((b % 2) * PV + v) * P
                            last = nc.tensor.matmul(k.ps[:, 4 + a, at:at + P], bp0[:, b, v, 0, P:T], U[:, b, 0, v, :], start=True, stop=True)
                    last.then_inc(x1_ready, 1)
                if nxt:
                    project_v(0, e1, h1, (1,))
                if prev:
                    turn_outputs(h - 1, 1)
                    project_outputs(*before, 0, (l2_out, 2 * (h + 1)))
                for a in range(2):
                    pe.wait_ge(x1_done, 2 * h + a + 1)
                    for b in (2 * a, 2 * a + 1):
                        for v in range(PV):
                            at = ((b % 2) * PV + v) * P
                            last = nc.tensor.matmul(k.ps[:, 2 + a, at:at + P], Z[e][:, unit(b, 1, v), :], R[:, b, 1, v, :], start=True, stop=True)
                    last.then_inc(u1_ready, 1)
                if nxt:
                    project_v(1, e1, h1)
                if prev:
                    turn_outputs(h - 1, 2)
                    project_outputs(*before, 1)
                for b in range(B):
                    pe.wait_ge(u1_out, 2 * h + (1 if b == 0 else 2))
                    for v in range(PV):
                        at = v * 2 * P
                        nc.tensor.matmul(k.ps[:, 2 + b, at:at + P], bp0[:, b, v, 1, 0:P], U[:, b, 0, v, :], start=True, stop=True)
                        nc.tensor.matmul(k.ps[:, 2 + b, at + P:at + 2 * P], bp0[:, b, v, 1, P:T], U[:, b, 0, v, :], start=True, stop=False)
                        last = nc.tensor.matmul(k.ps[:, 2 + b, at + P:at + 2 * P], bp1[:, b, v, 1, :], U[:, b, 1, v, :], start=False, stop=True)
                    last.then_inc(o_ready, 1)
                if prev:
                    turn_outputs(h - 1, 3)
                if nxt:
                    project_z(0, e1, h1)
                if prev:
                    project_outputs(*before, 2)
                if nxt:
                    project_z(1, e1, h1)
                if prev:
                    project_outputs(*before, 3)
                if nxt:
                    if prev:
                        pe.wait_ge(gT_ready, B * h)
                    norms_q(e1, h1)

            project_q(0, 0, 0, first=True)
            project_v(0, 0, 0)
            project_v(1, 0, 0)
            project_z(0, 0, 0)
            project_z(1, 0, 0)
            norms_q(0, 0)
            every_head(pe, body)
            for q in range(B + 1):
                if q < B:
                    turn_outputs(NK - 1, q, None if q else (l2_out, 2 * NK))
                if q:
                    project_outputs(LAST, 1, NK - 1, q - 1, None if q > 1 else (l2_out, 2 * NK))

        @block.scalar
        def _(act):
            def decay(h, b):
                act.wait_ge(arg_ready, B * h + b + 1)
                nc.scalar.activation(E[b][:, :, EC:EC + T], E[b][:, :, EC:EC + T], ACT.Exp)
                nc.scalar.activation(E[b][:, :, E1:E1 + P], E[b][:, :, E1:E1 + P], ACT.Exp).then_inc(e_ready, 1)

            def last_tap_q(m, e, h):
                if not is_first(h):
                    act.wait_ge(g_ready, B * h)
                    act.wait_ge(q_square, h)
                act.wait_ge(wf_loaded[e], 16 * (m + 1))
                for g in range(G):
                    act.wait_ge(q_proj, G * h + g + 1)
                    nc.scalar.activation(qT[:, g * BANK:(g + 1) * BANK], k.ps[:, g, :], ACT.Copy,
                                         scale=taps_of(e, 0)[:, TAPS - 1:TAPS]).then_inc(q_last, 1)

            def last_tap_v(v, e, h):
                if v == 0 and not is_first(h):
                    act.wait_ge(v_turned, B * h)
                for g in range(G):
                    act.wait_ge(v_proj, 4 * h + 2 * v + g + 1)
                    nc.scalar.activation(vT[:, v, g * BANK:(g + 1) * BANK], k.ps[:, g, :], ACT.Copy,
                                         scale=taps_of(e, 1 + v)[:, TAPS - 1:TAPS]).then_inc(v_last, 1)

            def tanh_z(v, h, halves=range(2)):
                for g in halves:
                    z = 4 * h + 2 * v + g
                    act.wait_ge(z_proj, z + 1)
                    if not is_first(z, 2):
                        act.wait_ge(sz_ready, z - 1)
                    nc.scalar.activation(th[g][:], k.ps[:, g, :], ACT.Tanh, scale=0.5).then_inc(th_ready, 1)

            def square_q(e, h):
                act.wait_ge(q_conv, G * (h + 1))
                if not is_first(h):
                    act.wait_ge(qn_ready, h)
                nc.scalar.activation(square[:], qT[:], ACT.Square).then_inc(q_square, 1)

            def minus(out, src, done):
                nc.scalar.activation(out, src, ACT.Copy, scale=-1.0).then_inc(done, 1)

            def square_o(h):
                act.wait_ge(o_out, B * (h + 1))
                if not is_first(h):
                    act.wait_ge(scaled, B * h)
                nc.scalar.activation(osq.rearrange("p u d -> p (u d)"), k.xn[:].rearrange("p i c -> p (i c)"), ACT.Square).then_inc(o_square, 1)

            def scale_v(e, h, b):
                act.wait_ge(v_turned, B * h + b + 1)
                if b == 0:
                    act.wait_ge(kabs_ready, h + 1)
                    if not is_first(h):
                        act.wait_ge(x1_done, 2 * h)
                for c in range(2):
                    last = nc.scalar.activation(R[:, b, c].rearrange("p v d -> p (v d)"), k.ps[:, 6 + b % 2, c * PV * P:(c + 1) * PV * P], ACT.Copy,
                                                scale=kabs[e][:, 2 * b + c:2 * b + c + 1])
                last.then_inc(r_ready, 1)

            def body(m, e, prev, nxt):
                h = 2 * m + e
                m1, e1, h1 = after(m, e)
                for b in range(B):
                    scale_v(e, h, b)
                if nxt:
                    last_tap_q(m1, e1, h1)
                act.wait_ge(t1_ready, h + 1)
                for g in (1, 3):
                    rows = slice(g * BLK, (g + 1) * BLK)
                    nc.scalar.copy(t1[rows].rearrange("p u k -> p (u k)"), k.ps[rows, 2, :]).then_inc(t1_out, 1)
                if nxt and e == 0 and m is not LAST:
                    inverse.scalar_exp(act, m)
                act.wait_ge(l1_ready, 2 * h + 1)
                lvl1 = lambda g: k.ps[g * BLK:(g + 1) * BLK, 3, :].rearrange("p (u k) -> p u k", k=BLK)
                minus(M[e][BLK:2 * BLK, :, 0:BLK], lvl1(1), l1_out)
                minus(Z[e][0:BLK, :, BLK:2 * BLK], lvl1(0), l1_out)
                act.wait_ge(l1_ready, 2 * h + 2)
                minus(Z[e][2 * BLK:3 * BLK, :, 3 * BLK:P], lvl1(2), l1_out)
                act.wait_ge(qn_ready, h + 1)
                for a in range(2):
                    act.wait_ge(t2_ready, 2 * h + a + 1)
                    nc.scalar.copy(t2[2 * BLK:P, a * TILES:(a + 1) * TILES, :], k.ps[2 * BLK:P, 4 + a, :].rearrange("p (u k) -> p u k", k=2 * BLK)).then_inc(t2_out, 1)
                for a in range(2):
                    act.wait_ge(l2_ready, 2 * h + a + 1)
                    minus(Z[e][0:2 * BLK, a * TILES:(a + 1) * TILES, 2 * BLK:P], k.ps[0:2 * BLK, 6 + a, :].rearrange("p (u k) -> p u k", k=2 * BLK), l2_out)
                if prev:
                    act.wait_ge(scaled, B * h)
                for c, ready, out in ((0, u0_ready, u0_out), (1, u1_ready, u1_out)):
                    for a in range(2):
                        act.wait_ge(ready, 2 * h + a + 1)
                        nc.scalar.copy(U[:, 2 * a:2 * a + 2, c], k.ps[:, 2 + a, :].rearrange("p (b v d) -> p b v d", b=2, v=PV)).then_inc(out, 1)
                    if nxt:
                        last_tap_v(c, e1, h1)
                if nxt:
                    decay(h1, 0)
                    decay(h1, 1)
                for b in range(B):
                    act.wait_ge(o_ready, B * h + b + 1)
                    if prev:
                        act.wait_ge(turned, B * (h - 1) + b + 1)
                    nc.scalar.copy(O[:, b].rearrange("p v c d -> p (v c d)"), k.ps[:, 2 + b, :]).then_inc(o_out, 1)
                if nxt:
                    tanh_z(0, h1)
                square_o(h)
                if nxt:
                    square_q(e1, h1)
                    tanh_z(1, h1)
                    decay(h1, 2)
                    decay(h1, 3)

            act.wait_ge(pads, B)
            last_tap_q(0, 0, 0)
            last_tap_v(0, 0, 0)
            last_tap_v(1, 0, 0)
            tanh_z(0, 0)
            tanh_z(1, 0)
            square_q(0, 0)
            for b in range(B):
                decay(0, b)
            every_head(act, body)

        @block.vector
        def _(dve):
            def exponent(m, e, h, b):
                if b == 0:
                    dve.wait_ge(in_loaded[e], 32 * (m + 1))
                if not is_first(h):
                    dve.wait_ge(bp_ready, B * (h - 1) + b + 1)
                for v in range(PV):
                    nc.vector.scalar_tensor_tensor(out=E[b][:, v, EC:EC + T], in0=cbc[e][:, v, b, :], scalar=col(k.ccol, 2 * b, PV * h + v),
                                                   in1=k.bound[:], op0=ALU.subtract, op1=ALU.min)
                    last = nc.vector.scalar_tensor_tensor(out=E[b][:, v, E1:E1 + P], in0=cbc[e][:, v, b, P:T], scalar=col(k.ccol, 2 * b + 1, PV * h + v),
                                                          in1=k.bound[:, 0:P], op0=ALU.subtract, op1=ALU.min)
                last.then_inc(arg_ready, 1)

            def weigh(e, h, b):
                dve.wait_ge(e_ready, B * h + b + 1)
                dve.wait_ge(g_ready, B * h + b + 1)
                if not is_first(h):
                    dve.wait_ge(o_ready, B * (h - 1) + b + 1)
                bank = 2 + 2 * (b % 2)
                for v in range(PV):
                    for c, out, at, n in ((0, bp0, EC, T), (1, bp1, E1, P)):
                        decays_of = E[b][:, v, at - 1:at + n]
                        two_steps = bass.AP(tensor=decays_of.tensor, offset=decays_of.offset, ap=[list(decays_of.ap[0]), [1, 2], [1, n]])
                        last = nc.vector.scalar_tensor_tensor(out=out[:, b, v], in0=k.ps[:, bank + c, 0:2 * n].rearrange("p (n t) -> p n t", n=2),
                                                              scalar=col(k.w, 2 * b + c, PV * h + v), in1=two_steps, op0=ALU.mult, op1=ALU.mult)
                last.then_inc(bp_ready, 1)

            def convolve(part, e, h, last_tap, tap, conv, of_head):
                out = qT[:] if part == 0 else vT[:, part - 1, :]
                for g in range(G):
                    u = of_head * h + max(part - 1, 0) * G + g
                    dve.wait_ge(last_tap, u + 1)

                    def done(n, ins):
                        if n < TAPS - 2:
                            ins.then_inc(tap, 1)
                            dve.wait_ge(tap, (TAPS - 2) * u + n + 1)
                        else:
                            ins.then_inc(conv, 1)
                    conv_taps(nc, dve, k.ps[:, g, :], out[:, g * BANK:(g + 1) * BANK], taps_of(e, part), done)

            def convolve_q(e, h):
                convolve(0, e, h, q_last, q_tap, q_conv, G)

            def convolve_v(v, e, h):
                convolve(1 + v, e, h, v_last, v_tap, v_conv, PV * G)

            def gate(v, e, h, halves=range(2)):
                if v == 0 and not is_first(h, 2):
                    dve.wait_ge(gT_ready, B * (h - 1))
                for g in halves:
                    dve.wait_ge(th_ready, 4 * h + 2 * v + g + 1)
                    nc.vector.scalar_tensor_tensor(out=sz[e][:, v, g * BANK:(g + 1) * BANK], in0=th[g][:], scalar=1.0, in1=k.ps[:, g, :],
                                                   op0=ALU.add, op1=ALU.mult).then_inc(sz_ready, 1)

            def keep_kabs(e, h):
                nc.vector.tensor_copy(kabs[e][:], pick(k.kabs, h)).then_inc(kabs_ready, 1)

            def keep_q(e, h):
                dve.wait_ge(qn_ready, h + 1)
                nc.vector.tensor_scalar(ssq[e][:], k.ps[:, 6, 0:TILES], NORM_EPS2, None, ALU.max).then_inc(q_kept, 1)

            def normalise(e, h):
                CH = 2
                dve.wait_ge(o_square, h + 1)
                dve.wait_ge(q_kept, h + 1)
                nc.vector.tensor_reduce(ms[:], osq, AX.X, ALU.add).then_inc(chain, 1)
                nc.vector.tensor_scalar(floor[:], ssq[e][:], RMS_EPS, None, ALU.mult).then_inc(chain, 1)
                dve.wait_ge(chain, 4 * h + CH)
                nc.vector.scalar_tensor_tensor(out=ms[:].rearrange("p (b v c) -> p b v c", v=PV, c=2)[:, :, 0], in0=ms[:].rearrange("p (b v c) -> p b v c", v=PV, c=2)[:, :, 0],
                                               scalar=1.0 / DV, in1=floor[:].rearrange("p (b c) -> p b c", c=2), op0=ALU.mult, op1=ALU.add).then_inc(chain, 1)
                nc.vector.scalar_tensor_tensor(out=ms[:].rearrange("p (b v c) -> p b v c", v=PV, c=2)[:, :, 1], in0=ms[:].rearrange("p (b v c) -> p b v c", v=PV, c=2)[:, :, 1],
                                               scalar=1.0 / DV, in1=floor[:].rearrange("p (b c) -> p b c", c=2), op0=ALU.mult, op1=ALU.add).then_inc(chain, 1)
                dve.wait_ge(chain, 4 * h + CH + 2)
                fast_rsqrt(nc, dve, ms[:], inv[:], tmp[:], root, h)
                for q in range(B):
                    nc.vector.tensor_tensor(O[:, q].rearrange("p v c d -> p (v c) d"), O[:, q].rearrange("p v c d -> p (v c) d"),
                                            inv[:, 4 * q:4 * q + 4].unsqueeze(2).broadcast_to([P, 4, P]), ALU.mult).then_inc(scaled, 1)

            def gate_outputs(e, h, q):
                dve.wait_ge(turned, B * h + q + 1)
                if not (is_first(h) and q < 2):
                    dve.wait_ge(y_ready, B * h + q - 1)
                nc.vector.scalar_tensor_tensor(out=gT[q % 2][:], in0=k.ps[:, 6, :].rearrange("p (v t) -> p v t", v=PV), scalar=nwh[:, 0:1],
                                               in1=sz[e][:, :, q * T:(q + 1) * T], op0=ALU.mult, op1=ALU.mult).then_inc(gT_ready, 1)

            def add_outputs(h, q):
                dve.wait_ge(y_ready, B * h + q + 1)
                if not is_first(h):
                    dve.wait_ge(added, B * (h - 1) + q + 1)
                nc.vector.tensor_tensor(k.x[:, 2 * q:2 * q + 2, :], k.ps[:, 7, :].rearrange("p (i c) -> p i c", i=2), k.x[:, 2 * q:2 * q + 2, :],
                                        ALU.add).then_inc(added, 1)

            def body(m, e, prev, nxt):
                h = 2 * m + e
                m1, e1, h1 = after(m, e)
                weigh(e, h, 0)
                weigh(e, h, 1)
                weigh(e, h, 2)
                weigh(e, h, 3)
                if nxt and e == 0 and m is not LAST:
                    inverse.vector_weights(dve, m)
                    inverse.vector_floor(dve, m)
                if prev:
                    normalise(1 - e, h - 1)
                if nxt:
                    convolve_q(e1, h1)
                    for b in range(B):
                        exponent(m1, e1, h1, b)
                    keep_kabs(e1, h1)
                if prev:
                    gate_outputs(1 - e, h - 1, 0)
                dve.wait_ge(r_ready, B * (h + 1))
                for a in range(2):
                    dve.wait_ge(x1_ready, 2 * h + a + 1)
                    nc.vector.tensor_tensor(R[:, 2 * a:2 * a + 2, 1], R[:, 2 * a:2 * a + 2, 1], k.ps[:, 4 + a, :].rearrange("p (b v d) -> p b v d", b=2, v=PV),
                                            ALU.subtract).then_inc(x1_done, 1)
                if prev:
                    gate_outputs(1 - e, h - 1, 1)
                if nxt and e == 1:
                    inverse.vector_transpose(dve, m)
                for v in range(PV):
                    if nxt:
                        convolve_v(v, e1, h1)
                    if prev:
                        add_outputs(h - 1, v)
                        gate_outputs(1 - e, h - 1, 2 + v)
                if nxt:
                    gate(0, e1, h1)
                if prev:
                    add_outputs(h - 1, 2)
                if nxt:
                    gate(1, e1, h1)
                if prev:
                    add_outputs(h - 1, 3)
                if nxt:
                    keep_q(e1, h1)

            dve.wait_ge(k.nw_loaded, 16)
            nc.vector.tensor_scalar(nwh[:], k.nw[:], 0.5, None, ALU.mult).then_inc(nwh_ready, 1)
            dve.wait_ge(nwh_ready, 1)
            dve.wait_ge(pads, B)
            convolve_q(0, 0)
            for v in range(PV):
                convolve_v(v, 0, 0)
            gate(0, 0, 0)
            gate(1, 0, 0)
            keep_q(0, 0)
            for b in range(B):
                exponent(0, 0, 0, b)
            keep_kabs(0, 0)
            every_head(dve, body)
            normalise(1, NK - 1)
            for q in range(B + 1):
                if q < B:
                    gate_outputs(1, NK - 1, q)
                if q:
                    add_outputs(NK - 1, q - 1)




def constants(nc, k, pool):
    nc.gpsimd.memset(k.neghalf[:], -0.5).then_inc(k.const_ready, 1)
    nc.gpsimd.memset(k.ident[:], 0.0).then_inc(k.ident_ready, 1)
    pool.wait_ge(k.ident_ready, 1)
    nc.gpsimd.affine_select(out=k.ident[:], in_=k.ident[:], compare_op=ALU.not_equal, fill=1.0, base=0, pattern=[[-1, P]],
                            channel_multiplier=1).then_inc(k.ident_ready, 1)
    nc.gpsimd.memset(k.ones[:], 1.0).then_inc(k.const_ready, 1)
    nc.gpsimd.memset(k.bound[:], 0.0).then_inc(k.const_ready, 1)
    pool.wait_ge(k.const_ready, 3)
    nc.gpsimd.affine_select(out=k.upto[:], in_=k.ones[:], compare_op=ALU.is_ge, fill=0.0, base=0, pattern=[[1, P]], channel_multiplier=-1)
    nc.gpsimd.affine_select(out=k.bound[:], in_=k.bound[:], compare_op=ALU.is_ge, fill=NEG, base=0, pattern=[[1, C]], channel_multiplier=-1)


def build(nc, d, out):
    tokens = lambda a: a.rearrange("(i p) c -> p i c", p=P)
    with ExitStack() as whole:
        k = Names()
        sb = lambda n, s: whole.enter_context(nc.sbuf_tensor(n, s, F32))
        sem = lambda n: whole.enter_context(nc.semaphore(n))

        def semaphore(name):
            k.taken.append(nc.alloc_semaphore(name))
            return k.taken[-1]

        k.taken, k.semaphore = [], semaphore
        scratch = lambda n, s: nc.dram_tensor(n, s, F32, kind="Internal").ap()
        k.x, k.xn, k.xT, k.ident, k.neghalf = sb("x", [P, TILES, C]), sb("xn", [P, TILES, C]), sb("xT", [P, KT, TOK]), sb("ident", [P, P]), sb("neghalf", [P, TILES])
        k.ps = whole.enter_context(nc.psum_tensor("ps", [P, 8, BANK], F32))
        k.x_loaded, k.ident_ready, k.const_ready = sem("x_loaded"), sem("ident_ready"), sem("const_ready")

        def load(eng, dst, src, loaded):
            eng.dma_start(dst, src).then_inc(loaded, 16)

        with ExitStack() as layer:
            sb = lambda n, s: layer.enter_context(nc.sbuf_tensor(n, s, F32))
            k.ones, k.upto, k.bound = sb("ones", [P, P]), sb("upto", [P, P]), sb("bound", [P, C])
            k.wba, k.alog, k.dtb, k.nw = sb("wba", [P, KT, 2 * NV]), sb("alog", [P, NV]), sb("dtb", [P, NV]), sb("nw", [P, 1])
            k.ccol, k.beta, k.w = sb("ccol", [P, TILES, NV]), sb("beta", [P, TILES, NV]), sb("w", [P, TILES, NV])
            k.rk, k.kabs, k.root_tmp = sb("rk", [P, NK, TILES]), sb("kabs", [P, NK, TILES]), sb("root_tmp", [P, NK * TILES])
            k.wba_loaded, k.alog_loaded, k.dtb_loaded, k.nw_loaded = sem("wba_loaded"), sem("alog_loaded"), sem("dtb_loaded"), sem("nw_loaded")
            k.crow_d, k.brow_d = scratch("crow_d", (NV, TOK)), scratch("brow_d", (NV, TOK))
            k.kT_d, k.gram_d = scratch("kT_d", (NK, DK, TOK)), scratch("gram_d", (NK, BLK, TOK))
            k.inv_d, k.invT_d = scratch("inv_d", (P, BLK * BLK)), scratch("invT_d", (P, BLK * BLK))
            k.wf = [sb(f"wf{e}", [P, KT * FRONT * P + (1 + PV) * TAPS]) for e in range(2)]
            k.wf_loaded = [sem(f"wf_loaded{e}") for e in range(2)]
            k.wk_d, k.wf_d, k.wo_d = d["wk"], d["wf"], d["wo"]

            with nc.Block() as block:
                @block.sync
                def _(sp):
                    load(sp, k.x[:], tokens(d["x"]), k.x_loaded)
                    load(sp, k.wba[:], d["wba"].rearrange("k p e -> p k e"), k.wba_loaded)
                    load(sp, k.alog[:], d["alog"].broadcast_to([P, NV]), k.alog_loaded)
                    load(sp, k.dtb[:], d["dtb"].broadcast_to([P, NV]), k.dtb_loaded)
                    load(sp, k.nw[:], d["nw"], k.nw_loaded)

                @block.gpsimd
                def _(pool):
                    constants(nc, k, pool)

            layernorm(nc, k, "ln0")
            decays(nc, k)
            keys(nc, k)
            heads(nc, k)
        nc.clear_and_free_semaphores(k.taken)
        nc.all_engine_barrier()

        sb = lambda n, s: whole.enter_context(nc.sbuf_tensor(n, s, F32))
        k.ctx, k.ctxT, k.diag = sb("ctx", [P, TILES, C]), sb("ctxT", [P, TILES, T]), sb("diag", [P, P])
        k.router, k.rscale, k.escale = sb("router", [P, KT, E0]), sb("rscale", [P, KT]), sb("escale", [P, E0])
        k.lower, k.mix = sb("lower", [P, E0 * E0]), sb("mix", [P, TILES, E0])
        k.wqkv, k.wo, k.rope, k.temp, k.wmask = sb("wqkv", [P, KT, 384]), sb("wo", [P, KT, C]), sb("rope", [P, 2, 3, 8]), sb("temp", [P, H1]), sb("wmask", [P, 160])
        (k.ctx_loaded, k.ctxT_loaded, k.diag_loaded, k.router_loaded, k.rscale_loaded, k.escale_loaded, k.lower_loaded, k.gate_loaded, k.linear_loaded,
         k.wqkv_loaded, k.wo_loaded, k.rope_loaded, k.temp_loaded, k.wmask_loaded, k.rw1_loaded, k.rb1_loaded, k.we1_loaded, k.be1_loaded) = (
            sem(n + "_loaded") for n in ("ctx", "ctxT", "diag", "router", "rscale", "escale", "lower", "gate", "linear",
                                         "wqkv", "wo1", "rope", "temp", "wmask", "rw1", "rb1", "we1", "be1"))
        k.shift_done, stored = sem("shift_done"), sem("stored")
        k.rw1, k.rb1 = sb("rw1", [P, KT, E1, C]), sb("rb1", [P, 2, E1])
        k.we1, k.be1 = sb("we1", [P, KT, E1, C]), sb("be1", [E1, C])

        with ExitStack() as layer:
            sb = lambda n, s: layer.enter_context(nc.sbuf_tensor(n, s, F32))
            k.gate, k.linear = sb("gate", [P, KT, E0, 2 * H0]), sb("linear", [P, KT, E0, C])

            def later_weights(sp):
                load(sp, k.ctx[:], tokens(d["ctx"]), k.ctx_loaded)
                load(sp, k.ctxT[:], tokens(d["ctxT"]), k.ctxT_loaded)
                load(sp, k.router[:], d["router"].rearrange("k p e -> p k e"), k.router_loaded)
                load(sp, k.rscale[:], d["rscale"], k.rscale_loaded)
                load(sp, k.escale[:], d["escale"].broadcast_to([P, E0]), k.escale_loaded)
                load(sp, k.lower[:], d["lower"].broadcast_to([P, E0 * E0]), k.lower_loaded)
                load(sp, k.gate[:], d["gate"].rearrange("k p e h -> p k e h"), k.gate_loaded)
                load(sp, k.linear[:], d["linear"].rearrange("k p e h -> p k e h"), k.linear_loaded)
                load(sp, k.wqkv[:], d["wqkv"].rearrange("k p e -> p k e"), k.wqkv_loaded)
                load(sp, k.rope[:], d["rope"].rearrange("h p a b -> p h a b"), k.rope_loaded)
                load(sp, k.temp[:], d["temp"].broadcast_to([P, H1]), k.temp_loaded)
                load(sp, k.wmask[:], d["wmask"], k.wmask_loaded)
                load(sp, k.wo[:], d["wo1"].rearrange("k p e -> p k e"), k.wo_loaded)
                load(sp, k.diag[:], d["diag"], k.diag_loaded)
                load(sp, k.rw1[:], d["rw1"].rearrange("k p e o -> p k e o"), k.rw1_loaded)
                load(sp, k.rb1[:], d["rb1"].rearrange("k p e -> p k e"), k.rb1_loaded)
                load(sp, k.we1[:], d["we1"].rearrange("k p e o -> p k e o"), k.we1_loaded)
                load(sp, k.be1[:], d["be1"], k.be1_loaded)

            layernorm(nc, k, "ln1", False, later_weights)
            cross_attention_0(nc, k)
            layernorm(nc, k, "ln2")
            moe_router_0(nc, k)
            moe_experts_0(nc, k)

        with ExitStack() as layer:
            sb = lambda n, s: layer.enter_context(nc.sbuf_tensor(n, s, F32))
            k.qT, k.kT, k.v, k.vprev = sb("qT", [P, GROUP, TOK]), sb("kT", [P, TOK]), sb("v", [P, TILES, 64]), sb("vprev", [WINDOW, B, 64])
            layernorm(nc, k, "ln3")
            windowed_qkv(nc, k)
            windowed_attention(nc, k)

        layernorm(nc, k, "ln4", False)
        cross_attention_1(nc, k)

        sb = lambda n, s: whole.enter_context(nc.sbuf_tensor(n, s, F32))
        k.share, k.shareT = sb("share", [P, TILES, E1]), sb("shareT", [E1, TOK])
        layernorm(nc, k, "ln5")
        soft_experts_1(nc, k)

        with nc.Block() as block:
            @block.sync
            def _(sp):
                sp.dma_start(tokens(out), k.x[:]).then_inc(stored, 16)
                sp.wait_ge(stored, 16)


def kernel(**inputs):
    import concourse.bacc as bacc
    from concourse.bass_utils import run_bass_kernel_spmd

    a = {n: np.asarray(v) for n, v in inputs.items()}
    QW, KW = NK * DK, 2 * NK * DK
    taps = a["L0_attn_conv_w"]
    wT = a["L0_attn_W_qkv"].T.reshape(KT, P, -1)
    by_head = lambda w, n: w.reshape(KT, P, NK, n, P)
    wk = np.concatenate([wT[:, :, QW:KW].reshape(KT, P, NK, DK).transpose(2, 1, 0, 3).reshape(NK, P, KT * DK), taps[QW:KW].reshape(NK, DK, TAPS)], 2)
    front = np.concatenate([by_head(wT[:, :, :QW], 1), by_head(wT[:, :, KW:], PV), by_head(a["L0_attn_W_z"].T, PV)], 3)
    front_taps = np.concatenate([taps[:QW].reshape(NK, 1, P, TAPS), taps[KW:].reshape(NK, PV, P, TAPS)], 1).transpose(0, 2, 1, 3)
    q_of_group = a["L1_attn_Wq"].reshape(H1 // GROUP, GROUP, 16, C).transpose(1, 0, 2, 3).reshape(C, C)
    angle = np.arange(T, dtype=np.float32)[:, None] * (1.0 / 10000.0 ** (np.arange(0, 16, 2, dtype=np.float32) / 16)).astype(np.float32)
    q_at, k_at = np.arange(P)[:, None], np.arange(P + WINDOW)[None]
    arrays = {
        "x": a["x"].reshape(TOK, C),
        "wk": wk,
        "wf": np.concatenate([front.transpose(2, 1, 0, 3, 4).reshape(NK, P, -1), front_taps.reshape(NK, P, -1)], 2),
        "wo": a["L0_attn_W_out"].T.reshape(NK, PV, P, C).transpose(0, 2, 1, 3).reshape(NK, P, PV * C),
        "wba": np.concatenate([a["L0_attn_W_b"], a["L0_attn_W_a"]], 0).T.reshape(KT, P, 2 * NV),
        "alog": a["L0_attn_A_log"].reshape(1, NV),
        "dtb": a["L0_attn_dt_bias"].reshape(1, NV),
        "nw": a["L0_attn_norm_w"].reshape(DV, 1),
        "ctx": a["ctx_2048"].reshape(TOK, C),
        "ctxT": a["ctx_2048"].transpose(0, 2, 1).reshape(B * C, T),
        "router": a["L0_ffn_router_logits"].reshape(KT, P, E0),
        "rscale": a["L0_ffn_router_scale"].reshape(KT, P).T,
        "escale": a["L0_ffn_per_expert_scale"].reshape(1, E0),
        "lower": np.tril(np.ones((E0, E0), np.float32), -1).reshape(1, E0 * E0),
        "gate": a["L0_ffn_gating_einsum"].transpose(3, 0, 1, 2).reshape(KT, P, E0, 2 * H0),
        "linear": a["L0_ffn_linear"].transpose(1, 0, 2).reshape(KT, P, E0, C),
        "wqkv": np.concatenate([q_of_group, a["L1_attn_Wkv"]], 0).T.reshape(KT, P, -1),
        "wo1": a["L1_attn_Wo"].T.reshape(KT, P, C),
        "rope": np.stack([np.cos(angle), -np.sin(angle), np.sin(angle)], 1).astype(np.float32).reshape(KT, P, 3, 8),
        "temp": a["L1_attn_qk_temp"].reshape(H1 // GROUP, GROUP).T.reshape(1, H1),
        "wmask": np.where((k_at > q_at) & (k_at <= q_at + WINDOW), 0, NEG).astype(np.float32),
        "diag": np.kron(np.eye(4), np.ones((32, 32))).astype(np.float32),
        "rw1": a["L1_ffn_router_w"].reshape(C, E1, C).transpose(2, 1, 0).reshape(KT, P, E1, C),
        "rb1": a["L1_ffn_router_b"].reshape(KT, P, E1),
        "we1": a["L1_ffn_expert_w"].transpose(2, 0, 1).reshape(KT, P, E1, C),
        "be1": a["L1_ffn_expert_b"],
    }
    nc = bacc.Bacc("TRN2", target_bir_lowering=False, num_devices=1)
    arrays = {f"in_{n}": np.ascontiguousarray(v) for n, v in arrays.items()}
    d = {n[3:]: nc.dram_tensor(n, v.shape, F32, kind="ExternalInput").ap() for n, v in arrays.items()}
    build(nc, d, nc.dram_tensor("out", (TOK, C), F32, kind="ExternalOutput").ap())
    result = run_bass_kernel_spmd(nc, [arrays], core_ids=[0])
    return result.results[0]["out"].reshape(B, T, C)
```
